# Optimizing a Trainium2 kernel written in Bass

```python
import numpy as np
import jax
import jax.numpy as jnp

def _softmax(x, axis=-1):
    return jax.nn.softmax(x, axis=axis)

def _gelu(x):
    return jax.nn.gelu(x, approximate=True)

def _silu(x):
    return jax.nn.silu(x)

def _sigmoid(x):
    return jax.nn.sigmoid(x)

def _layernorm(x, axis=-1, eps=1e-05):
    m = jnp.mean(x, axis=axis, keepdims=True)
    v = jnp.var(x, axis=axis, keepdims=True)
    return (x - m) / jnp.sqrt(v + eps)

def _scatter_add(tgt, idx, src, axis=0):
    return tgt.at[idx].add(src)

def _segment_sum(src, seg, n):
    return jax.ops.segment_sum(src, seg, n)
kernel_name = 'mk_seq_postln_d1_jaxref_r4_92fd38'

def setup_inputs(seed: int=0):
    np.random.seed(seed)
    _w = jnp.asarray

    def _L0_attn_setup():
        import jax, jax.numpy as jnp
        import numpy as np
        EMBED_DIM = 256
        PROJ_DIM = 64
        key = jax.random.key(seed)
        kx, kq, kk = jax.random.split(key, 3)
        x = jax.random.normal(kx, (8, 1024, EMBED_DIM), dtype=jnp.float32)
        scale = 1.0 / PROJ_DIM ** 0.5
        q_proj = jax.random.normal(kq, (EMBED_DIM, PROJ_DIM), dtype=jnp.float32) * scale
        k_proj = jax.random.normal(kk, (EMBED_DIM, PROJ_DIM), dtype=jnp.float32) * scale
        return {'x': x, 'q_proj': q_proj, 'k_proj': k_proj}
    _L0_attn_in = _L0_attn_setup()

    def _L0_ffn_setup():
        import jax, jax.numpy as jnp
        import numpy as np
        B, S, D, H, E, F, K = (2, 256, 256, 16, 8, 1024, 2)
        EPS = 1e-05

        def _layernorm(x, g, b):
            mu = jnp.mean(x, axis=-1, keepdims=True)
            var = jnp.mean(jnp.square(x - mu), axis=-1, keepdims=True)
            return (x - mu) * jax.lax.rsqrt(var + EPS) * g + b
        key = jax.random.key(seed)
        ks = jax.random.split(key, 12)
        w = lambda k, shape: jax.random.normal(k, shape, dtype=jnp.float32) * 0.02
        return {'x': jax.random.normal(ks[0], (B, S, D), dtype=jnp.float32), 'ln1_g': jnp.ones((D,), jnp.float32), 'ln1_b': jnp.zeros((D,), jnp.float32), 'ln2_g': jnp.ones((D,), jnp.float32), 'ln2_b': jnp.zeros((D,), jnp.float32), 'Wq': w(ks[1], (D, D)), 'Wk': w(ks[2], (D, D)), 'Wv': w(ks[3], (D, D)), 'Wo': w(ks[4], (D, D)), 'Wg': w(ks[5], (D, E)), 'W1': w(ks[6], (E, D, F)), 'b1': jnp.zeros((E, F), jnp.float32), 'W2': w(ks[7], (E, F, D)), 'b2': jnp.zeros((E, D), jnp.float32)}
    _L0_ffn_in = _L0_ffn_setup()
    _d = {'L0_attn_x': _L0_attn_in['x'], 'L0_attn_q_proj': _L0_attn_in['q_proj'], 'L0_attn_k_proj': _L0_attn_in['k_proj'], 'L0_ffn_ln1_g': _L0_ffn_in['ln1_g'], 'L0_ffn_ln1_b': _L0_ffn_in['ln1_b'], 'L0_ffn_ln2_g': _L0_ffn_in['ln2_g'], 'L0_ffn_ln2_b': _L0_ffn_in['ln2_b'], 'L0_ffn_Wq': _L0_ffn_in['Wq'], 'L0_ffn_Wk': _L0_ffn_in['Wk'], 'L0_ffn_Wv': _L0_ffn_in['Wv'], 'L0_ffn_Wo': _L0_ffn_in['Wo'], 'L0_ffn_Wg': _L0_ffn_in['Wg'], 'L0_ffn_W1': _L0_ffn_in['W1'], 'L0_ffn_b1': _L0_ffn_in['b1'], 'L0_ffn_W2': _L0_ffn_in['W2'], 'L0_ffn_b2': _L0_ffn_in['b2']}
    _x0 = _d['L0_attn_x']
    _d['L0_attn_x'] = jax.random.normal(jax.random.fold_in(jax.random.key(seed), 1), (1, 4096, 256), dtype=_x0.dtype)
    del _x0
    return _d

def reference(L0_attn_x, L0_attn_q_proj, L0_attn_k_proj, L0_ffn_ln1_g, L0_ffn_ln1_b, L0_ffn_ln2_g, L0_ffn_ln2_b, L0_ffn_Wq, L0_ffn_Wk, L0_ffn_Wv, L0_ffn_Wo, L0_ffn_Wg, L0_ffn_W1, L0_ffn_b1, L0_ffn_W2, L0_ffn_b2):

    def _L0_attn_ref(x, q_proj, k_proj):
        import jax, jax.numpy as jnp
        import numpy as np
        EMBED_DIM = 256
        PROJ_DIM = 64
        q_prime = jnp.exp(jnp.einsum('bld,de->ble', x, q_proj))
        k_prime = jnp.exp(jnp.einsum('bld,de->ble', x, k_proj))
        kv = jnp.einsum('ble,bld->bed', k_prime, x)
        num = jnp.einsum('ble,bed->bld', q_prime, kv)
        z = 1.0 / (jnp.sum(q_prime, axis=-1, keepdims=True) + 1e-08)
        return num * z

    def _L0_ffn_ref(x, ln1_g, ln1_b, ln2_g, ln2_b, Wq, Wk, Wv, Wo, Wg, W1, b1, W2, b2):
        import jax, jax.numpy as jnp
        import numpy as np
        B, S, D, H, E, F, K = (2, 256, 256, 16, 8, 1024, 2)
        EPS = 1e-05

        def _layernorm(x, g, b):
            mu = jnp.mean(x, axis=-1, keepdims=True)
            var = jnp.mean(jnp.square(x - mu), axis=-1, keepdims=True)
            return (x - mu) * jax.lax.rsqrt(var + EPS) * g + b
        Bb, Ss, Dd = x.shape
        Dh = Dd // H
        h = _layernorm(x, ln1_g, ln1_b)
        q = (h @ Wq).reshape(Bb, Ss, H, Dh)
        k = (h @ Wk).reshape(Bb, Ss, H, Dh)
        v = (h @ Wv).reshape(Bb, Ss, H, Dh)
        scores = jnp.einsum('bqhd,bkhd->bhqk', q, k) / jnp.sqrt(jnp.float32(Dh))
        attn = jax.nn.softmax(scores, axis=-1)
        ctx = jnp.einsum('bhqk,bkhd->bqhd', attn, v).reshape(Bb, Ss, Dd)
        x = x + ctx @ Wo
        m = _layernorm(x, ln2_g, ln2_b)
        xt = m.reshape(-1, Dd)
        T = xt.shape[0]
        probs = jax.nn.softmax(xt @ Wg, axis=-1)
        wts, idx = jax.lax.top_k(probs, K)
        wts = wts / jnp.sum(wts, axis=-1, keepdims=True)
        h1 = jax.nn.gelu(jnp.einsum('td,edf->etf', xt, W1) + b1[:, None, :])
        ye = jnp.einsum('etf,efd->etd', h1, W2) + b2[:, None, :]
        sel = ye[idx, jnp.arange(T)[:, None], :]
        moe_out = jnp.sum(wts[..., None] * sel, axis=1).reshape(Bb, Ss, Dd)
        return x + moe_out
    x = L0_attn_x
    x = _layernorm(x + _L0_attn_ref(x, L0_attn_q_proj, L0_attn_k_proj), axis=-1)
    x = _layernorm(x + _L0_ffn_ref(x, L0_ffn_ln1_g, L0_ffn_ln1_b, L0_ffn_ln2_g, L0_ffn_ln2_b, L0_ffn_Wq, L0_ffn_Wk, L0_ffn_Wv, L0_ffn_Wo, L0_ffn_Wg, L0_ffn_W1, L0_ffn_b1, L0_ffn_W2, L0_ffn_b2), axis=-1)
    return x

_drawn_inputs = setup_inputs


def setup_inputs(seed=0):
    import zlib

    import numpy as np

    out = dict(_drawn_inputs(seed))
    spreads = {'L0_ffn_ln1_g': (1.0, 0.6),
     'L0_ffn_ln1_b': (0.0, 0.8),
     'L0_ffn_ln2_g': (1.0, 0.6),
     'L0_ffn_ln2_b': (0.0, 0.409),
     'L0_ffn_b1': (0.0, 0.618),
     'L0_ffn_b2': (0.0, 0.1)}
    factors = {'L0_ffn_Wq': 8.0, 'L0_ffn_Wk': 8.0}
    for name, (base, spread) in spreads.items():
        noise = np.random.default_rng([zlib.crc32(name.encode()), seed]).standard_normal(out[name].shape)
        drawn = base * np.exp(spread * noise) if base else spread * noise
        out[name] = jnp.asarray(drawn.astype(out[name].dtype))
    for name, factor in factors.items():
        out[name] = (out[name] * factor).astype(out[name].dtype)
    return out
```

```python
import concourse.bass as bass
from concourse import mybir
from concourse.alu_op_type import AluOpType as ALU
from contextlib import ExitStack

F32 = mybir.dt.float32
F32R = mybir.dt.float32r
BF16 = mybir.dt.bfloat16
F16 = mybir.dt.float16
U32 = mybir.dt.uint32
I32 = mybir.dt.int32
ACT = mybir.ActivationFunctionType
AX = mybir.AxisListType
ds = bass.ds

P = 128
TOKENS, D = 4096, 256
HALVES = D // P
TILES = TOKENS // P
CHUNK = 512
CHUNKS = TOKENS // CHUNK
TPC = CHUNK // P
PROJ = 64
HEADS, DH = 16, 16
EXPERTS, FF = 8, 1024
FT = FF // P
EPS = 1e-5
Z_EPS = 1e-8
PARTS = 3

Q_PARTS = (0, 0, 0, 1, 1, 2)
K_PARTS = (0, 1, 2, 0, 1, 0)
SROWS = len(Q_PARTS) * DH
MROWS = 2
AROWS = SROWS + MROWS

V_ONE = PARTS * DH
V_COLS = 64
O_COLS = DH + 1

STEP = 2 * P
STEPS = TOKENS // STEP
KCH = TOKENS // CHUNK
UNITS = TPC * KCH
RING = HEADS * CHUNKS


class Chain:

    def __init__(self, eng, sem):
        self.eng, self.sem, self.base, self.n = eng, sem, 0, 0

    def enter(self, it, per):
        self.outer, self.per, self.before = self.base, per, self.n
        self.base, self.n = self.base + self.n + it * per, 0

    def leave(self, rounds):
        assert self.n == self.per, (self.n, self.per)
        self.base, self.n = self.outer, self.before + self.per * rounds

    def inc(self, ins):
        ins.then_inc(self.sem, 1)
        self.n += 1

    def wait(self):
        self.eng.wait_ge(self.sem, self.base + self.n)


def linear_attention(nc, dram, keep):
    with ExitStack() as ctx:
        def sb(name, shape, dt=F32):
            return ctx.enter_context(nc.sbuf_tensor(name, shape, dt))

        def ps(name, shape, dt=F32):
            return ctx.enter_context(nc.psum_tensor(name, shape, dt))

        def sem(name):
            return ctx.enter_context(nc.semaphore(name))

        x_all, v_all, ident = keep["x_all"], keep["v_all"], keep["ident"]
        x_in = sb("x_in", [P, 2, TPC, D])
        xT = sb("xT", [P, 2, HALVES, CHUNK])
        proj_q = sb("proj_q", [P, HALVES, PROJ])
        proj_k = sb("proj_k", [P, HALVES, PROJ])
        w_qkv = sb("w_qkv", [P, 3, HALVES, D])
        gain1 = sb("gain1", [P, HALVES])
        bias1 = sb("bias1", [P, HALVES])
        k_feat = sb("k_feat", [P, 2, TPC, PROJ])
        q_feat = sb("q_feat", [PROJ, TOKENS])
        q_here = sb("q_here", [PROJ, 2, CHUNK])
        kv = sb("kv", [PROJ, D + 1])
        z = sb("z", [P, TPC])
        y_here = sb("y_here", [P, TPC, D])
        stats_here = sb("stats_here", [P, TPC * 6])
        stats = sb("stats", [P, TILES * 6])
        mean_var = sb("mean_var", [P, TILES, 2])
        std = sb("std", [P, TILES])
        rstd = sb("rstd", [P, TILES])
        hn = sb("hn", [P, 2, TPC, D])
        hT = sb("hT", [P, 2, HALVES, CHUNK])
        rest = sb("rest", [P, 4, CHUNK])
        parts = sb("parts", [P, 2, 4, PARTS, CHUNK], BF16)

        banks = ps("banks", [P, 8, CHUNK])
        tr_ps = banks[:, 0:2, :]
        kf_ps = banks[:, 2, 0:TPC * PROJ].rearrange("p (t e) -> p t e", t=TPC)
        qf_ps = banks[0:PROJ, 3, :]
        kv_ps = banks[0:PROJ, 2, 0:D]
        num_ps = banks[:, 4:8, 0:D + 1]
        qk_ps = banks[:, 2:6, :]
        v_ps = banks[:, 6:8, :].rearrange("p b (t d) -> p (b t) d", t=2)

        proj_in, weights_in, affine_in = sem("proj_in"), sem("weights_in"), sem("affine_in")
        consts_set = sem("consts_set")
        x_in_full, x_in_free = [sem("x_in_full0"), sem("x_in_full1")], sem("x_in_free")
        x_all_full = sem("x_all_full")
        xT_in_psum, xT_ready = sem("xT_in_psum"), sem("xT_ready")
        feat_in_psum, feat_ready = sem("feat_in_psum"), sem("feat_ready")
        kv_in_psum, kv_added = sem("kv_in_psum"), sem("kv_added")
        q_here_ready = sem("q_here_ready")
        num_in_psum, y_ready = sem("num_in_psum"), sem("y_ready")
        var_ready, std_ready = sem("var_ready"), sem("std_ready")
        hn_ready, hnT_in_psum, hT_ready = sem("hn_ready"), sem("hnT_in_psum"), sem("hT_ready")
        qk_in_psum, v_in_psum, v_copied = sem("qk_in_psum"), sem("v_in_psum"), sem("v_copied")
        high_ready, rest_ready, mid_ready, low_ready = (
            sem("high_ready"), sem("rest_ready"), sem("mid_ready"), sem("low_ready"))
        parts_out = [sem("parts_out0"), sem("parts_out1")]
        parts_free = sem("parts_free")
        dve_chain = sem("dve_chain")

        x_chunks = dram["x"].rearrange("a (c t p) d -> (a c) p t d", p=P, t=TPC)
        block = ctx.enter_context(nc.Block())

        @block.sync
        def _(sp):
            sp.dma_start(proj_q[:, :, :], dram["q_proj"].rearrange("(j p) e -> p j e", p=P)).then_inc(proj_in, 16)
            sp.dma_start(proj_k[:, :, :], dram["k_proj"].rearrange("(j p) e -> p j e", p=P)).then_inc(proj_in, 16)
            with sp.Fori(0, CHUNKS // 2) as it:
                for b in range(2):
                    c = it * 2 + b
                    sp.wait_ge(x_in_free, c + 1)
                    sp.dma_start(x_in[:, b, :, :], x_chunks[ds(c, 1), :, :, :].rearrange("a p t d -> (a p) t d")
                                 ).then_inc(x_in_full[b], 16)
            sp.dma_start(x_all[:, :, :], dram["x"].rearrange("a (t p) d -> p (a t) d", p=P)).then_inc(x_all_full, 16)
            for n, w in enumerate(("Wq", "Wk", "Wv")):
                sp.dma_start(w_qkv[:, n, :, :], dram[w].rearrange("(j p) e -> p j e", p=P)).then_inc(weights_in, 16)
            sp.sem_inc(parts_free, 2)
            with sp.Fori(0, CHUNKS // 2) as it:
                for b in range(2):
                    c = it * 2 + b
                    for s in range(4):
                        sp.wait_ge(low_ready, c * 4 + (s + 1))
                        dst = dram["qs" if s < 2 else "ks"][:, P * (s % 2):P * (s % 2) + P, ds(c * CHUNK, CHUNK)]
                        sp.dma_start(dst.rearrange("n p t -> p n t"), parts[:, b, s, :, :]).then_inc(parts_out[b], 16)
                    sp.wait_ge(parts_out[b], it * 64 + 64)
                    sp.sem_inc(parts_free, 1)
            for b in range(2):
                sp.wait_ge(parts_out[b], 16 * 4 * CHUNKS // 2)

        @block.gpsimd
        def _(pool):
            nc.gpsimd.memset(ident[:, :], 0.0).then_inc(consts_set, 1)
            nc.gpsimd.memset(kv[:, :], 0.0).then_inc(consts_set, 1)
            pool.wait_ge(consts_set, 2)
            nc.gpsimd.affine_select(out=ident[:, :], in_=ident[:, :], compare_op=ALU.not_equal, fill=1.0,
                                    base=0, pattern=[[-1, P]], channel_multiplier=1).then_inc(consts_set, 1)
            nc.gpsimd.memset(kv[:, D:D + 1], 1.0).then_inc(consts_set, 1)
            pool.dma_start(gain1[:, :], dram["ln1_g"].rearrange("(j p) -> p j", p=P), allow_slow_non_contiguous=True).then_inc(affine_in, 16)
            pool.dma_start(bias1[:, :], dram["ln1_b"].rearrange("(j p) -> p j", p=P), allow_slow_non_contiguous=True).then_inc(affine_in, 16)
        @block.tensor
        def _(pe):
            pe.sem_inc(x_in_free, 2)
            pe.wait_ge(consts_set, 4)
            pe.wait_ge(proj_in, 32)
            with pe.Fori(0, CHUNKS // 2) as it:
                for b in range(2):
                    c = it * 2 + b
                    pe.wait_ge(x_in_full[b], it * 16 + 16)
                    for j in range(HALVES):
                        for t in range(TPC):
                            last = nc.tensor.transpose(tr_ps[:, j, P * t:P * t + P],
                                                       x_in[:, b, t, P * j:P * j + P], ident[:, :])
                    last.then_inc(xT_in_psum, 1)
                    pe.wait_ge(xT_ready, c * 2 + 2)
                    for t in range(TPC):
                        for j in range(HALVES):
                            nc.tensor.matmul(kf_ps[:, t, :], xT[:, b, j, P * t:P * t + P], proj_k[:, j, :],
                                             start=(j == 0), stop=(j == HALVES - 1))
                    for j in range(HALVES):
                        last = nc.tensor.matmul(qf_ps, proj_q[:, j, :], xT[:, b, j, :],
                                                start=(j == 0), stop=(j == HALVES - 1))
                    last.then_inc(feat_in_psum, 1)
                    pe.wait_ge(feat_ready, c * 2 + 2)
                    for t in range(TPC):
                        last = nc.tensor.matmul(kv_ps, k_feat[:, b, t, :], x_in[:, b, t, :],
                                                start=(t == 0), stop=(t == TPC - 1))
                    last.then_inc(kv_in_psum, 1)
                    pe.wait_ge(kv_added, c + 1)
                    pe.sem_inc(x_in_free, 1)
            with pe.Fori(0, CHUNKS // 2) as it:
                for b in range(2):
                    c = it * 2 + b
                    pe.wait_ge(q_here_ready, c + 1)
                    pe.wait_ge(y_ready, c * TPC + TPC)
                    for t in range(TPC):
                        last = nc.tensor.matmul(num_ps[:, t, :], q_here[:, b, P * t:P * t + P], kv[:, :],
                                                start=True, stop=True)
                    last.then_inc(num_in_psum, 1)
            pe.wait_ge(weights_in, 3 * 16)
            pe.wait_ge(y_ready, TILES + TPC)
            with pe.Fori(0, CHUNKS // 2) as it:
                for b in range(2):
                    c = it * 2 + b
                    pe.wait_ge(hn_ready, c + 1)
                    for j in range(HALVES):
                        for t in range(TPC):
                            last = nc.tensor.transpose(tr_ps[:, j, P * t:P * t + P],
                                                       hn[:, b, t, P * j:P * j + P], ident[:, :])
                    last.then_inc(hnT_in_psum, 1)
                    pe.wait_ge(hT_ready, c * 2 + 2)
                    for s in range(4):
                        pe.wait_ge(rest_ready, c * 4 + (s + 1))
                        for j in range(HALVES):
                            last = nc.tensor.matmul(qk_ps[:, s, :], w_qkv[:, s // 2, j, P * (s % 2):P * (s % 2) + P],
                                                    hT[:, b, j, :], start=(j == 0), stop=(j == HALVES - 1))
                        last.then_inc(qk_in_psum, 1)
                    pe.wait_ge(v_copied, c * 2 + 2)
                    for t in range(TPC):
                        for j in range(HALVES):
                            last = nc.tensor.matmul(v_ps[:, t, :], hT[:, b, j, P * t:P * t + P], w_qkv[:, 2, j, :],
                                                    start=(j == 0), stop=(j == HALVES - 1))
                        if t % 2:
                            last.then_inc(v_in_psum, 1)

        @block.scalar
        def _(act):
            act.preload_act_table(ACT.Exp)
            with act.Fori(0, CHUNKS // 2) as it:
                for b in range(2):
                    c = it * 2 + b
                    act.wait_ge(xT_in_psum, c + 1)
                    for j in range(HALVES):
                        nc.scalar.activation(xT[:, b, j, :], tr_ps[:, j, :], ACT.Copy).then_inc(xT_ready, 1)
                    act.wait_ge(feat_in_psum, c + 1)
                    nc.scalar.activation(k_feat[:, b, :, :], kf_ps, ACT.Exp).then_inc(feat_ready, 1)
                    nc.scalar.activation(q_feat[:, ds(c * CHUNK, CHUNK)], qf_ps, ACT.Exp).then_inc(feat_ready, 1)
            act.wait_ge(feat_ready, 2 * CHUNKS)
            act.sem_inc(num_in_psum, 1)
            with act.Fori(0, CHUNKS // 2) as it:
                for b in range(2):
                    c = it * 2 + b
                    act.wait_ge(num_in_psum, c + 1)
                    nc.scalar.activation(q_here[:, b, :], q_feat[:, ds(c * CHUNK, CHUNK)], ACT.Copy
                                         ).then_inc(q_here_ready, 1)
            act.preload_act_table(ACT.Sqrt)
            for n in range(2):
                act.wait_ge(var_ready, n + 1)
                nc.scalar.activation(std[:, :], std[:, :], ACT.Sqrt).then_inc(std_ready, 1)
            act.preload_act_table(ACT.Exp)
            act.wait_ge(affine_in, 2 * 16)
            act.sem_inc(v_copied, 2)
            with act.Fori(0, CHUNKS // 2) as it:
                for b in range(2):
                    c = it * 2 + b
                    act.wait_ge(hnT_in_psum, c + 1)
                    for j in range(HALVES):
                        nc.scalar.activation(hT[:, b, j, :], tr_ps[:, j, :], ACT.Identity,
                                             bias=bias1[:, j:j + 1], scale=gain1[:, j:j + 1]).then_inc(hT_ready, 1)
                    act.wait_ge(parts_free, c + 1)
                    for s in range(4):
                        act.wait_ge(qk_in_psum, c * 4 + (s + 1))
                        nc.scalar.activation(parts[:, b, s, 0, :], qk_ps[:, s, :], ACT.Copy,
                                             scale=(DH ** -0.5 if s < 2 else 1.0)).then_inc(high_ready, 1)
                    for s in range(4):
                        act.wait_ge(rest_ready, c * 4 + (s + 5))
                        nc.scalar.activation(parts[:, b, s, 1, :], rest[:, s, :], ACT.Copy).then_inc(mid_ready, 1)
                    for n in range(2):
                        act.wait_ge(v_in_psum, c * 2 + (n + 1))
                        nc.scalar.activation(v_all[:, ds(c * TPC + 2 * n, 2), :], v_ps[:, 2 * n:2 * n + 2, :],
                                             ACT.Copy).then_inc(v_copied, 1)

        @block.vector
        def _(dve):
            ch = Chain(dve, dve_chain)
            dve.wait_ge(consts_set, 4)
            with dve.Fori(0, CHUNKS) as c:
                dve.wait_ge(kv_in_psum, c + 1)
                nc.vector.tensor_tensor(kv[:, 0:D], kv[:, 0:D], kv_ps, ALU.add).then_inc(kv_added, 1)
                dve.wait_ge(kv_added, c + 1)
            dve.wait_ge(x_all_full, 16)
            dve.sem_inc(y_ready, TPC)

            def tile(c, t):
                return x_all[:, ds(c * TPC + t, 1), :].rearrange("p a d -> p (a d)")

            def keep_rows(c):
                ch.wait()
                for t in range(TPC):
                    ch.inc(nc.vector.bn_stats(stats_here[:, 6 * t:6 * t + 6], y_here[:, t, :]))
                ch.wait()
                ch.inc(nc.vector.tensor_scalar(stats[:, ds(c * TPC * 6, TPC * 6)], stats_here[:, :], 1.0, None, ALU.mult))
                ch.inc(nc.vector.tensor_scalar(x_all[:, ds(c * TPC, TPC), :], y_here[:, :, :], 1.0, None, ALU.mult))
                ch.wait()

            def reciprocal_std(n):
                for t in range(TILES):
                    ch.inc(nc.vector.bn_aggr(mean_var[:, t, :], stats[:, 6 * t:6 * t + 6]))
                ch.wait()
                nc.vector.tensor_scalar(std[:, :], mean_var[:, :, 1], EPS, None, ALU.add).then_inc(var_ready, 1)
                dve.wait_ge(std_ready, n + 1)
                ch.inc(nc.vector.reciprocal(rstd[:, :], std[:, :]))
                ch.wait()

            with dve.Fori(0, CHUNKS) as c:
                dve.wait_ge(num_in_psum, c + 2)
                ch.enter(c, 2 + 2 * TPC + 2)
                ch.inc(nc.vector.tensor_scalar(z[:, :], num_ps[:, :, D], Z_EPS, None, ALU.add))
                ch.wait()
                ch.inc(nc.vector.reciprocal(z[:, :], z[:, :]))
                ch.wait()
                for t in range(TPC):
                    ch.inc(nc.vector.scalar_tensor_tensor(y_here[:, t, :], num_ps[:, t, 0:D], z[:, t:t + 1], tile(c, t),
                                                          ALU.mult, ALU.add))
                keep_rows(c)
                ch.leave(CHUNKS)
                dve.sem_inc(y_ready, TPC)
            reciprocal_std(0)
            with dve.Fori(0, CHUNKS) as c:
                ch.enter(c, 2 * TPC + 2)
                for t in range(TPC):
                    ch.inc(nc.vector.tensor_scalar(
                        y_here[:, t, :], tile(c, t), mean_var[:, ds(c * TPC + t, 1), 0], rstd[:, ds(c * TPC + t, 1)],
                        ALU.subtract, ALU.mult))
                keep_rows(c)
                ch.leave(CHUNKS)
            reciprocal_std(1)
            dve.sem_inc(rest_ready, 4)

            def normalize(c, b):
                for t in range(TPC):
                    last = nc.vector.tensor_scalar(
                        hn[:, b, t, :], tile(c, t), mean_var[:, ds(c * TPC + t, 1), 0], rstd[:, ds(c * TPC + t, 1)],
                        ALU.subtract, ALU.mult)
                last.then_inc(hn_ready, 1)

            with dve.Fori(0, CHUNKS // 2) as it:
                for b in range(2):
                    c = it * 2 + b
                    normalize(c, b)
                    for s in range(4):
                        dve.wait_ge(high_ready, c * 4 + (s + 1))
                        nc.vector.scalar_tensor_tensor(rest[:, s, :], qk_ps[:, s, :], DH ** -0.5 if s < 2 else 1.0,
                                                       parts[:, b, s, 0, :], ALU.mult, ALU.subtract
                                                       ).then_inc(rest_ready, 1)
                    for s in range(4):
                        dve.wait_ge(mid_ready, c * 4 + (s + 1))
                        nc.vector.tensor_tensor(parts[:, b, s, 2, :], rest[:, s, :], parts[:, b, s, 1, :], ALU.subtract
                                                ).then_inc(low_ready, 1)


def softmax_attention(nc, dram, keep):
    with ExitStack() as ctx:
        def sb(name, shape, dt=F32):
            return ctx.enter_context(nc.sbuf_tensor(name, shape, dt))

        def ps(name, shape, dt=F32):
            return ctx.enter_context(nc.psum_tensor(name, shape, dt))

        def sem(name):
            return ctx.enter_context(nc.semaphore(name))

        v_all, ident, ctx_slots = keep["v_all"], keep["ident"], keep["ctx_slots"]
        q_ring = sb("q_ring", [AROWS, 2 * TOKENS], BF16)
        k_ring = sb("k_ring", [AROWS, 2 * TOKENS], BF16)
        v_parts = sb("v_parts", [P, 2, TILES, V_COLS], BF16)
        v_here = sb("v_here", [P, TILES, DH])
        v_rest = sb("v_rest", [P, TILES, DH])
        zeros = sb("zeros", [P, TILES, DH])
        gather = sb("gather", [P, O_COLS])
        probs = sb("probs", [P, 4, STEP // P, CHUNK])
        probs_low = sb("probs_low", [P, 4, STEP // P, CHUNK], F16)
        unit_max = sb("unit_max", [P, TPC, KCH])
        tile_max = sb("tile_max", [P, TPC])
        max_parts = sb("max_parts", [TPC, MROWS, P], BF16)
        o_here = sb("o_here", [P, CHUNK])
        o_scale = sb("o_scale", [P, TPC])

        s2_ps = ps("s2_ps", [P, 2, STEP // P, CHUNK])
        s1_ps = ps("s1_ps", [P, 2, CHUNK])
        o_ps = ps("o_ps", [P, CHUNK])
        misc_ps = ps("misc_ps", [P, CHUNK])
        out_ps = misc_ps[:, 0:TPC * O_COLS].rearrange("p (t c) -> p t c", t=TPC)
        maxT_ps = misc_ps[0:TPC, P:2 * P]

        qk_in, head_ready = sem("qk_in"), sem("head_ready")
        v_ready, consts_ready, gather_ready = sem("v_ready"), sem("consts_ready"), sem("gather_ready")
        s2_done, exp_done, low_done, pv_done = sem("s2_done"), sem("exp_done"), sem("low_done"), sem("pv_done")
        s1_done, s1_read, tile_max_done = sem("s1_done"), sem("s1_read"), sem("tile_max_done")
        maxT_done, max_split, rows_made = sem("maxT_done"), sem("max_split"), sem("rows_made")
        row_in, rows_in = sem("row_in"), sem("rows_in")
        o_copied, o_turned, o_scaled, o_stored = sem("o_copied"), sem("o_turned"), sem("o_scaled"), sem("o_stored")
        pool_chain, start_values, sync_passed = sem("pool_chain"), sem("start_values"), sem("sync_passed")

        def per_step(eng, body):
            def steps(head, par, lo, hi, ahead):
                with eng.Fori(lo, hi) as qc:
                    body(head * CHUNKS + qc, head, par, qc, ahead)

            with eng.Fori(0, HEADS // 2 - 1) as pair:
                for par in range(2):
                    steps(pair * 2 + par, par, 0, CHUNKS, True)
            steps(HEADS - 2, 0, 0, CHUNKS, True)
            steps(HEADS - 1, 1, 0, 1, True)
            steps(HEADS - 1, 1, 1, CHUNKS, False)

        block = ctx.enter_context(nc.Block())

        @block.sync
        def _(sp):
            def load_head(h, col):
                for ring, src, of in ((q_ring, "qs", Q_PARTS), (k_ring, "ks", K_PARTS)):
                    for n, part in enumerate(of):
                        sp.dma_start(ring[DH * n:DH * n + DH, ds(col, TOKENS)],
                                     dram[src][part, ds(h * DH, DH), :]).then_inc(qk_in, 16)
                sp.wait_ge(qk_in, (h + 1) * (2 * len(Q_PARTS) * 16))
                sp.sem_inc(head_ready, 1)

            def rows(n):
                col = sp.snap(((n + 15) & 15) * CHUNK)
                sp.wait_ge(rows_made, n + 2)
                sp.sem_inc(sync_passed, 1)
                for r in range(MROWS):
                    sp.dma_start(q_ring[SROWS + r:SROWS + r + 1, ds(col, CHUNK)].rearrange("a (t n) -> a t n", t=TPC),
                                 max_parts[:, r, :]).then_inc(row_in, 16)
                sp.wait_ge(row_in, n * (MROWS * 16) + MROWS * 16)
                sp.sem_inc(rows_in, 1)

            load_head(sp.snap(0), sp.snap(0))
            with sp.Fori(0, CHUNKS - 1) as n:
                rows(n)
            with sp.Fori(0, HEADS - 1) as h:
                next_head, col = sp.snap(h + 1), sp.snap(((h + 1) & 1) * TOKENS)
                sp.wait_ge(pv_done, h * (CHUNKS * STEPS) + 4)
                sp.sem_inc(sync_passed, 1)
                load_head(next_head, col)
                with sp.Fori(0, CHUNKS) as qc:
                    rows(h * CHUNKS + (qc + CHUNKS - 1))
            with sp.Fori(0, CHUNKS) as qc:
                rows(qc + HEADS * CHUNKS - 1)

        @block.gpsimd
        def _(pool):
            ch = Chain(pool, pool_chain)
            nc.gpsimd.memset(k_ring[SROWS:AROWS, :], 1.0).then_inc(consts_ready, 1)
            pool.wait_ge(consts_ready, 1)
            nc.gpsimd.memset(v_parts[:, :, :, V_ONE:V_COLS], 0.0).then_inc(consts_ready, 1)
            nc.gpsimd.memset(zeros[:, :, :], 0.0).then_inc(consts_ready, 1)
            pool.wait_ge(consts_ready, 3)
            nc.gpsimd.memset(v_parts[:, :, :, V_ONE:V_ONE + 1], 1.0).then_inc(consts_ready, 1)
            ch.inc(nc.gpsimd.tensor_tensor(gather[:, 0:DH], ident[:, 0:DH], ident[:, DH:2 * DH], ALU.add))
            for r in (2 * DH, V_COLS, V_COLS + DH, V_COLS + 2 * DH):
                ch.wait()
                ch.inc(nc.gpsimd.tensor_tensor(gather[:, 0:DH], gather[:, 0:DH], ident[:, r:r + DH], ALU.add))
            nc.gpsimd.tensor_tensor(gather[:, DH:O_COLS], ident[:, V_ONE:V_ONE + 1],
                                    ident[:, V_COLS + V_ONE:V_COLS + V_ONE + 1], ALU.add).then_inc(gather_ready, 1)

            def split_v(h, par):
                high, mid, low = (v_parts[:, par, :, DH * n:DH * n + DH] for n in range(PARTS))
                ch.inc(nc.gpsimd.tensor_copy(v_here[:, :, :], v_all[:, :, ds(h * DH, DH)]))
                ch.wait()
                ch.inc(nc.gpsimd.tensor_tensor(high, v_here[:, :, :], zeros[:, :, :], ALU.add))
                ch.wait()
                ch.inc(nc.gpsimd.tensor_tensor(v_rest[:, :, :], v_here[:, :, :], high, ALU.subtract))
                ch.wait()
                ch.inc(nc.gpsimd.tensor_tensor(mid, v_rest[:, :, :], zeros[:, :, :], ALU.add))
                ch.wait()
                nc.gpsimd.tensor_tensor(low, v_rest[:, :, :], mid, ALU.subtract).then_inc(v_ready, 1)
                pool.wait_ge(v_ready, h + 1)

            pool.wait_ge(consts_ready, 4)
            for h in range(2):
                split_v(h, h)
            with pool.Fori(0, HEADS // 2 - 1) as pair:
                ch.enter(pair, 8)
                for par in range(2):
                    pool.wait_ge(pv_done, (pair * 2 + (par + 1)) * (CHUNKS * STEPS) + 4)
                    split_v(pair * 2 + (par + 2), par)
                ch.leave(HEADS // 2 - 1)

        @block.tensor
        def _(pe):
            pe.wait_ge(consts_ready, 4)
            pe.wait_ge(gather_ready, 1)
            pe.sem_inc(o_turned, 1)
            pe.sem_inc(pv_done, 4)

            def unit(n, u):
                pe.wait_ge(s1_read, n * UNITS + (u + 1))
                q = (n & 15) * CHUNK + P * (u // KCH)
                k = ((n >> 3) & 1) * TOKENS + CHUNK * (u % KCH)
                nc.tensor.matmul(s1_ps[:, u % 2, :], q_ring[0:SROWS, ds(q, P)], k_ring[0:SROWS, ds(k, CHUNK)],
                                 start=True, stop=True).then_inc(s1_done, 1)

            def turn_max(n):
                pe.wait_ge(tile_max_done, n + 1)
                pe.wait_ge(rows_made, n + 1)
                nc.tensor.transpose(maxT_ps, tile_max[:, :], ident[:, :]).then_inc(maxT_done, 1)

            def turn_o(i):
                pe.wait_ge(o_copied, i + 1)
                pe.wait_ge(o_stored, i + 1)
                for t in range(TPC):
                    last = nc.tensor.matmul(out_ps[:, t, :], o_here[:, P * t:P * t + P], gather[:, :],
                                            start=True, stop=True)
                last.then_inc(o_turned, 1)

            def step(i, head, par, qc, ahead):
                i = pe.snap(i)
                n = i + (CHUNKS - 1)
                if ahead:
                    pe.wait_ge(head_ready, (n >> 3) + 1)
                pe.wait_ge(rows_in, i + 3)
                pe.wait_ge(v_ready, head + 1)
                q = q_ring[:, ds(qc * CHUNK + par * TOKENS, CHUNK)]

                def values(t):
                    pe.wait_ge(low_done, i * STEPS + (t + 1))
                    if t == 0:
                        pe.wait_ge(o_copied, i + 1)
                    high = probs[:, t % 4, :, :].bitcast(BF16).rearrange("p k (n two) -> p k n two", two=2)
                    for low, part in enumerate((high[:, :, :, 1], probs_low[:, t % 4, :, :])):
                        for k in range(2):
                            last = nc.tensor.matmul(
                                o_ps[V_COLS * k:V_COLS * k + V_COLS, :], v_parts[:, par, 2 * t + k, :], part[:, k, :],
                                start=(t == 0 and low == 0), stop=(t == STEPS - 1 and low == 1))
                    last.then_inc(pv_done, 1)

                for t in range(STEPS):
                    pe.wait_ge(exp_done, i * STEPS + (t + 1))
                    for k in range(2):
                        col = par * TOKENS + STEP * t + P * k
                        last = nc.tensor.matmul(s2_ps[:, t % 2, k, :], k_ring[:, col:col + P], q, start=True, stop=True)
                    last.then_inc(s2_done, 1)
                    if ahead:
                        unit(n, 2 * t)
                        unit(n, 2 * t + 1)
                    if t == 3:
                        pe.wait_ge(rows_made, n + 1)
                        turn_o(i)
                        turn_max(n)
                    if t >= 1:
                        values(t - 1)
                values(STEPS - 1)

            pe.wait_ge(head_ready, 1)
            with pe.Fori(0, CHUNKS - 1) as n:
                for u in range(UNITS):
                    unit(n, u)
                    if u == 3:
                        turn_max(n)
            per_step(pe, step)
            turn_o(RING)

        @block.scalar
        def _(act):
            act.preload_act_table(ACT.Exp)
            act.sem_inc(exp_done, 2)

            def copy_o(i):
                act.wait_ge(pv_done, i * STEPS + 4)
                act.wait_ge(o_turned, i + 1)
                nc.scalar.activation(o_here[:, :], o_ps[:, :], ACT.Copy).then_inc(o_copied, 1)

            def step(i, head, par, qc, ahead):
                i = act.snap(i)
                for t in range(STEPS):
                    act.wait_ge(s2_done, i * STEPS + (t + 1))
                    act.wait_ge(pv_done, i * STEPS + (t + 1))
                    nc.scalar.activation(probs[:, t % 4, :, :], s2_ps[:, t % 2, :, :], ACT.Exp).then_inc(exp_done, 1)
                    if t == 0:
                        copy_o(i)

            act.wait_ge(o_scaled, 1)
            per_step(act, step)
            copy_o(RING)

        @block.vector
        def _(dve):
            nc.vector.memset(o_ps[:, :], 1.0).then_inc(o_scaled, 1)
            nc.vector.memset(unit_max[:, :, :], 0.0).then_inc(start_values, 1)
            dve.wait_ge(start_values, 1)
            dve.sem_inc(s1_read, 2)
            dve.sem_inc(rows_made, 1)
            dve.sem_inc(rows_in, 1)
            dve.sem_inc(o_stored, 1)

            def finish_max(n):
                dve.wait_ge(maxT_done, n + 1)
                dve.wait_ge(rows_in, n + 1)
                nc.vector.tensor_scalar(max_parts[:, 0, :], maxT_ps, -1.0, None, ALU.mult).then_inc(max_split, 1)
                dve.wait_ge(max_split, n + 1)
                nc.vector.scalar_tensor_tensor(max_parts[:, 1, :], maxT_ps, -1.0, max_parts[:, 0, :],
                                               ALU.mult, ALU.subtract).then_inc(rows_made, 1)

            def finish_o(i):
                dve.wait_ge(o_turned, i + 2)
                nc.vector.reciprocal(o_scale[:, :], out_ps[:, :, DH]).then_inc(o_scaled, 1)
                dve.wait_ge(o_scaled, i + 2)
                nc.vector.tensor_tensor(ctx_slots[:, ds(i, 1), :, :].rearrange("p a t c -> p (a t) c"), out_ps[:, :, 0:DH],
                                        o_scale[:, :].unsqueeze(2).to_broadcast([P, TPC, DH]), ALU.mult
                                        ).then_inc(o_stored, 1)

            def reduce_tiles(n, units):
                dve.wait_ge(s1_read, units)
                nc.vector.tensor_reduce(tile_max[:, :], unit_max[:, :, :], AX.X, ALU.max).then_inc(tile_max_done, 1)
                dve.wait_ge(tile_max_done, n + 1)

            def unit(n, u):
                dve.wait_ge(s1_done, n * UNITS + (u + 1))
                nc.vector.tensor_reduce(unit_max[:, u // KCH, u % KCH:u % KCH + 1], s1_ps[:, u % 2, :], AX.X, ALU.max
                                        ).then_inc(s1_read, 1)

            def step(i, head, par, qc, ahead):
                i = dve.snap(i)
                n = i + (CHUNKS - 1)
                reduce_tiles(n, n * UNITS + 2 if ahead else RING * UNITS + 2)
                for t in range(STEPS):
                    if ahead:
                        unit(n, 2 * t)
                        unit(n, 2 * t + 1)
                    dve.wait_ge(exp_done, i * STEPS + (t + 3))
                    high = probs[:, t % 4, :, :].bitcast(BF16).rearrange("p k (n two) -> p k n two", two=2)
                    nc.vector.tensor_tensor(probs_low[:, t % 4, :, :], probs[:, t % 4, :, :], high[:, :, :, 1],
                                            ALU.subtract).then_inc(low_done, 1)
                    if t == 4:
                        finish_max(n)
                        finish_o(i)

            with dve.Fori(0, CHUNKS - 1) as n:
                reduce_tiles(n, n * UNITS + 2)
                for u in range(UNITS):
                    unit(n, u)
                    if u == 4:
                        finish_max(n)
            per_step(dve, step)
            finish_o(RING)


def row_statistics(nc, dve, ch, stats, mean_var, std, rstd, var_ready, std_ready, n):
    for t in range(TILES):
        ch.inc(nc.vector.bn_aggr(mean_var[:, t, :], stats[:, 6 * t:6 * t + 6]))
    ch.wait()
    nc.vector.tensor_scalar(std[:, :], mean_var[:, :, 1], EPS, None, ALU.add).then_inc(var_ready, 1)
    dve.wait_ge(std_ready, n + 1)
    ch.inc(nc.vector.reciprocal(rstd[:, :], std[:, :]))
    ch.wait()


def output_projection(nc, dram, keep):
    with ExitStack() as ctx:
        def sb(name, shape, dt=F32):
            return ctx.enter_context(nc.sbuf_tensor(name, shape, dt))

        def sem(name):
            return ctx.enter_context(nc.semaphore(name))

        x1, x2, ident, ctx_slots = keep["x_all"], keep["v_all"], keep["ident"], keep["ctx_slots"]
        stats = keep["stats"]
        w_o = sb("w_o", [P, HALVES, D])
        heads_here = sb("heads_here", [P, 2, TPC, D])
        headsT = sb("headsT", [P, 2, HALVES, CHUNK])
        y_here = sb("y2_here", [P, TPC, D])
        stats_here = sb("stats2_here", [P, TPC * 6])
        banks = ctx.enter_context(nc.psum_tensor("banks_o", [P, 8, CHUNK], F32))
        tr_ps = banks[:, 0:2, :]
        att_ps = banks[:, 2:4, :].rearrange("p b (t d) -> p (b t) d", t=2)

        wo_in, heads_ready, turned, headsT_ready, att_done, x2_ready = (
            sem("wo_in"), sem("heads_ready"), sem("turned"), sem("headsT_ready"), sem("att_done"), sem("x2_ready"))
        dve_chain = sem("dve_chain_o")
        block = ctx.enter_context(nc.Block())

        @block.sync
        def _(sp):
            sp.dma_start(w_o[:, :, :], dram["Wo"].rearrange("(j p) e -> p j e", p=P)).then_inc(wo_in, 16)

        @block.scalar
        def _(act):
            act.preload_act_table(ACT.Copy)
            slots = ctx_slots[:, 1:RING + 1, :, :].rearrange("p (h q) t c -> p h q t c", q=CHUNKS)
            with act.Fori(0, CHUNKS // 2) as it:
                for b in range(2):
                    c = it * 2 + b
                    for t in range(TPC):
                        last = nc.scalar.activation(
                            heads_here[:, b, t, :].rearrange("p (h c) -> p h c", c=DH),
                            slots[:, :, ds(c, 1), t, :].rearrange("p h q c -> p (h q) c"), ACT.Copy)
                    last.then_inc(heads_ready, 1)
                    act.wait_ge(turned, c + 1)
                    for j in range(HALVES):
                        nc.scalar.activation(headsT[:, b, j, :], tr_ps[:, j, :], ACT.Copy).then_inc(headsT_ready, 1)

        @block.tensor
        def _(pe):
            pe.wait_ge(wo_in, 16)
            with pe.Fori(0, CHUNKS // 2) as it:
                for b in range(2):
                    c = it * 2 + b
                    pe.wait_ge(heads_ready, c + 1)
                    for j in range(HALVES):
                        for t in range(TPC):
                            last = nc.tensor.transpose(tr_ps[:, j, P * t:P * t + P],
                                                       heads_here[:, b, t, P * j:P * j + P], ident[:, :])
                    last.then_inc(turned, 1)
                    pe.wait_ge(headsT_ready, c * 2 + 2)
                    pe.wait_ge(x2_ready, c + 1)
                    for t in range(TPC):
                        for j in range(HALVES):
                            last = nc.tensor.matmul(att_ps[:, t, :], headsT[:, b, j, P * t:P * t + P], w_o[:, j, :],
                                                    start=(j == 0), stop=(j == HALVES - 1))
                    last.then_inc(att_done, 1)

        @block.vector
        def _(dve):
            ch = Chain(dve, dve_chain)
            dve.sem_inc(x2_ready, 1)
            with dve.Fori(0, CHUNKS) as c:
                dve.wait_ge(att_done, c + 1)
                ch.enter(c, TPC + 2)
                nc.vector.tensor_tensor(y_here[:, :, :], att_ps, x1[:, ds(c * TPC, TPC), :], ALU.add).then_inc(x2_ready, 1)
                dve.wait_ge(x2_ready, c + 2)
                for t in range(TPC):
                    ch.inc(nc.vector.bn_stats(stats_here[:, 6 * t:6 * t + 6], y_here[:, t, :]))
                ch.wait()
                ch.inc(nc.vector.tensor_scalar(stats[:, ds(c * TPC * 6, TPC * 6)], stats_here[:, :], 1.0, None, ALU.mult))
                ch.inc(nc.vector.tensor_scalar(x2[:, ds(c * TPC, TPC), :], y_here[:, :, :], 1.0, None, ALU.mult))
                ch.wait()
                ch.leave(CHUNKS)


def routing(nc, dram, keep):
    with ExitStack() as ctx:
        def sb(name, shape, dt=F32):
            return ctx.enter_context(nc.sbuf_tensor(name, shape, dt))

        def sem(name):
            return ctx.enter_context(nc.semaphore(name))

        x1, x2, ident, stats = keep["x_all"], keep["v_all"], keep["ident"], keep["stats"]
        m_high, m_low, weights = keep["m_high"], keep["m_low"], keep["weights"]
        mean_var, std, rstd = keep["mean_var"], keep["std"], keep["rstd"]
        w_g = sb("w_g", [P, HALVES, EXPERTS])
        b_2 = sb("b_2", [EXPERTS, D])
        gain2 = sb("gain2", [P, HALVES])
        bias2 = sb("bias2", [P, HALVES])
        hn = sb("hn2", [P, 2, TPC, D])
        mT = sb("mT", [P, 2, HALVES, CHUNK])
        count_i = sb("count_i", [P, EXPERTS], I32)
        count = sb("count", [P, EXPERTS])
        top_logit = sb("top_logit", [P, TPC])
        shifted = sb("shifted", [P, TPC, EXPERTS])
        expd = sb("expd", [P, TPC, EXPERTS])
        total = sb("total", [P, TPC])
        prob = sb("prob", [P, TPC, EXPERTS])
        top = sb("top", [P, TPC, EXPERTS])
        top_at = sb("top_at", [P, TPC, EXPERTS], U32)
        at = sb("at", [P, TPC, 2])
        pair = sb("pair", [P, TPC])
        share = sb("share", [P, TPC, 2])
        chosen = sb("chosen", [P, 2, TPC, EXPERTS])
        weights_here = sb("weights_here", [P, TPC, EXPERTS])
        weightsT = sb("weightsT", [EXPERTS, CHUNK])
        y_here = sb("y3_here", [P, TPC, D])
        banks = ctx.enter_context(nc.psum_tensor("banks_r", [P, 8, CHUNK], F32))
        tr_ps = banks[:, 0:2, :]
        logit_ps = banks[:, 2, 0:TPC * EXPERTS].rearrange("p (t e) -> p t e", t=TPC)
        wT_ps = banks[0:EXPERTS, 3, :]
        b2_ps = banks[:, 4:6, :].rearrange("p b (t d) -> p (b t) d", t=2)

        router_in, affine_in, consts_ready = sem("router_in"), sem("affine2_in"), sem("consts2_ready")
        var_ready, std_ready = sem("var2_ready"), sem("std2_ready")
        hn_ready, turned, mT_ready, high_ready, low_ready = (
            sem("hn2_ready"), sem("turned2"), sem("mT_ready"), sem("m_high_ready"), sem("m_low_ready"))
        logits_done, shifted_ready, exp_ready, weights_ready = (
            sem("logits_done"), sem("shifted_ready"), sem("exp_ready"), sem("weights_ready"))
        wT_done, wT_ready, b2_done, b2_added = sem("wT_done"), sem("wT_ready"), sem("b2_done"), sem("b2_added")
        dve_chain, passed = sem("dve_chain_r"), sem("passed")
        block = ctx.enter_context(nc.Block())

        @block.sync
        def _(sp):
            sp.dma_start(w_g[:, :, :], dram["Wg"].rearrange("(j p) e -> p j e", p=P)).then_inc(router_in, 16)
            sp.dma_start(b_2[:, :], dram["b2"]).then_inc(router_in, 16)

        @block.gpsimd
        def _(pool):
            pool.dma_start(gain2[:, :], dram["ln2_g"].rearrange("(j p) -> p j", p=P),
                           allow_slow_non_contiguous=True).then_inc(affine_in, 16)
            pool.dma_start(bias2[:, :], dram["ln2_b"].rearrange("(j p) -> p j", p=P),
                           allow_slow_non_contiguous=True).then_inc(affine_in, 16)
            nc.gpsimd.iota(count_i[:, :], [[1, EXPERTS]], base=0, channel_multiplier=0).then_inc(consts_ready, 1)
            pool.wait_ge(consts_ready, 1)
            nc.gpsimd.tensor_copy(count[:, :], count_i[:, :]).then_inc(consts_ready, 1)

        @block.scalar
        def _(act):
            act.preload_act_table(ACT.Sqrt)
            act.wait_ge(var_ready, 1)
            nc.scalar.activation(std[:, :], std[:, :], ACT.Sqrt).then_inc(std_ready, 1)
            act.preload_act_table(ACT.Exp)
            act.wait_ge(affine_in, 2 * 16)
            with act.Fori(0, CHUNKS // 2) as it:
                for b in range(2):
                    c = it * 2 + b
                    act.wait_ge(turned, c + 1)
                    for j in range(HALVES):
                        nc.scalar.activation(mT[:, b, j, :], tr_ps[:, j, :], ACT.Identity,
                                             bias=bias2[:, j:j + 1], scale=gain2[:, j:j + 1]).then_inc(mT_ready, 1)
                    act.wait_ge(mT_ready, c * 2 + 2)
                    nc.scalar.activation(m_high[:, ds(c, 1), :, :].rearrange("p a j n -> p (a j) n"), mT[:, b, :, :],
                                         ACT.Copy).then_inc(high_ready, 1)
                    act.wait_ge(shifted_ready, c + 1)
                    nc.scalar.activation(expd[:, :, :], shifted[:, :, :], ACT.Exp).then_inc(exp_ready, 1)
                    act.wait_ge(wT_done, c + 1)
                    nc.scalar.activation(weightsT[:, :], wT_ps, ACT.Copy).then_inc(wT_ready, 1)

        @block.tensor
        def _(pe):
            pe.wait_ge(router_in, 32)
            with pe.Fori(0, CHUNKS // 2) as it:
                for b in range(2):
                    c = it * 2 + b
                    pe.wait_ge(hn_ready, c + 1)
                    for j in range(HALVES):
                        for t in range(TPC):
                            last = nc.tensor.transpose(tr_ps[:, j, P * t:P * t + P],
                                                       hn[:, b, t, P * j:P * j + P], ident[:, :])
                    last.then_inc(turned, 1)
                    pe.wait_ge(mT_ready, c * 2 + 2)
                    for t in range(TPC):
                        for j in range(HALVES):
                            last = nc.tensor.matmul(logit_ps[:, t, :], mT[:, b, j, P * t:P * t + P], w_g[:, j, :],
                                                    start=(j == 0), stop=(j == HALVES - 1))
                    last.then_inc(logits_done, 1)
                    pe.wait_ge(weights_ready, c + 1)
                    for t in range(TPC):
                        last = nc.tensor.transpose(wT_ps[:, P * t:P * t + P], weights_here[:, t, :], ident[:, :])
                    last.then_inc(wT_done, 1)
                    pe.wait_ge(wT_ready, c + 1)
                    pe.wait_ge(b2_added, c + 1)
                    for t in range(TPC):
                        last = nc.tensor.matmul(b2_ps[:, t, :], weightsT[:, P * t:P * t + P], b_2[:, :],
                                                start=True, stop=True)
                    last.then_inc(b2_done, 1)

        @block.vector
        def _(dve):
            ch = Chain(dve, dve_chain)
            row_statistics(nc, dve, ch, stats, mean_var, std, rstd, var_ready, std_ready, 0)
            dve.wait_ge(consts_ready, 2)
            dve.sem_inc(b2_added, 1)

            def hold():
                ch.wait()
                dve.sem_inc(passed, 1)

            with dve.Fori(0, CHUNKS // 2) as it:
                ch.enter(it, 2 * 17)
                for b in range(2):
                    c = it * 2 + b
                    for t in range(TPC):
                        last = nc.vector.tensor_scalar(
                            hn[:, b, t, :], x2[:, ds(c * TPC + t, 1), :].rearrange("p a d -> p (a d)"),
                            mean_var[:, ds(c * TPC + t, 1), 0], rstd[:, ds(c * TPC + t, 1)], ALU.subtract, ALU.mult)
                    last.then_inc(hn_ready, 1)
                    ch.inc(nc.vector.tensor_tensor(y_here[:, :, :], x1[:, ds(c * TPC, TPC), :], x2[:, ds(c * TPC, TPC), :], ALU.add))
                    dve.wait_ge(high_ready, c + 1)
                    nc.vector.tensor_tensor(
                        m_low[:, ds(c, 1), :, :].rearrange("p a j n -> p (a j) n"), mT[:, b, :, :],
                        m_high[:, ds(c, 1), :, :].bitcast(F32).rearrange("p a j n -> p (a j) n"), ALU.subtract
                    ).then_inc(low_ready, 1)
                    dve.wait_ge(logits_done, c + 1)
                    ch.inc(nc.vector.tensor_reduce(top_logit[:, :], logit_ps, AX.X, ALU.max))
                    ch.wait()
                    nc.vector.tensor_tensor(shifted[:, :, :], logit_ps,
                                            top_logit[:, :].unsqueeze(2).to_broadcast([P, TPC, EXPERTS]), ALU.subtract
                                            ).then_inc(shifted_ready, 1)
                    dve.wait_ge(exp_ready, c + 1)
                    ch.inc(nc.vector.tensor_reduce(total[:, :], expd[:, :, :], AX.X, ALU.add))
                    ch.wait()
                    ch.inc(nc.vector.reciprocal(total[:, :], total[:, :]))
                    ch.wait()
                    ch.inc(nc.vector.tensor_tensor(prob[:, :, :], expd[:, :, :],
                                                   total[:, :].unsqueeze(2).to_broadcast([P, TPC, EXPERTS]), ALU.mult))
                    hold()
                    for t in range(TPC):
                        ch.inc(nc.vector.max(top[:, t, :], prob[:, t, :]))
                    hold()
                    for t in range(TPC):
                        last = nc.vector.max_index(top_at[:, t, :], top[:, t, :], prob[:, t, :])
                    ch.inc(last)
                    ch.inc(nc.vector.tensor_tensor(pair[:, :], top[:, :, 0], top[:, :, 1], ALU.add))
                    ch.wait()
                    ch.inc(nc.vector.reciprocal(pair[:, :], pair[:, :]))
                    ch.inc(nc.vector.tensor_scalar(at[:, :, :], top_at[:, :, 0:2], 1.0, None, ALU.mult))
                    ch.wait()
                    ch.inc(nc.vector.tensor_tensor(share[:, :, :], top[:, :, 0:2],
                                                   pair[:, :].unsqueeze(2).to_broadcast([P, TPC, 2]), ALU.mult))
                    ch.wait()
                    for n in range(2):
                        for t in range(TPC):
                            last = nc.vector.tensor_scalar(chosen[:, n, t, :], count[:, :], at[:, t, n:n + 1],
                                                           share[:, t, n:n + 1], ALU.is_equal, ALU.mult)
                    ch.inc(last)
                    ch.wait()
                    nc.vector.tensor_tensor(weights_here[:, :, :], chosen[:, 0, :, :], chosen[:, 1, :, :], ALU.add
                                            ).then_inc(weights_ready, 1)
                    ch.inc(nc.vector.tensor_tensor(weights[:, ds(c * TPC, TPC), :], chosen[:, 0, :, :],
                                                   chosen[:, 1, :, :], ALU.add))
                    dve.wait_ge(b2_done, c + 1)
                    ch.wait()
                    ch.inc(nc.vector.tensor_tensor(x1[:, ds(c * TPC, TPC), :], y_here[:, :, :], b2_ps, ALU.add))
                    ch.wait()
                    dve.sem_inc(b2_added, 1)
                ch.leave(CHUNKS // 2)


def experts(nc, dram, keep):
    with ExitStack() as ctx:
        def sb(name, shape, dt=F32):
            return ctx.enter_context(nc.sbuf_tensor(name, shape, dt))

        def sem(name):
            return ctx.enter_context(nc.semaphore(name))

        acc, m_high, m_low, weights = keep["x_all"], keep["m_high"], keep["m_low"], keep["weights"]
        w1_in = sb("w1_in", [P, HALVES, FF])
        w2_in = sb("w2_in", [P, FT, D])
        b1_in = sb("b1_in", [P, EXPERTS, FT])
        w1_high = sb("w1_high", [P, 2, HALVES, FT, P], F32R)
        w1_low = sb("w1_low", [P, 2, HALVES, FT, P], F32R)
        w2_high = sb("w2_high", [P, 2, FT, D], F32R)
        w2_low = sb("w2_low", [P, 2, FT, D], F32R)
        b1_here = sb("b1_here", [P, 2, FT])
        zero = sb("zero", [P, 1])
        hidden = sb("hidden", [P, 2, CHUNK])
        hidden_high = sb("hidden_high", [P, 4, CHUNK], F32R)
        hidden_low = sb("hidden_low", [P, 4, CHUNK], F32R)
        h_ps = ctx.enter_context(nc.psum_tensor("h_ps", [P, 4, CHUNK], F32))
        y_ps = ctx.enter_context(nc.psum_tensor("y_ps", [P, 2, 2, CHUNK], F32))

        b1_full, zero_set = sem("b1_full"), sem("zero_set")
        w1_full, w2_full, w1_split, w2_split, w_ready = (
            sem("w1_full"), sem("w2_full"), sem("w1_split"), sem("w2_split"), sem("w_ready"))
        w_chain = sem("w_chain")
        h_done, h_read, gelu_done, high_done, low_done, hidden_used = (
            sem("h_done"), sem("h_read"), sem("gelu_done"), sem("high_done"), sem("low_done"), sem("hidden_used"))
        y_done, y_read = sem("y_done"), sem("y_read")
        block = ctx.enter_context(nc.Block())

        def per_step(eng, body, expert=None):
            with eng.Fori(0, EXPERTS // 2) as pair:
                for eb in range(2):
                    if expert is not None:
                        expert(pair * 2 + eb)
                    with eng.Fori(0, CHUNKS // 2) as it:
                        for cb in range(2):
                            body(eng.snap((pair * 2 + eb) * CHUNKS + (it * 2 + cb)), pair * 2 + eb, eb, it * 2 + cb, cb)

        @block.sync
        def _(sp):
            sp.dma_start(b1_in[:, :, :], dram["b1"].rearrange("e (p t) -> p e t", t=FT)).then_inc(b1_full, 16)
            sp.sem_inc(w1_split, 1)
            sp.sem_inc(w2_split, 1)
            with sp.Fori(0, EXPERTS) as e:
                sp.wait_ge(w1_split, e + 1)
                sp.sem_inc(w_chain, 1)
                sp.dma_start(w1_in[:, :, :], dram["W1"][ds(e, 1), :, :].rearrange("a (j p) f -> p (a j) f", p=P)
                             ).then_inc(w1_full, 16)
                sp.wait_ge(w2_split, e + 1)
                sp.sem_inc(w_chain, 1)
                sp.dma_start(w2_in[:, :, :], dram["W2"][ds(e, 1), :, :].rearrange("a (p t) d -> (a p) t d", t=FT)
                             ).then_inc(w2_full, 16)

        @block.gpsimd
        def _(pool):
            nc.gpsimd.memset(zero[:, :], 0.0).then_inc(zero_set, 1)
            pool.wait_ge(zero_set, 1)
            pool.wait_ge(b1_full, 16)
            with pool.Fori(0, EXPERTS // 2) as pair:
                for b in range(2):
                    e = pair * 2 + b
                    pool.wait_ge(y_done, (e + 1) * CHUNKS + 1)
                    pool.wait_ge(w1_full, e * 16 + 16)
                    w1 = w1_in[:, :, :].rearrange("p j (i t) -> p j t i", t=FT)
                    for j in range(HALVES):
                        nc.gpsimd.tensor_tensor(w1_high[:, b, j, :, :], w1[:, j, :, :],
                                                zero[:, :].unsqueeze(2).to_broadcast([P, FT, P]), ALU.add
                                                ).then_inc(w_ready, 1)
                    pool.wait_ge(w_ready, e * 7 + 2)
                    for j in range(HALVES):
                        nc.gpsimd.tensor_tensor(w1_low[:, b, j, :, :], w1[:, j, :, :],
                                                w1_high[:, b, j, :, :].bitcast(F32), ALU.subtract).then_inc(w_ready, 1)
                    pool.wait_ge(w_ready, e * 7 + 4)
                    pool.sem_inc(w1_split, 1)
                    pool.wait_ge(w2_full, e * 16 + 16)
                    nc.gpsimd.tensor_tensor(w2_high[:, b, :, :], w2_in[:, :, :],
                                            zero[:, :].unsqueeze(2).to_broadcast([P, FT, D]), ALU.add).then_inc(w_ready, 1)
                    pool.wait_ge(w_ready, e * 7 + 5)
                    nc.gpsimd.tensor_tensor(w2_low[:, b, :, :], w2_in[:, :, :], w2_high[:, b, :, :].bitcast(F32),
                                            ALU.subtract).then_inc(w_ready, 1)
                    pool.wait_ge(w_ready, e * 7 + 6)
                    pool.sem_inc(w2_split, 1)
                    nc.gpsimd.tensor_copy(b1_here[:, b, :], b1_in[:, ds(e, 1), :].rearrange("p a t -> p (a t)")
                                          ).then_inc(w_ready, 1)
                    pool.wait_ge(w_ready, e * 7 + 7)
                    pool.sem_inc(w_chain, 1)

        @block.tensor
        def _(pe):
            pe.sem_inc(y_done, 2 * CHUNKS + 1)
            pe.sem_inc(hidden_used, 4)

            def step(s, e, eb, c, cb):
                pe.wait_ge(w_ready, e * 7 + 7)
                pe.wait_ge(y_read, s + 1)
                high = m_high[:, ds(c, 1), :, :].rearrange("p a j n -> p (a j) n")
                low = m_low[:, ds(c, 1), :, :].rearrange("p a j n -> p (a j) n")

                def up(f):
                    pe.wait_ge(h_read, s * FT + (f + 1))
                    for j in range(HALVES):
                        for n, (w, m) in enumerate(((w1_high, high), (w1_high, low), (w1_low, high))):
                            last = nc.tensor.matmul(h_ps[:, f % 4, :], w[:, eb, j, f, :], m[:, j, :],
                                                    start=(j == 0 and n == 0), stop=(j == HALVES - 1 and n == 2))
                    last.then_inc(h_done, 1)

                def down(f):
                    pe.wait_ge(low_done, s * FT + (f + 3))
                    for t in range(TPC):
                        cols = slice(P * t, P * t + P)
                        for n, (h, w) in enumerate(((hidden_high, w2_high), (hidden_high, w2_low), (hidden_low, w2_high))):
                            last = nc.tensor.matmul(y_ps[:, cb, t // 2, D * (t % 2):D * (t % 2) + D], h[:, f % 4, cols],
                                                    w[:, eb, f, :], start=(f == 0 and n == 0 and t % 2 == 0),
                                                    stop=(f == FT - 1 and n == 2), skip_group_check=True)
                    last.then_inc(hidden_used, 1)
                    return last

                for f in range(FT):
                    up(f)
                    if f >= 2:
                        down(f - 2)
                down(FT - 2)
                down(FT - 1)
                pe.wait_ge(hidden_used, s * FT + (FT + 4))
                pe.sem_inc(y_done, 1)

            per_step(pe, step)

        @block.scalar
        def _(act):
            act.preload_act_table(ACT.Gelu_apprx_tanh)
            act.sem_inc(h_read, 4)
            act.sem_inc(low_done, 2)

            def step(s, e, eb, c, cb):
                act.wait_ge(w_ready, e * 7 + 7)
                for f in range(FT):
                    act.wait_ge(h_done, s * FT + (f + 1))
                    act.wait_ge(low_done, s * FT + (f + 1))
                    nc.scalar.activation(hidden[:, f % 2, :], h_ps[:, f % 4, :], ACT.Gelu_apprx_tanh,
                                         bias=b1_here[:, eb, f:f + 1]).then_inc(h_read, 1)
                    act.wait_ge(h_read, s * FT + (f + 5))
                    act.wait_ge(hidden_used, s * FT + (f + 1))
                    nc.scalar.activation(hidden_high[:, f % 4, :], hidden[:, f % 2, :], ACT.Copy).then_inc(high_done, 1)

            per_step(act, step)

        @block.vector
        def _(dve):
            dve.sem_inc(y_read, 2)

            def step(s, e, eb, c, cb):
                for f in range(FT):
                    dve.wait_ge(high_done, s * FT + (f + 1))
                    nc.vector.tensor_tensor(hidden_low[:, f % 4, :], hidden[:, f % 2, :],
                                            hidden_high[:, f % 4, :].bitcast(F32), ALU.subtract).then_inc(low_done, 1)
                dve.wait_ge(y_done, s + (2 * CHUNKS + 2))
                for t in range(TPC):
                    rows = acc[:, ds(c * TPC + t, 1), :].rearrange("p a d -> p (a d)")
                    last = nc.vector.scalar_tensor_tensor(
                        rows, y_ps[:, cb, t // 2, D * (t % 2):D * (t % 2) + D],
                        weights[:, ds(c * TPC + t, 1), ds(e, 1)].rearrange("p a b -> p (a b)"), rows, ALU.mult, ALU.add)
                last.then_inc(y_read, 1)

            per_step(dve, step)


def last_norm(nc, dram, keep):
    with ExitStack() as ctx:
        def sem(name):
            return ctx.enter_context(nc.semaphore(name))

        acc, stats = keep["x_all"], keep["stats"]
        mean_var, std, rstd = keep["mean_var"], keep["std"], keep["rstd"]
        rows_out = ctx.enter_context(nc.sbuf_tensor("rows_out", [P, 2, TPC, D], F32))
        var_ready, std_ready, rows_ready, rows_free = sem("var3_ready"), sem("std3_ready"), sem("rows_ready"), sem("rows_free")
        stored = [sem("stored0"), sem("stored1")]
        dve_chain, passed = sem("dve_chain_n"), sem("sync_passed_n")
        out_chunks = dram["out"].rearrange("a (c t p) d -> (a c) p t d", p=P, t=TPC)
        block = ctx.enter_context(nc.Block())

        @block.scalar
        def _(act):
            act.preload_act_table(ACT.Sqrt)
            act.wait_ge(var_ready, 1)
            nc.scalar.activation(std[:, :], std[:, :], ACT.Sqrt).then_inc(std_ready, 1)

        @block.vector
        def _(dve):
            ch = Chain(dve, dve_chain)
            with dve.Fori(0, CHUNKS) as c:
                ch.enter(c, TPC)
                for t in range(TPC):
                    ch.inc(nc.vector.bn_stats(stats[:, ds(c * (TPC * 6) + 6 * t, 6)],
                                              acc[:, ds(c * TPC + t, 1), :].rearrange("p a d -> p (a d)")))
                ch.leave(CHUNKS)
            ch.wait()
            row_statistics(nc, dve, ch, stats, mean_var, std, rstd, var_ready, std_ready, 0)
            with dve.Fori(0, CHUNKS // 2) as it:
                for b in range(2):
                    c = it * 2 + b
                    dve.wait_ge(rows_free, c + 1)
                    for t in range(TPC):
                        last = nc.vector.tensor_scalar(
                            rows_out[:, b, t, :], acc[:, ds(c * TPC + t, 1), :].rearrange("p a d -> p (a d)"),
                            mean_var[:, ds(c * TPC + t, 1), 0], rstd[:, ds(c * TPC + t, 1)], ALU.subtract, ALU.mult)
                    last.then_inc(rows_ready, 1)

        @block.sync
        def _(sp):
            sp.sem_inc(rows_free, 2)
            with sp.Fori(0, CHUNKS // 2) as it:
                for b in range(2):
                    c = it * 2 + b
                    sp.wait_ge(rows_ready, c + 1)
                    sp.sem_inc(passed, 1)
                    sp.dma_start(out_chunks[ds(c, 1), :, :, :].rearrange("a p t d -> (a p) t d"), rows_out[:, b, :, :]
                                 ).then_inc(stored[b], 16)
                    sp.wait_ge(stored[b], it * 16 + 16)
                    sp.sem_inc(rows_free, 1)
            for b in range(2):
                sp.wait_ge(stored[b], 16 * CHUNKS // 2)


def program(nc, dram):
    def left(stack, name, shape, dt=F32):
        return stack.enter_context(nc.sbuf_tensor(name, shape, dt))

    def right(stack, name, shape, dt=F32):
        return stack.enter_context(nc.sbuf_tensor(name, shape, dt, side="right"))

    with ExitStack() as whole:
        keep = {
            "ident": left(whole, "ident", [P, P]),
            "x_all": left(whole, "x_all", [P, TILES, D]),
            "stats": left(whole, "row_stats", [P, TILES * 6]),
            "mean_var": left(whole, "row_mean_var", [P, TILES, 2]),
            "std": left(whole, "row_std", [P, TILES]),
            "rstd": left(whole, "row_rstd", [P, TILES]),
            "weights": left(whole, "weights", [P, TILES, EXPERTS]),
        }
        with ExitStack() as through_routing:
            keep["v_all"] = right(through_routing, "v_all", [P, TILES, D])
            with ExitStack() as through_attention:
                keep["ctx_slots"] = right(through_attention, "ctx_slots", [P, RING + 1, TPC, DH])
                linear_attention(nc, dram, keep)
                softmax_attention(nc, dram, keep)
                output_projection(nc, dram, keep)
            for name in ("m_high", "m_low"):
                keep[name] = left(whole, name, [P, CHUNKS, HALVES, CHUNK], F32R)
            routing(nc, dram, keep)
        experts(nc, dram, keep)
        last_norm(nc, dram, keep)


_INS = ["x", "q_proj", "k_proj", "ln1_g", "ln1_b", "ln2_g", "ln2_b", "Wq", "Wk", "Wv", "Wo", "Wg", "W1", "b1", "W2", "b2"]
_OF = {"x": "L0_attn_x", "q_proj": "L0_attn_q_proj", "k_proj": "L0_attn_k_proj"}


def kernel(**inputs):
    import numpy as np
    import concourse.bacc as bacc
    from concourse.bass_utils import run_bass_kernel_spmd as run

    nc = bacc.Bacc("TRN2", target_bir_lowering=False, num_devices=1)
    arrays, dram = {}, {}
    for name in _INS:
        a = np.ascontiguousarray(inputs[_OF.get(name, "L0_ffn_" + name)])
        arrays["in_" + name] = a
        dram[name] = nc.dram_tensor("in_" + name, a.shape, F32, kind="ExternalInput").ap()
    for name in ("qs", "ks"):
        dram[name] = nc.dram_tensor(name + "_dram", (PARTS, D, TOKENS), BF16).ap()
    dram["out"] = nc.dram_tensor("out_0", (1, TOKENS, D), F32, kind="ExternalOutput").ap()
    program(nc, dram)
    r = run(nc, [arrays], core_ids=[0])
    return r.results[0]["out_0"]
```

```python
import concourse.bass as bass
from concourse import mybir
from concourse.alu_op_type import AluOpType as ALU
from contextlib import ExitStack

F32 = mybir.dt.float32
F32R = mybir.dt.float32r
BF16 = mybir.dt.bfloat16
F16 = mybir.dt.float16
U32 = mybir.dt.uint32
I32 = mybir.dt.int32
ACT = mybir.ActivationFunctionType
AX = mybir.AxisListType
ds = bass.ds

P = 128
TOKENS, D = 4096, 256
HALVES = D // P
TILES = TOKENS // P
CHUNK = 512
CHUNKS = TOKENS // CHUNK
TPC = CHUNK // P
PROJ = 64
HEADS, DH = 16, 16
EXPERTS, FF = 8, 1024
FT = FF // P
TOP = 2
SLOT_TILES = (TOP * TOKENS + EXPERTS * (CHUNK - 1)) // CHUNK
EPS = 1e-5
Z_EPS = 1e-8
PARTS = 3

Q_PARTS = (0, 0, 0, 1, 1, 2)
K_PARTS = (0, 1, 2, 0, 1, 0)
SROWS = len(Q_PARTS) * DH
MROWS = 2
AROWS = SROWS + MROWS

V_ONE = PARTS * DH
V_COLS = 64
O_COLS = DH + 1

STEP = 2 * P
STEPS = TOKENS // STEP
KCH = TOKENS // CHUNK // 2
UNITS = TPC * KCH
HALF = CHUNK // 2
LEAST = -3.4e38
LAG = 3
BUFS = 4
POOL_SPLITS = tuple(t for t in range(STEPS) if (t + 1) * 5 // STEPS > t * 5 // STEPS)
DVE_SPLITS = tuple(t for t in range(STEPS) if t not in POOL_SPLITS)
RING = HEADS * CHUNKS


class Chain:

    def __init__(self, eng, sem):
        self.eng, self.sem, self.base, self.n = eng, sem, 0, 0

    def enter(self, it, per):
        self.outer, self.per, self.before = self.base, per, self.n
        self.base, self.n = self.base + self.n + it * per, 0

    def leave(self, rounds):
        assert self.n == self.per, (self.n, self.per)
        self.base, self.n = self.outer, self.before + self.per * rounds

    def inc(self, ins):
        ins.then_inc(self.sem, 1)
        self.n += 1

    def wait(self):
        self.eng.wait_ge(self.sem, self.base + self.n)


def linear_attention(nc, dram, keep):
    with ExitStack() as ctx:
        def sb(name, shape, dt=F32):
            return ctx.enter_context(nc.sbuf_tensor(name, shape, dt))

        def ps(name, shape, dt=F32):
            return ctx.enter_context(nc.psum_tensor(name, shape, dt))

        def sem(name):
            return ctx.enter_context(nc.semaphore(name))

        x_all, v_all, ident = keep["x_all"], keep["v_all"], keep["ident"]
        x_in = sb("x_in", [P, 2, TPC, D])
        xT = sb("xT", [P, 2, HALVES, CHUNK])
        proj_q = sb("proj_q", [P, HALVES, PROJ])
        proj_k = sb("proj_k", [P, HALVES, PROJ])
        w_qkv = sb("w_qkv", [P, 3, HALVES, D])
        gain1 = sb("gain1", [P, HALVES])
        bias1 = sb("bias1", [P, HALVES])
        k_feat = sb("k_feat", [P, 2, TPC, PROJ])
        q_feat = sb("q_feat", [PROJ, TOKENS])
        q_here = sb("q_here", [PROJ, 2, CHUNK])
        kv = sb("kv", [PROJ, D + 1])
        z = sb("z", [P, TPC])
        y_here = sb("y_here", [P, TPC, D])
        stats_here = sb("stats_here", [P, TPC * 6])
        stats = sb("stats", [P, TILES * 6])
        mean_var = sb("mean_var", [P, TILES, 2])
        std = sb("std", [P, TILES])
        rstd = sb("rstd", [P, TILES])
        hn = sb("hn", [P, 2, TPC, D])
        hT = sb("hT", [P, 2, HALVES, CHUNK])
        k_diff = sb("k_diff", [P, HALVES, HALF])
        rest = sb("rest", [P, 5, CHUNK])
        parts = sb("parts", [P, 2, 5, PARTS, CHUNK], BF16)

        banks = ps("banks", [P, 8, CHUNK])
        tr_ps = banks[:, 0:2, :]
        kf_ps = banks[:, 2, 0:TPC * PROJ].rearrange("p (t e) -> p t e", t=TPC)
        qf_ps = banks[0:PROJ, 3, :]
        kv_ps = banks[0:PROJ, 2, 0:D]
        num_ps = banks[:, 4:8, 0:D + 1]
        qk_ps = banks[:, 2:6, :]
        v_ps = banks[:, 6:8, :].rearrange("p b (t d) -> p (b t) d", t=2)

        proj_in, weights_in, affine_in = sem("proj_in"), sem("weights_in"), sem("affine_in")
        consts_set = sem("consts_set")
        x_in_full, x_in_free = [sem("x_in_full0"), sem("x_in_full1")], sem("x_in_free")
        x_all_full = sem("x_all_full")
        xT_in_psum, xT_ready = sem("xT_in_psum"), sem("xT_ready")
        feat_in_psum, feat_ready = sem("feat_in_psum"), sem("feat_ready")
        kv_in_psum, kv_added = sem("kv_in_psum"), sem("kv_added")
        q_here_ready = sem("q_here_ready")
        num_in_psum, y_ready = sem("num_in_psum"), sem("y_ready")
        var_ready, std_ready = sem("var_ready"), sem("std_ready")
        hn_ready, hnT_in_psum, hT_ready = sem("hn_ready"), sem("hnT_in_psum"), sem("hT_ready")
        qk_in_psum, v_in_psum, v_copied = sem("qk_in_psum"), sem("v_in_psum"), sem("v_copied")
        high_ready, rest_ready, mid_ready, low_ready = (
            sem("high_ready"), sem("rest_ready"), sem("mid_ready"), sem("low_ready"))
        parts_out = [sem("parts_out0"), sem("parts_out1")]
        parts_free = sem("parts_free")
        half_copied = sem("half_copied")
        diff_ready, x1_ready, x1_out = sem("diff_ready"), sem("x1_ready"), sem("x1_out")
        dve_chain = sem("dve_chain")

        x_chunks = dram["x"].rearrange("a (c t p) d -> (a c) p t d", p=P, t=TPC)
        block = ctx.enter_context(nc.Block())

        @block.sync
        def _(sp):
            sp.dma_start(proj_q[:, :, :], dram["q_proj"].rearrange("(j p) e -> p j e", p=P)).then_inc(proj_in, 16)
            sp.dma_start(proj_k[:, :, :], dram["k_proj"].rearrange("(j p) e -> p j e", p=P)).then_inc(proj_in, 16)
            with sp.Fori(0, CHUNKS // 2) as it:
                for b in range(2):
                    c = it * 2 + b
                    sp.wait_ge(x_in_free, c + 1)
                    sp.dma_start(x_in[:, b, :, :], x_chunks[ds(c, 1), :, :, :].rearrange("a p t d -> (a p) t d")
                                 ).then_inc(x_in_full[b], 16)
            sp.dma_start(x_all[:, :, :], dram["x"].rearrange("a (t p) d -> p (a t) d", p=P)).then_inc(x_all_full, 16)
            for n, w in enumerate(("Wq", "Wk", "Wv")):
                sp.dma_start(w_qkv[:, n, :, :], dram[w].rearrange("(j p) e -> p j e", p=P)).then_inc(weights_in, 16)
            sp.wait_ge(x1_ready, 1)
            sp.dma_start(dram["x1"], x_all[:, :, :]).then_inc(x1_out, 16)
            sp.sem_inc(parts_free, 2)
            with sp.Fori(0, CHUNKS // 2) as it:
                for b in range(2):
                    c = it * 2 + b
                    for s in range(4):
                        sp.wait_ge(low_ready, c * 5 + (s + 1))
                        dst = dram["qs" if s < 2 else "ks"][:, P * (s % 2):P * (s % 2) + P, ds(c * CHUNK, CHUNK)]
                        sp.dma_start(dst.rearrange("n p t -> p n t"), parts[:, b, s, :, :]).then_inc(parts_out[b], 16)
                    sp.wait_ge(low_ready, c * 5 + 5)
                    for j in range(HALVES):
                        dst = dram["kd"][:, P * j:P * j + P, ds(c * HALF, HALF)]
                        sp.dma_start(dst.rearrange("n p t -> p n t"), parts[:, b, 4, :, HALF * j:HALF * j + HALF]
                                     ).then_inc(parts_out[b], 16)
                    sp.wait_ge(parts_out[b], it * 96 + 96)
                    sp.sem_inc(parts_free, 1)
            for b in range(2):
                sp.wait_ge(parts_out[b], 16 * 6 * CHUNKS // 2)
            sp.wait_ge(x1_out, 16)

        @block.gpsimd
        def _(pool):
            nc.gpsimd.memset(ident[:, :], 0.0).then_inc(consts_set, 1)
            nc.gpsimd.memset(kv[:, :], 0.0).then_inc(consts_set, 1)
            pool.wait_ge(consts_set, 2)
            nc.gpsimd.affine_select(out=ident[:, :], in_=ident[:, :], compare_op=ALU.not_equal, fill=1.0,
                                    base=0, pattern=[[-1, P]], channel_multiplier=1).then_inc(consts_set, 1)
            nc.gpsimd.memset(kv[:, D:D + 1], 1.0).then_inc(consts_set, 1)
            pool.dma_start(gain1[:, :], dram["ln1_g"].rearrange("(j p) -> p j", p=P), allow_slow_non_contiguous=True).then_inc(affine_in, 16)
            pool.dma_start(bias1[:, :], dram["ln1_b"].rearrange("(j p) -> p j", p=P), allow_slow_non_contiguous=True).then_inc(affine_in, 16)
        @block.tensor
        def _(pe):
            pe.sem_inc(x_in_free, 2)
            pe.wait_ge(consts_set, 4)
            pe.wait_ge(proj_in, 32)
            with pe.Fori(0, CHUNKS // 2) as it:
                for b in range(2):
                    c = it * 2 + b
                    pe.wait_ge(x_in_full[b], it * 16 + 16)
                    for j in range(HALVES):
                        for t in range(TPC):
                            last = nc.tensor.transpose(tr_ps[:, j, P * t:P * t + P],
                                                       x_in[:, b, t, P * j:P * j + P], ident[:, :])
                    last.then_inc(xT_in_psum, 1)
                    pe.wait_ge(xT_ready, c * 2 + 2)
                    for t in range(TPC):
                        for j in range(HALVES):
                            nc.tensor.matmul(kf_ps[:, t, :], xT[:, b, j, P * t:P * t + P], proj_k[:, j, :],
                                             start=(j == 0), stop=(j == HALVES - 1))
                    for j in range(HALVES):
                        last = nc.tensor.matmul(qf_ps, proj_q[:, j, :], xT[:, b, j, :],
                                                start=(j == 0), stop=(j == HALVES - 1))
                    last.then_inc(feat_in_psum, 1)
                    pe.wait_ge(feat_ready, c * 2 + 2)
                    for t in range(TPC):
                        last = nc.tensor.matmul(kv_ps, k_feat[:, b, t, :], x_in[:, b, t, :],
                                                start=(t == 0), stop=(t == TPC - 1))
                    last.then_inc(kv_in_psum, 1)
                    pe.wait_ge(kv_added, c + 1)
                    pe.sem_inc(x_in_free, 1)
            with pe.Fori(0, CHUNKS // 2) as it:
                for b in range(2):
                    c = it * 2 + b
                    pe.wait_ge(q_here_ready, c + 1)
                    pe.wait_ge(y_ready, c * TPC + TPC)
                    for t in range(TPC):
                        last = nc.tensor.matmul(num_ps[:, t, :], q_here[:, b, P * t:P * t + P], kv[:, :],
                                                start=True, stop=True)
                    last.then_inc(num_in_psum, 1)
            pe.wait_ge(weights_in, 3 * 16)
            pe.wait_ge(y_ready, TILES + TPC)
            with pe.Fori(0, CHUNKS // 2) as it:
                for b in range(2):
                    c = it * 2 + b
                    pe.wait_ge(hn_ready, c + 1)
                    for j in range(HALVES):
                        for t in range(TPC):
                            last = nc.tensor.transpose(tr_ps[:, j, P * t:P * t + P],
                                                       hn[:, b, t, P * j:P * j + P], ident[:, :])
                    last.then_inc(hnT_in_psum, 1)
                    pe.wait_ge(hT_ready, c * 2 + 2)
                    for s in range(4):
                        pe.wait_ge(rest_ready, c * 5 + (s + 1))
                        for j in range(HALVES):
                            last = nc.tensor.matmul(qk_ps[:, s, :], w_qkv[:, s // 2, j, P * (s % 2):P * (s % 2) + P],
                                                    hT[:, b, j, :], start=(j == 0), stop=(j == HALVES - 1))
                        last.then_inc(qk_in_psum, 1)
                    pe.wait_ge(v_copied, c * 2 + 2)
                    for t in range(TPC):
                        for j in range(HALVES):
                            last = nc.tensor.matmul(v_ps[:, t, :], hT[:, b, j, P * t:P * t + P], w_qkv[:, 2, j, :],
                                                    start=(j == 0), stop=(j == HALVES - 1))
                        if t % 2:
                            last.then_inc(v_in_psum, 1)

        @block.scalar
        def _(act):
            act.preload_act_table(ACT.Exp)
            with act.Fori(0, CHUNKS // 2) as it:
                for b in range(2):
                    c = it * 2 + b
                    act.wait_ge(xT_in_psum, c + 1)
                    for j in range(HALVES):
                        nc.scalar.activation(xT[:, b, j, :], tr_ps[:, j, :], ACT.Copy).then_inc(xT_ready, 1)
                    act.wait_ge(feat_in_psum, c + 1)
                    nc.scalar.activation(k_feat[:, b, :, :], kf_ps, ACT.Exp).then_inc(feat_ready, 1)
                    nc.scalar.activation(q_feat[:, ds(c * CHUNK, CHUNK)], qf_ps, ACT.Exp).then_inc(feat_ready, 1)
            act.wait_ge(feat_ready, 2 * CHUNKS)
            act.sem_inc(num_in_psum, 1)
            with act.Fori(0, CHUNKS // 2) as it:
                for b in range(2):
                    c = it * 2 + b
                    act.wait_ge(num_in_psum, c + 1)
                    nc.scalar.activation(q_here[:, b, :], q_feat[:, ds(c * CHUNK, CHUNK)], ACT.Copy
                                         ).then_inc(q_here_ready, 1)
            act.preload_act_table(ACT.Sqrt)
            for n in range(2):
                act.wait_ge(var_ready, n + 1)
                nc.scalar.activation(std[:, :], std[:, :], ACT.Sqrt).then_inc(std_ready, 1)
            act.preload_act_table(ACT.Exp)
            act.wait_ge(affine_in, 2 * 16)
            act.sem_inc(v_copied, 2)
            with act.Fori(0, CHUNKS // 2) as it:
                for b in range(2):
                    c = it * 2 + b
                    act.wait_ge(hnT_in_psum, c + 1)
                    for j in range(HALVES):
                        nc.scalar.activation(hT[:, b, j, :], tr_ps[:, j, :], ACT.Identity,
                                             bias=bias1[:, j:j + 1], scale=gain1[:, j:j + 1]).then_inc(hT_ready, 1)
                    act.wait_ge(parts_free, c + 1)
                    for s in range(4):
                        act.wait_ge(qk_in_psum, c * 4 + (s + 1))
                        nc.scalar.activation(parts[:, b, s, 0, :], qk_ps[:, s, :], ACT.Copy,
                                             scale=(DH ** -0.5 if s < 2 else 1.0)).then_inc(high_ready, 1)
                    act.wait_ge(diff_ready, c + 1)
                    nc.scalar.activation(parts[:, b, 4, 0, :], k_diff[:, :, :], ACT.Copy).then_inc(high_ready, 1)
                    for s in range(5):
                        act.wait_ge(rest_ready, c * 5 + (s + 6))
                        nc.scalar.activation(parts[:, b, s, 1, :], rest[:, s, :], ACT.Copy).then_inc(mid_ready, 1)
                    for n in range(2):
                        act.wait_ge(v_in_psum, c * 2 + (n + 1))
                        nc.scalar.activation(v_all[:, ds(c * TPC + 2 * n, 2), :], v_ps[:, 2 * n:2 * n + 2, :],
                                             ACT.Copy).then_inc(v_copied, 1)

        @block.vector
        def _(dve):
            ch = Chain(dve, dve_chain)
            dve.wait_ge(consts_set, 4)
            with dve.Fori(0, CHUNKS) as c:
                dve.wait_ge(kv_in_psum, c + 1)
                nc.vector.tensor_tensor(kv[:, 0:D], kv[:, 0:D], kv_ps, ALU.add).then_inc(kv_added, 1)
                dve.wait_ge(kv_added, c + 1)
            dve.wait_ge(x_all_full, 16)
            dve.sem_inc(y_ready, TPC)

            def tile(c, t):
                return x_all[:, ds(c * TPC + t, 1), :].rearrange("p a d -> p (a d)")

            def keep_rows(c):
                ch.wait()
                for t in range(TPC):
                    ch.inc(nc.vector.bn_stats(stats_here[:, 6 * t:6 * t + 6], y_here[:, t, :]))
                ch.wait()
                ch.inc(nc.vector.tensor_scalar(stats[:, ds(c * TPC * 6, TPC * 6)], stats_here[:, :], 1.0, None, ALU.mult))
                ch.inc(nc.vector.tensor_scalar(x_all[:, ds(c * TPC, TPC), :], y_here[:, :, :], 1.0, None, ALU.mult))
                ch.wait()

            def reciprocal_std(n):
                for t in range(TILES):
                    ch.inc(nc.vector.bn_aggr(mean_var[:, t, :], stats[:, 6 * t:6 * t + 6]))
                ch.wait()
                nc.vector.tensor_scalar(std[:, :], mean_var[:, :, 1], EPS, None, ALU.add).then_inc(var_ready, 1)
                dve.wait_ge(std_ready, n + 1)
                ch.inc(nc.vector.reciprocal(rstd[:, :], std[:, :]))
                ch.wait()

            with dve.Fori(0, CHUNKS) as c:
                dve.wait_ge(num_in_psum, c + 2)
                ch.enter(c, 2 + 2 * TPC + 2)
                ch.inc(nc.vector.tensor_scalar(z[:, :], num_ps[:, :, D], Z_EPS, None, ALU.add))
                ch.wait()
                ch.inc(nc.vector.reciprocal(z[:, :], z[:, :]))
                ch.wait()
                for t in range(TPC):
                    ch.inc(nc.vector.scalar_tensor_tensor(y_here[:, t, :], num_ps[:, t, 0:D], z[:, t:t + 1], tile(c, t),
                                                          ALU.mult, ALU.add))
                keep_rows(c)
                ch.leave(CHUNKS)
                dve.sem_inc(y_ready, TPC)
            reciprocal_std(0)
            with dve.Fori(0, CHUNKS) as c:
                ch.enter(c, 2 * TPC + 2)
                for t in range(TPC):
                    ch.inc(nc.vector.tensor_scalar(
                        y_here[:, t, :], tile(c, t), mean_var[:, ds(c * TPC + t, 1), 0], rstd[:, ds(c * TPC + t, 1)],
                        ALU.subtract, ALU.mult))
                keep_rows(c)
                ch.leave(CHUNKS)
            reciprocal_std(1)
            dve.sem_inc(x1_ready, 1)
            dve.sem_inc(rest_ready, 5)

            def normalize(c, b):
                for t in range(TPC):
                    last = nc.vector.tensor_scalar(
                        hn[:, b, t, :], tile(c, t), mean_var[:, ds(c * TPC + t, 1), 0], rstd[:, ds(c * TPC + t, 1)],
                        ALU.subtract, ALU.mult)
                last.then_inc(hn_ready, 1)

            with dve.Fori(0, CHUNKS // 2) as it:
                for b in range(2):
                    c = it * 2 + b
                    normalize(c, b)
                    for s in range(4):
                        if s == 2:
                            dve.wait_ge(high_ready, c * 5 + 4)
                            nc.vector.tensor_scalar(k_diff[:, :, :], qk_ps[:, 2:4, HALF:CHUNK], 1.0, None, ALU.mult
                                                    ).then_inc(half_copied, 1)
                            dve.wait_ge(half_copied, c + 1)
                            nc.vector.tensor_tensor(k_diff[:, :, :], qk_ps[:, 2:4, 0:HALF], k_diff[:, :, :],
                                                    ALU.subtract).then_inc(diff_ready, 1)
                        dve.wait_ge(high_ready, c * 5 + (s + 1))
                        nc.vector.scalar_tensor_tensor(rest[:, s, :], qk_ps[:, s, :], DH ** -0.5 if s < 2 else 1.0,
                                                       parts[:, b, s, 0, :], ALU.mult, ALU.subtract
                                                       ).then_inc(rest_ready, 1)
                    dve.wait_ge(high_ready, c * 5 + 5)
                    nc.vector.tensor_tensor(rest[:, 4, :].rearrange("p (j t) -> p j t", j=HALVES), k_diff[:, :, :],
                                            parts[:, b, 4, 0, :].rearrange("p (j t) -> p j t", j=HALVES), ALU.subtract
                                            ).then_inc(rest_ready, 1)
                    for s in range(5):
                        dve.wait_ge(mid_ready, c * 5 + (s + 1))
                        nc.vector.tensor_tensor(parts[:, b, s, 2, :], rest[:, s, :], parts[:, b, s, 1, :], ALU.subtract
                                                ).then_inc(low_ready, 1)


def softmax_attention(nc, dram, keep):
    with ExitStack() as ctx:
        def sb(name, shape, dt=F32):
            return ctx.enter_context(nc.sbuf_tensor(name, shape, dt))

        def ps(name, shape, dt=F32):
            return ctx.enter_context(nc.psum_tensor(name, shape, dt))

        def sem(name):
            return ctx.enter_context(nc.semaphore(name))

        v_all, ident, ctx_slots = keep["v_all"], keep["ident"], keep["ctx_slots"]
        q_ring = sb("q_ring", [AROWS, 2 * TOKENS], BF16)
        k_ring = sb("k_ring", [AROWS, 2 * TOKENS], BF16)
        kd_ring = sb("kd_ring", [SROWS, 2 * TOKENS // 2], BF16)
        v_parts = sb("v_parts", [P, 2, TILES, V_COLS], BF16)
        v_here = sb("v_here", [P, TILES, DH])
        v_rest = sb("v_rest", [P, TILES, DH])
        zeros = sb("zeros", [P, TILES, DH])
        gather = sb("gather", [P, O_COLS])
        probs = sb("probs", [P, BUFS, STEP // P, CHUNK])
        probs_low = sb("probs_low", [P, BUFS, STEP // P, CHUNK], F16)
        excess = sb("excess", [P, 2, CHUNK])
        unit_max = sb("unit_max", [P, TPC, KCH])
        tile_max = sb("tile_max", [P, TPC])
        max_parts = sb("max_parts", [TPC, MROWS, P], BF16)
        o_here = sb("o_here", [P, CHUNK])
        o_scale = sb("o_scale", [P, TPC])

        s2_ps = ps("s2_ps", [P, STEP // P, CHUNK])
        diff_ps = ps("diff_ps", [P, 2, CHUNK])
        b_ps = ps("b_ps", [P, 2, CHUNK])
        o_ps = ps("o_ps", [P, CHUNK])
        misc_ps = ps("misc_ps", [P, CHUNK])
        out_ps = misc_ps[:, 0:TPC * O_COLS].rearrange("p (t c) -> p t c", t=TPC)
        maxT_ps = misc_ps[0:TPC, P:2 * P]

        qk_in, head_ready = sem("qk_in"), sem("head_ready")
        v_ready, consts_ready, gather_ready = sem("v_ready"), sem("consts_ready"), sem("gather_ready")
        s2_done, exp_done, low_done, pv_done = sem("s2_done"), sem("exp_done"), sem("low_done"), sem("pv_done")
        pool_low_done = sem("pool_low_done")
        diff_done, b_done, excess_ready = sem("diff_done"), sem("b_done"), sem("excess_ready")
        s1_read, tile_max_done = sem("s1_read"), sem("tile_max_done")
        maxT_done, max_split, rows_made = sem("maxT_done"), sem("max_split"), sem("rows_made")
        row_in, rows_in = sem("row_in"), sem("rows_in")
        o_copied, o_turned, o_scaled, o_stored = sem("o_copied"), sem("o_turned"), sem("o_scaled"), sem("o_stored")
        pool_chain, start_values, sync_passed = sem("pool_chain"), sem("start_values"), sem("sync_passed")
        pool_passed, dve_passed = sem("pool_passed"), sem("dve_passed")

        def per_step(eng, body):
            def steps(head, par, last_ahead):
                with eng.Fori(0, 1) as qc:
                    body(head * CHUNKS + qc, head, par, 1 - par, qc, True)
                with eng.Fori(1, CHUNKS) as qc:
                    body(head * CHUNKS + qc, head, par, par, qc, last_ahead)

            with eng.Fori(0, HEADS // 2 - 1) as pair:
                for par in range(2):
                    steps(pair * 2 + par, par, True)
            steps(HEADS - 2, 0, True)
            steps(HEADS - 1, 1, False)

        block = ctx.enter_context(nc.Block())

        @block.sync
        def _(sp):
            def load_head(h, col, kd_col):
                for ring, src, of in ((q_ring, "qs", Q_PARTS), (k_ring, "ks", K_PARTS)):
                    for n, part in enumerate(of):
                        sp.dma_start(ring[DH * n:DH * n + DH, ds(col, TOKENS)],
                                     dram[src][part, ds(h * DH, DH), :]).then_inc(qk_in, 16)
                for n, part in enumerate(K_PARTS):
                    sp.dma_start(kd_ring[DH * n:DH * n + DH, ds(kd_col, TOKENS // 2)],
                                 dram["kd"][part, ds(h * DH, DH), :]).then_inc(qk_in, 16)
                sp.wait_ge(qk_in, (h + 1) * (3 * len(Q_PARTS) * 16))
                sp.sem_inc(head_ready, 1)

            def rows(n):
                col = sp.snap(((n + 15) & 15) * CHUNK)
                sp.wait_ge(rows_made, n + 2)
                sp.sem_inc(sync_passed, 1)
                for r in range(MROWS):
                    sp.dma_start(q_ring[SROWS + r:SROWS + r + 1, ds(col, CHUNK)].rearrange("a (t n) -> a t n", t=TPC),
                                 max_parts[:, r, :]).then_inc(row_in, 16)
                sp.wait_ge(row_in, n * (MROWS * 16) + MROWS * 16)
                sp.sem_inc(rows_in, 1)

            load_head(sp.snap(0), sp.snap(0), sp.snap(0))
            with sp.Fori(0, CHUNKS - 1) as n:
                rows(n)
            with sp.Fori(0, HEADS - 1) as h:
                next_head, col = sp.snap(h + 1), sp.snap(((h + 1) & 1) * TOKENS)
                sp.wait_ge(pv_done, h * (CHUNKS * STEPS) + 4)
                sp.sem_inc(sync_passed, 1)
                load_head(next_head, col, sp.snap(((h + 1) & 1) * (TOKENS // 2)))
                with sp.Fori(0, CHUNKS) as qc:
                    rows(h * CHUNKS + (qc + CHUNKS - 1))
            with sp.Fori(0, CHUNKS) as qc:
                rows(qc + HEADS * CHUNKS - 1)

        @block.gpsimd
        def _(pool):
            ch = Chain(pool, pool_chain)
            nc.gpsimd.memset(k_ring[SROWS:AROWS, :], 1.0).then_inc(consts_ready, 1)
            pool.wait_ge(consts_ready, 1)
            nc.gpsimd.memset(v_parts[:, :, :, V_ONE:V_COLS], 0.0).then_inc(consts_ready, 1)
            nc.gpsimd.memset(zeros[:, :, :], 0.0).then_inc(consts_ready, 1)
            pool.wait_ge(consts_ready, 3)
            nc.gpsimd.memset(v_parts[:, :, :, V_ONE:V_ONE + 1], 1.0).then_inc(consts_ready, 1)
            ch.inc(nc.gpsimd.tensor_tensor(gather[:, 0:DH], ident[:, 0:DH], ident[:, DH:2 * DH], ALU.add))
            for r in (2 * DH, V_COLS, V_COLS + DH, V_COLS + 2 * DH):
                ch.wait()
                ch.inc(nc.gpsimd.tensor_tensor(gather[:, 0:DH], gather[:, 0:DH], ident[:, r:r + DH], ALU.add))
            nc.gpsimd.tensor_tensor(gather[:, DH:O_COLS], ident[:, V_ONE:V_ONE + 1],
                                    ident[:, V_COLS + V_ONE:V_COLS + V_ONE + 1], ALU.add).then_inc(gather_ready, 1)

            def split_v(h, par):
                high, mid, low = (v_parts[:, par, :, DH * n:DH * n + DH] for n in range(PARTS))
                ch.inc(nc.gpsimd.tensor_copy(v_here[:, :, :], v_all[:, :, ds(h * DH, DH)]))
                ch.wait()
                ch.inc(nc.gpsimd.tensor_tensor(high, v_here[:, :, :], zeros[:, :, :], ALU.add))
                ch.wait()
                ch.inc(nc.gpsimd.tensor_tensor(v_rest[:, :, :], v_here[:, :, :], high, ALU.subtract))
                ch.wait()
                ch.inc(nc.gpsimd.tensor_tensor(mid, v_rest[:, :, :], zeros[:, :, :], ALU.add))
                ch.wait()
                nc.gpsimd.tensor_tensor(low, v_rest[:, :, :], mid, ALU.subtract).then_inc(v_ready, 1)
                pool.wait_ge(v_ready, h + 1)
                pool.sem_inc(pool_passed, 1)

            def split_probs(i):
                for t in POOL_SPLITS:
                    high = probs[:, t % BUFS, :, :].bitcast(BF16).rearrange("p k (n two) -> p k n two", two=2)
                    pool.wait_ge(exp_done, i * (2 * STEPS) + (2 * t + 4))
                    pool.sem_inc(pool_passed, 1)
                    nc.gpsimd.tensor_tensor(probs_low[:, t % BUFS, :, :], probs[:, t % BUFS, :, :], high[:, :, :, 1],
                                            ALU.subtract).then_inc(pool_low_done, 1)

            def split_head(head, lo=0):
                with pool.Fori(lo, CHUNKS) as qc:
                    split_probs(pool.snap(head * CHUNKS + qc))

            pool.wait_ge(consts_ready, 4)
            for h in range(2):
                split_v(h, h)
            pool.wait_ge(start_values, 4)
            pool.sem_inc(pool_low_done, len(POOL_SPLITS))
            split_head(0)
            with pool.Fori(0, HEADS // 2 - 1) as pair:
                ch.enter(pair, 8)
                for par in range(2):
                    split_probs(pool.snap((pair * 2 + (par + 1)) * CHUNKS))
                    pool.wait_ge(pv_done, (pair * 2 + (par + 1)) * (CHUNKS * STEPS) + 4)
                    split_v(pair * 2 + (par + 2), par)
                    split_head(pair * 2 + (par + 1), 1)
                ch.leave(HEADS // 2 - 1)
            split_head(HEADS - 1)

        @block.tensor
        def _(pe):
            pe.wait_ge(consts_ready, 4)
            pe.wait_ge(gather_ready, 1)
            pe.wait_ge(v_ready, 2)
            pe.sem_inc(o_turned, 1)
            pe.sem_inc(pv_done, 1)

            def diff_unit(n, u):
                pe.wait_ge(excess_ready, n * UNITS + (u + 1))
                q = (n & 15) * CHUNK + P * (u // KCH)
                k = ((n >> 3) & 1) * (TOKENS // 2) + CHUNK * (u % KCH)
                nc.tensor.matmul(diff_ps[:, u % 2, :], q_ring[0:SROWS, ds(q, P)], kd_ring[:, ds(k, CHUNK)],
                                 start=True, stop=True).then_inc(diff_done, 1)

            def b_unit(n, u):
                pe.wait_ge(s1_read, n * UNITS + (u + 1))
                q = (n & 15) * CHUNK + P * (u // KCH)
                k = ((n >> 3) & 1) * TOKENS + 2 * CHUNK * (u % KCH)
                keys = k_ring[0:SROWS, ds(k, 2 * CHUNK)].rearrange("r (c h n) -> r c h n", c=2, h=2)
                nc.tensor.matmul(b_ps[:, u % 2, :], q_ring[0:SROWS, ds(q, P)], keys[:, :, 1, :],
                                 start=True, stop=True).then_inc(b_done, 1)

            def turn_max(n):
                pe.wait_ge(tile_max_done, n + 1)
                pe.wait_ge(rows_made, n + 1)
                nc.tensor.transpose(maxT_ps, tile_max[:, :], ident[:, :]).then_inc(maxT_done, 1)

            def turn_o(i):
                pe.wait_ge(o_copied, i + 1)
                pe.wait_ge(o_stored, i + 1)
                for t in range(TPC):
                    last = nc.tensor.matmul(out_ps[:, t, :], o_here[:, P * t:P * t + P], gather[:, :],
                                            start=True, stop=True)
                last.then_inc(o_turned, 1)

            def values(i, par, t):
                at, rows = t % STEPS, t // STEPS
                if at in POOL_SPLITS:
                    pe.wait_ge(pool_low_done, (i + (1 + rows)) * len(POOL_SPLITS) + (POOL_SPLITS.index(at) + 1))
                else:
                    pe.wait_ge(low_done, (i + (1 + rows)) * len(DVE_SPLITS) + (DVE_SPLITS.index(at) + 1))
                if t == 0:
                    pe.wait_ge(o_copied, i + 1)
                high = probs[:, at % BUFS, :, :].bitcast(BF16).rearrange("p k (n two) -> p k n two", two=2)
                for low, part in enumerate((high[:, :, :, 1], probs_low[:, at % BUFS, :, :])):
                    for k in range(2):
                        last = nc.tensor.matmul(
                            o_ps[V_COLS * k:V_COLS * k + V_COLS, :], v_parts[:, par, 2 * at + k, :], part[:, k, :],
                            start=(t == 0 and low == 0), stop=(at == STEPS - 1 and low == 1))
                last.then_inc(pv_done, 1)

            def step(i, head, par, par_before, qc, ahead):
                i = pe.snap(i)
                n = i + (CHUNKS - 1)
                if ahead:
                    pe.wait_ge(head_ready, (n >> 3) + 1)
                pe.wait_ge(rows_in, i + 3)
                pe.wait_ge(v_ready, head + 1)
                q = q_ring[:, ds(qc * CHUNK + par * TOKENS, CHUNK)]

                def scores(t, k):
                    pe.wait_ge(exp_done, i * (2 * STEPS) + (2 * t + k + 1))
                    col = par * TOKENS + STEP * t + P * k
                    nc.tensor.matmul(s2_ps[:, k, :], k_ring[:, col:col + P], q, start=True, stop=True
                                     ).then_inc(s2_done, 1)

                for t in range(STEPS):
                    scores(t, 0)
                    if ahead:
                        diff_unit(n, t)
                    scores(t, 1)
                    if ahead:
                        b_unit(n, t)
                    values(i, par if t >= LAG else par_before, t - LAG)
                    if t == 5:
                        pe.wait_ge(rows_made, n + 1)
                        turn_o(i)
                        turn_max(n)

            pe.wait_ge(head_ready, 1)
            with pe.Fori(0, CHUNKS - 1) as n:
                for u in range(UNITS):
                    diff_unit(n, u)
                    b_unit(n, u)
                    if u == 3:
                        turn_max(n)
            pe.wait_ge(start_values, 4)
            for k in range(2):
                nc.tensor.matmul(o_ps[V_COLS * k:V_COLS * k + V_COLS, :], v_parts[:, 1, 0, :], probs_low[:, 0, 0, :],
                                 start=True, stop=False)
            per_step(pe, step)
            for t in range(-LAG, 0):
                values(pe.snap(RING), 1, t)
            turn_o(RING)

        @block.scalar
        def _(act):
            act.preload_act_table(ACT.Exp)
            act.sem_inc(exp_done, 2)
            act.sem_inc(excess_ready, 2)

            def excess_unit(n, u):
                act.wait_ge(diff_done, n * UNITS + (u + 1))
                act.wait_ge(s1_read, n * UNITS + (u + 1))
                nc.scalar.activation(excess[:, u % 2, :], diff_ps[:, u % 2, :], ACT.Relu).then_inc(excess_ready, 1)

            def copy_o(i):
                act.wait_ge(pv_done, i * STEPS + 4)
                act.wait_ge(o_turned, i + 1)
                nc.scalar.activation(o_here[:, :], o_ps[:, :], ACT.Copy).then_inc(o_copied, 1)

            def step(i, head, par, par_before, qc, ahead):
                i = act.snap(i)
                for t in range(STEPS):
                    act.wait_ge(pv_done, i * STEPS + (t + 1))
                    for k in range(2):
                        act.wait_ge(s2_done, i * (2 * STEPS) + (2 * t + k + 1))
                        nc.scalar.activation(probs[:, t % BUFS, k, :], s2_ps[:, k, :], ACT.Exp).then_inc(exp_done, 1)
                        if k == 0 and t == LAG:
                            copy_o(i)
                        if k == 0 and ahead:
                            excess_unit(i + (CHUNKS - 1), t)

            act.wait_ge(start_values, 4)
            with act.Fori(0, CHUNKS - 1) as n:
                for u in range(UNITS):
                    excess_unit(n, u)
            per_step(act, step)
            copy_o(RING)

        @block.vector
        def _(dve):
            dve.sem_inc(o_scaled, 1)
            nc.vector.memset(unit_max[:, :, :], 0.0).then_inc(start_values, 1)
            nc.vector.memset(probs[:, :, :, :], 1.0).then_inc(start_values, 1)
            nc.vector.memset(probs_low[:, :, :, :], 0.0).then_inc(start_values, 1)
            dve.wait_ge(start_values, 3)
            dve.sem_inc(start_values, 1)
            dve.sem_inc(low_done, len(DVE_SPLITS))
            dve.sem_inc(s1_read, 2)
            dve.sem_inc(rows_made, 1)
            dve.sem_inc(rows_in, 1)
            dve.sem_inc(o_stored, 1)

            def finish_max(n):
                dve.wait_ge(maxT_done, n + 1)
                dve.wait_ge(rows_in, n + 1)
                nc.vector.tensor_scalar(max_parts[:, 0, :], maxT_ps, -1.0, None, ALU.mult).then_inc(max_split, 1)
                dve.wait_ge(max_split, n + 1)
                nc.vector.scalar_tensor_tensor(max_parts[:, 1, :], maxT_ps, -1.0, max_parts[:, 0, :],
                                               ALU.mult, ALU.subtract).then_inc(rows_made, 1)

            def finish_o(i):
                dve.wait_ge(o_turned, i + 2)
                nc.vector.reciprocal(o_scale[:, :], out_ps[:, :, DH]).then_inc(o_scaled, 1)
                dve.wait_ge(o_scaled, i + 2)
                nc.vector.tensor_tensor(ctx_slots[:, ds(i, 1), :, :].rearrange("p a t c -> p (a t) c"), out_ps[:, :, 0:DH],
                                        o_scale[:, :].unsqueeze(2).to_broadcast([P, TPC, DH]), ALU.mult
                                        ).then_inc(o_stored, 1)

            def reduce_tiles(n, units):
                dve.wait_ge(s1_read, units)
                nc.vector.tensor_reduce(tile_max[:, :], unit_max[:, :, :], AX.X, ALU.max).then_inc(tile_max_done, 1)
                dve.wait_ge(tile_max_done, n + 1)

            def unit(n, u):
                dve.wait_ge(b_done, n * UNITS + (u + 1))
                dve.wait_ge(excess_ready, n * UNITS + (u + 3))
                dve.sem_inc(dve_passed, 1)
                nc.vector.tensor_tensor_reduce(excess[:, u % 2, :], b_ps[:, u % 2, :], excess[:, u % 2, :], 1.0, LEAST,
                                               ALU.add, ALU.max, unit_max[:, u // KCH, u % KCH:u % KCH + 1]
                                               ).then_inc(s1_read, 1)

            def low(i, t):
                dve.wait_ge(exp_done, i * (2 * STEPS) + (2 * t + 4))
                high = probs[:, t % BUFS, :, :].bitcast(BF16).rearrange("p k (n two) -> p k n two", two=2)
                nc.vector.tensor_tensor(probs_low[:, t % BUFS, :, :], probs[:, t % BUFS, :, :], high[:, :, :, 1],
                                        ALU.subtract).then_inc(low_done, 1)

            def step(i, head, par, par_before, qc, ahead):
                i = dve.snap(i)
                n = i + (CHUNKS - 1)
                reduce_tiles(n, n * UNITS + 2 if ahead else RING * UNITS + 2)
                for t in range(STEPS):
                    if t - 1 in DVE_SPLITS:
                        low(i, t - 1)
                    if ahead:
                        unit(n, t)
                    if t == 7:
                        finish_max(n)
                        finish_o(i)

            with dve.Fori(0, CHUNKS - 1) as n:
                reduce_tiles(n, n * UNITS + 2)
                for u in range(UNITS):
                    unit(n, u)
                    if u == 4:
                        finish_max(n)
            per_step(dve, step)
            finish_o(RING)


def row_statistics(nc, dve, ch, stats, mean_var, std, rstd, var_ready, std_ready, n):
    for t in range(TILES):
        ch.inc(nc.vector.bn_aggr(mean_var[:, t, :], stats[:, 6 * t:6 * t + 6]))
    ch.wait()
    nc.vector.tensor_scalar(std[:, :], mean_var[:, :, 1], EPS, None, ALU.add).then_inc(var_ready, 1)
    dve.wait_ge(std_ready, n + 1)
    ch.inc(nc.vector.reciprocal(rstd[:, :], std[:, :]))
    ch.wait()


def output_projection(nc, dram, keep):
    with ExitStack() as ctx:
        def sb(name, shape, dt=F32):
            return ctx.enter_context(nc.sbuf_tensor(name, shape, dt))

        def sem(name):
            return ctx.enter_context(nc.semaphore(name))

        x1, x2, ident, ctx_slots = keep["x_all"], keep["v_all"], keep["ident"], keep["ctx_slots"]
        stats = keep["stats"]
        w_o = sb("w_o", [P, HALVES, D])
        heads_here = sb("heads_here", [P, 2, TPC, D])
        headsT = sb("headsT", [P, 2, HALVES, CHUNK])
        y_here = sb("y2_here", [P, TPC, D])
        stats_here = sb("stats2_here", [P, TPC * 6])
        banks = ctx.enter_context(nc.psum_tensor("banks_o", [P, 8, CHUNK], F32))
        tr_ps = banks[:, 0:2, :]
        att_ps = banks[:, 2:4, :].rearrange("p b (t d) -> p (b t) d", t=2)

        wo_in, heads_ready, turned, headsT_ready, att_done, x2_ready = (
            sem("wo_in"), sem("heads_ready"), sem("turned"), sem("headsT_ready"), sem("att_done"), sem("x2_ready"))
        dve_chain, x1_in = sem("dve_chain_o"), sem("x1_in")
        block = ctx.enter_context(nc.Block())

        @block.sync
        def _(sp):
            sp.dma_start(w_o[:, :, :], dram["Wo"].rearrange("(j p) e -> p j e", p=P)).then_inc(wo_in, 16)
            sp.dma_start(x1[:, :, :], dram["x1"]).then_inc(x1_in, 16)

        @block.scalar
        def _(act):
            act.preload_act_table(ACT.Copy)
            slots = ctx_slots[:, 1:RING + 1, :, :].rearrange("p (h q) t c -> p h q t c", q=CHUNKS)
            with act.Fori(0, CHUNKS // 2) as it:
                for b in range(2):
                    c = it * 2 + b
                    for t in range(TPC):
                        last = nc.scalar.activation(
                            heads_here[:, b, t, :].rearrange("p (h c) -> p h c", c=DH),
                            slots[:, :, ds(c, 1), t, :].rearrange("p h q c -> p (h q) c"), ACT.Copy)
                    last.then_inc(heads_ready, 1)
                    act.wait_ge(turned, c + 1)
                    for j in range(HALVES):
                        nc.scalar.activation(headsT[:, b, j, :], tr_ps[:, j, :], ACT.Copy).then_inc(headsT_ready, 1)

        @block.tensor
        def _(pe):
            pe.wait_ge(wo_in, 16)
            with pe.Fori(0, CHUNKS // 2) as it:
                for b in range(2):
                    c = it * 2 + b
                    pe.wait_ge(heads_ready, c + 1)
                    for j in range(HALVES):
                        for t in range(TPC):
                            last = nc.tensor.transpose(tr_ps[:, j, P * t:P * t + P],
                                                       heads_here[:, b, t, P * j:P * j + P], ident[:, :])
                    last.then_inc(turned, 1)
                    pe.wait_ge(headsT_ready, c * 2 + 2)
                    pe.wait_ge(x2_ready, c + 1)
                    for t in range(TPC):
                        for j in range(HALVES):
                            last = nc.tensor.matmul(att_ps[:, t, :], headsT[:, b, j, P * t:P * t + P], w_o[:, j, :],
                                                    start=(j == 0), stop=(j == HALVES - 1))
                    last.then_inc(att_done, 1)

        @block.vector
        def _(dve):
            ch = Chain(dve, dve_chain)
            dve.wait_ge(x1_in, 16)
            dve.sem_inc(x2_ready, 1)
            with dve.Fori(0, CHUNKS) as c:
                dve.wait_ge(att_done, c + 1)
                ch.enter(c, TPC + 2)
                nc.vector.tensor_tensor(y_here[:, :, :], att_ps, x1[:, ds(c * TPC, TPC), :], ALU.add).then_inc(x2_ready, 1)
                dve.wait_ge(x2_ready, c + 2)
                for t in range(TPC):
                    ch.inc(nc.vector.bn_stats(stats_here[:, 6 * t:6 * t + 6], y_here[:, t, :]))
                ch.wait()
                ch.inc(nc.vector.tensor_scalar(stats[:, ds(c * TPC * 6, TPC * 6)], stats_here[:, :], 1.0, None, ALU.mult))
                ch.inc(nc.vector.tensor_scalar(x2[:, ds(c * TPC, TPC), :], y_here[:, :, :], 1.0, None, ALU.mult))
                ch.wait()
                ch.leave(CHUNKS)


def routing(nc, dram, keep):
    with ExitStack() as ctx:
        def sb(name, shape, dt=F32):
            return ctx.enter_context(nc.sbuf_tensor(name, shape, dt))

        def sem(name):
            return ctx.enter_context(nc.semaphore(name))

        x1, x2, ident, stats = keep["x_all"], keep["v_all"], keep["ident"], keep["stats"]
        chosen_at, chosen_share = keep["chosen_at"], keep["chosen_share"]
        mean_var, std, rstd = keep["mean_var"], keep["std"], keep["rstd"]
        w_g = sb("w_g", [P, HALVES, EXPERTS])
        b_2 = sb("b_2", [EXPERTS, D])
        gain2 = sb("gain2", [P, HALVES])
        bias2 = sb("bias2", [P, HALVES])
        hn = sb("hn2", [P, 2, TPC, D])
        mT = sb("mT", [P, 2, HALVES, CHUNK])
        count_i = sb("count_i", [P, EXPERTS], I32)
        count = sb("count", [P, EXPERTS])
        top_logit = sb("top_logit", [P, TPC])
        shifted = sb("shifted", [P, TPC, EXPERTS])
        expd = sb("expd", [P, TPC, EXPERTS])
        total = sb("total", [P, TPC])
        prob = sb("prob", [P, TPC, EXPERTS])
        top = sb("top", [P, TPC, EXPERTS])
        top_at = sb("top_at", [P, TPC, EXPERTS], U32)
        at = sb("at", [P, TPC, 2])
        pair = sb("pair", [P, TPC])
        share = sb("share", [P, TPC, 2])
        chosen = sb("chosen", [P, 2, TPC, EXPERTS])
        weights_here = sb("weights_here", [P, TPC, EXPERTS])
        weightsT = sb("weightsT", [EXPERTS, CHUNK])
        y_here = sb("y3_here", [P, TPC, D])
        zeros = sb("zero_rows", [P, TPC, D])
        banks = ctx.enter_context(nc.psum_tensor("banks_r", [P, 8, CHUNK], F32))
        tr_ps = banks[:, 0:2, :]
        logit_ps = banks[:, 2, 0:TPC * EXPERTS].rearrange("p (t e) -> p t e", t=TPC)
        wT_ps = banks[0:EXPERTS, 3, :]
        b2_ps = banks[:, 4:6, :].rearrange("p b (t d) -> p (b t) d", t=2)

        router_in, affine_in, consts_ready = sem("router_in"), sem("affine2_in"), sem("consts2_ready")
        var_ready, std_ready = sem("var2_ready"), sem("std2_ready")
        hn_ready, turned, mT_ready = sem("hn2_ready"), sem("turned2"), sem("mT_ready")
        sum_ready, hn_kept, pool_passed = sem("sum_ready"), sem("hn_kept"), sem("pool_passed_r")
        zeros_set, zeros_out = sem("zeros_set"), sem("zeros_out")
        logits_done, shifted_ready, exp_ready, weights_ready = (
            sem("logits_done"), sem("shifted_ready"), sem("exp_ready"), sem("weights_ready"))
        wT_done, wT_ready, b2_done, b2_added = sem("wT_done"), sem("wT_ready"), sem("b2_done"), sem("b2_added")
        dve_chain, passed = sem("dve_chain_r"), sem("passed")
        block = ctx.enter_context(nc.Block())

        @block.sync
        def _(sp):
            sp.dma_start(w_g[:, :, :], dram["Wg"].rearrange("(j p) e -> p j e", p=P)).then_inc(router_in, 16)
            sp.dma_start(b_2[:, :], dram["b2"]).then_inc(router_in, 16)
            sp.wait_ge(zeros_set, 1)
            with sp.Fori(0, SLOT_TILES + 1) as j:
                sp.dma_start(dram["slots"][ds(j * CHUNK, CHUNK), :].rearrange("(t p) d -> p t d", p=P), zeros[:, :, :]
                             ).then_inc(zeros_out, 16)
            sp.wait_ge(zeros_out, 16 * (SLOT_TILES + 1))

        @block.gpsimd
        def _(pool):
            pool.dma_start(gain2[:, :], dram["ln2_g"].rearrange("(j p) -> p j", p=P),
                           allow_slow_non_contiguous=True).then_inc(affine_in, 16)
            pool.dma_start(bias2[:, :], dram["ln2_b"].rearrange("(j p) -> p j", p=P),
                           allow_slow_non_contiguous=True).then_inc(affine_in, 16)
            nc.gpsimd.iota(count_i[:, :], [[1, EXPERTS]], base=0, channel_multiplier=0).then_inc(consts_ready, 1)
            pool.wait_ge(consts_ready, 1)
            nc.gpsimd.tensor_copy(count[:, :], count_i[:, :]).then_inc(consts_ready, 1)
            nc.gpsimd.memset(zeros[:, :, :], 0.0).then_inc(zeros_set, 1)
            with pool.Fori(0, CHUNKS // 2) as it:
                for b in range(2):
                    c = it * 2 + b
                    pool.wait_ge(sum_ready, c + 1)
                    pool.wait_ge(hn_ready, c + 1)
                    pool.sem_inc(pool_passed, 1)
                    nc.gpsimd.tensor_copy(x2[:, ds(c * TPC, TPC), :], hn[:, b, :, :]).then_inc(hn_kept, 1)

        @block.scalar
        def _(act):
            act.preload_act_table(ACT.Sqrt)
            act.wait_ge(var_ready, 1)
            nc.scalar.activation(std[:, :], std[:, :], ACT.Sqrt).then_inc(std_ready, 1)
            act.preload_act_table(ACT.Exp)
            act.wait_ge(affine_in, 2 * 16)
            with act.Fori(0, CHUNKS // 2) as it:
                for b in range(2):
                    c = it * 2 + b
                    act.wait_ge(turned, c + 1)
                    for j in range(HALVES):
                        nc.scalar.activation(mT[:, b, j, :], tr_ps[:, j, :], ACT.Identity,
                                             bias=bias2[:, j:j + 1], scale=gain2[:, j:j + 1]).then_inc(mT_ready, 1)
                    act.wait_ge(shifted_ready, c + 1)
                    nc.scalar.activation(expd[:, :, :], shifted[:, :, :], ACT.Exp).then_inc(exp_ready, 1)
                    act.wait_ge(wT_done, c + 1)
                    nc.scalar.activation(weightsT[:, :], wT_ps, ACT.Copy).then_inc(wT_ready, 1)

        @block.tensor
        def _(pe):
            pe.wait_ge(router_in, 32)
            with pe.Fori(0, CHUNKS // 2) as it:
                for b in range(2):
                    c = it * 2 + b
                    pe.wait_ge(hn_ready, c + 1)
                    for j in range(HALVES):
                        for t in range(TPC):
                            last = nc.tensor.transpose(tr_ps[:, j, P * t:P * t + P],
                                                       hn[:, b, t, P * j:P * j + P], ident[:, :])
                    last.then_inc(turned, 1)
                    pe.wait_ge(mT_ready, c * 2 + 2)
                    for t in range(TPC):
                        for j in range(HALVES):
                            last = nc.tensor.matmul(logit_ps[:, t, :], mT[:, b, j, P * t:P * t + P], w_g[:, j, :],
                                                    start=(j == 0), stop=(j == HALVES - 1))
                    last.then_inc(logits_done, 1)
                    pe.wait_ge(weights_ready, c + 1)
                    for t in range(TPC):
                        last = nc.tensor.transpose(wT_ps[:, P * t:P * t + P], weights_here[:, t, :], ident[:, :])
                    last.then_inc(wT_done, 1)
                    pe.wait_ge(wT_ready, c + 1)
                    pe.wait_ge(b2_added, c + 1)
                    for t in range(TPC):
                        last = nc.tensor.matmul(b2_ps[:, t, :], weightsT[:, P * t:P * t + P], b_2[:, :],
                                                start=True, stop=True)
                    last.then_inc(b2_done, 1)

        @block.vector
        def _(dve):
            ch = Chain(dve, dve_chain)
            row_statistics(nc, dve, ch, stats, mean_var, std, rstd, var_ready, std_ready, 0)
            dve.wait_ge(consts_ready, 2)
            dve.sem_inc(b2_added, 1)
            dve.sem_inc(hn_kept, 2)

            def hold():
                ch.wait()
                dve.sem_inc(passed, 1)

            with dve.Fori(0, CHUNKS // 2) as it:
                ch.enter(it, 2 * 18)
                for b in range(2):
                    c = it * 2 + b
                    dve.wait_ge(hn_kept, c + 1)
                    for t in range(TPC):
                        last = nc.vector.tensor_scalar(
                            hn[:, b, t, :], x2[:, ds(c * TPC + t, 1), :].rearrange("p a d -> p (a d)"),
                            mean_var[:, ds(c * TPC + t, 1), 0], rstd[:, ds(c * TPC + t, 1)], ALU.subtract, ALU.mult)
                    last.then_inc(hn_ready, 1)
                    ch.inc(nc.vector.tensor_tensor(y_here[:, :, :], x1[:, ds(c * TPC, TPC), :], x2[:, ds(c * TPC, TPC), :], ALU.add))
                    ch.wait()
                    dve.sem_inc(sum_ready, 1)
                    dve.wait_ge(logits_done, c + 1)
                    ch.inc(nc.vector.tensor_reduce(top_logit[:, :], logit_ps, AX.X, ALU.max))
                    ch.wait()
                    nc.vector.tensor_tensor(shifted[:, :, :], logit_ps,
                                            top_logit[:, :].unsqueeze(2).to_broadcast([P, TPC, EXPERTS]), ALU.subtract
                                            ).then_inc(shifted_ready, 1)
                    dve.wait_ge(exp_ready, c + 1)
                    ch.inc(nc.vector.tensor_reduce(total[:, :], expd[:, :, :], AX.X, ALU.add))
                    ch.wait()
                    ch.inc(nc.vector.reciprocal(total[:, :], total[:, :]))
                    ch.wait()
                    ch.inc(nc.vector.tensor_tensor(prob[:, :, :], expd[:, :, :],
                                                   total[:, :].unsqueeze(2).to_broadcast([P, TPC, EXPERTS]), ALU.mult))
                    hold()
                    for t in range(TPC):
                        ch.inc(nc.vector.max(top[:, t, :], prob[:, t, :]))
                    hold()
                    for t in range(TPC):
                        last = nc.vector.max_index(top_at[:, t, :], top[:, t, :], prob[:, t, :])
                    ch.inc(last)
                    ch.inc(nc.vector.tensor_tensor(pair[:, :], top[:, :, 0], top[:, :, 1], ALU.add))
                    ch.wait()
                    ch.inc(nc.vector.reciprocal(pair[:, :], pair[:, :]))
                    ch.inc(nc.vector.tensor_scalar(at[:, :, :], top_at[:, :, 0:2], 1.0, None, ALU.mult))
                    ch.wait()
                    ch.inc(nc.vector.tensor_tensor(share[:, :, :], top[:, :, 0:2],
                                                   pair[:, :].unsqueeze(2).to_broadcast([P, TPC, 2]), ALU.mult))
                    ch.wait()
                    for n in range(2):
                        for t in range(TPC):
                            last = nc.vector.tensor_scalar(chosen[:, n, t, :], count[:, :], at[:, t, n:n + 1],
                                                           share[:, t, n:n + 1], ALU.is_equal, ALU.mult)
                    ch.inc(last)
                    ch.wait()
                    nc.vector.tensor_tensor(weights_here[:, :, :], chosen[:, 0, :, :], chosen[:, 1, :, :], ALU.add
                                            ).then_inc(weights_ready, 1)
                    ch.inc(nc.vector.tensor_scalar(chosen_at[:, ds(c * TPC, TPC), :], at[:, :, :], 1.0, None, ALU.mult))
                    ch.inc(nc.vector.tensor_scalar(chosen_share[:, ds(c * TPC, TPC), :], share[:, :, :], 1.0, None,
                                                   ALU.mult))
                    dve.wait_ge(b2_done, c + 1)
                    ch.wait()
                    ch.inc(nc.vector.tensor_tensor(x1[:, ds(c * TPC, TPC), :], y_here[:, :, :], b2_ps, ALU.add))
                    ch.wait()
                    dve.sem_inc(b2_added, 1)
                ch.leave(CHUNKS // 2)


def dispatch(nc, dram, keep):
    with ExitStack() as ctx:
        def sb(name, shape, dt=F32):
            return ctx.enter_context(nc.sbuf_tensor(name, shape, dt))

        def sem(name):
            return ctx.enter_context(nc.semaphore(name))

        hn, chosen_at, slot_of, tile_expert = keep["v_all"], keep["chosen_at"], keep["slot_of"], keep["tile_expert"]
        NT = SLOT_TILES + 1
        earlier = sb("earlier", [P, P])
        ones = sb("ones", [P, P])
        count_i = sb("count_i_d", [P, NT], I32)
        count = sb("count_d", [P, NT])
        picks = sb("picks", [P, TOP, TILES, EXPERTS])
        both = sb("both", [P, TILES, EXPERTS])
        totals = sb("totals", [P, TILES, EXPERTS])
        sums = sb("sums", [P, 2, TILES, EXPERTS])
        rank = sb("rank", [P, TILES, EXPERTS])
        starts = sb("starts", [P, EXPERTS])
        table = sb("table", [P, EXPERTS, EXPERTS])
        tiles_of = sb("tiles_of", [P, EXPERTS])
        tile_end = sb("tile_end", [P, EXPERTS])
        base = sb("base", [P, EXPERTS])
        slot_f = sb("slot_f", [P, TOP, TILES])
        over = sb("over", [P, NT, EXPERTS])
        expert_f = sb("expert_f", [P, NT])
        rows = sb("rows", [P, 2, TPC, D])
        slot_here = sb("slot_here", [P, 2, TPC * TOP], U32)
        counts_ps = ctx.enter_context(nc.psum_tensor("counts_ps", [P, 2, CHUNK], F32))
        within_ps = counts_ps[:, 0, 0:TILES * EXPERTS].rearrange("p (t e) -> p t e", e=EXPERTS)
        total_ps = counts_ps[:, 1, 0:TILES * EXPERTS].rearrange("p (t e) -> p t e", e=EXPERTS)

        consts_ready, both_ready, counted, slots_ready = (
            sem("consts_ready_d"), sem("both_ready"), sem("counted"), sem("slots_ready"))
        rows_staged, slot_copied, rows_free, pool_passed = (
            sem("rows_staged"), sem("slot_copied"), sem("rows_free_d"), sem("pool_passed_d"))
        scattered = [sem("scattered0"), sem("scattered1")]
        dve_chain = sem("dve_chain_d")
        block = ctx.enter_context(nc.Block())

        @block.gpsimd
        def _(pool):
            nc.gpsimd.iota(count_i[:, :], [[1, NT]], base=0, channel_multiplier=0).then_inc(consts_ready, 1)
            nc.gpsimd.memset(ones[:, :], 1.0).then_inc(consts_ready, 1)
            pool.wait_ge(consts_ready, 2)
            nc.gpsimd.tensor_copy(count[:, :], count_i[:, :]).then_inc(consts_ready, 1)
            nc.gpsimd.affine_select(out=earlier[:, :], in_=ones[:, :], compare_op=ALU.is_gt, fill=0.0,
                                    base=0, pattern=[[1, P]], channel_multiplier=-1).then_inc(consts_ready, 1)
            pool.wait_ge(slots_ready, 1)
            with pool.Fori(0, CHUNKS // 2) as it:
                for b in range(2):
                    c = it * 2 + b
                    nc.gpsimd.tensor_copy(slot_here[:, b, :].rearrange("p (t n) -> p t n", n=TOP),
                                          slot_of[:, ds(c * TPC, TPC), :]).then_inc(slot_copied, 1)
                    pool.wait_ge(slot_copied, c + 1)
                    pool.wait_ge(rows_staged, c + 1)
                    pool.sem_inc(pool_passed, 1)
                    for k in range(TPC * TOP):
                        nc.gpsimd.indirect_dma_start(
                            dram["slots"], bass.IndirectOffsetOnAxis(slot_here[:, b, k:k + 1], 0),
                            rows[:, b, k // TOP, :], None).then_inc(scattered[b], 16)
                for b in range(2):
                    pool.wait_ge(scattered[b], it * (16 * TPC * TOP) + 16 * TPC * TOP)
                    pool.sem_inc(rows_free, 1)

        @block.tensor
        def _(pe):
            pe.wait_ge(consts_ready, 4)
            pe.wait_ge(both_ready, 1)
            flat = both[:, :, :].rearrange("p t e -> p (t e)")
            for n, of in enumerate((earlier, ones)):
                nc.tensor.matmul(counts_ps[:, n, 0:TILES * EXPERTS], of[:, :], flat, start=True, stop=True
                                 ).then_inc(counted, 1)

        @block.scalar
        def _(act):
            act.sem_inc(rows_free, 2)
            with act.Fori(0, CHUNKS // 2) as it:
                for b in range(2):
                    c = it * 2 + b
                    act.wait_ge(rows_free, c + 1)
                    nc.scalar.activation(rows[:, b, :, :], hn[:, ds(c * TPC, TPC), :], ACT.Copy).then_inc(rows_staged, 1)

        @block.vector
        def _(dve):
            ch = Chain(dve, dve_chain)

            def do(ins):
                ch.inc(ins)
                ch.wait()

            dve.wait_ge(consts_ready, 4)
            experts_row = count[:, 0:EXPERTS].unsqueeze(1)
            for n in range(TOP):
                do(nc.vector.tensor_tensor(picks[:, n, :, :], experts_row.to_broadcast([P, TILES, EXPERTS]),
                                           chosen_at[:, :, n].unsqueeze(2).to_broadcast([P, TILES, EXPERTS]),
                                           ALU.is_equal))
            nc.vector.tensor_tensor(both[:, :, :], picks[:, 0, :, :], picks[:, 1, :, :], ALU.add).then_inc(both_ready, 1)
            dve.wait_ge(counted, 2)
            ch.inc(nc.vector.tensor_scalar(totals[:, :, :], total_ps, 1.0, None, ALU.mult))
            do(nc.vector.tensor_scalar(sums[:, 0, :, :], total_ps, 1.0, None, ALU.mult))
            now, far = 0, 1
            while far < TILES:
                ch.inc(nc.vector.tensor_scalar(sums[:, 1 - now, 0:far, :], sums[:, now, 0:far, :], 1.0, None, ALU.mult))
                do(nc.vector.tensor_tensor(sums[:, 1 - now, far:TILES, :], sums[:, now, far:TILES, :],
                                           sums[:, now, 0:TILES - far, :], ALU.add))
                now, far = 1 - now, far * 2
            do(nc.vector.tensor_tensor(rank[:, :, :], sums[:, now, :, :], totals[:, :, :], ALU.subtract))
            do(nc.vector.tensor_tensor(rank[:, :, :], rank[:, :, :], within_ps, ALU.add))
            do(nc.vector.tensor_scalar(starts[:, :], count[:, 0:EXPERTS], float(CHUNK), None, ALU.mult))
            square = [P, EXPERTS, EXPERTS]
            do(nc.vector.tensor_tensor(table[:, :, :], sums[:, now, TILES - 1, :].unsqueeze(2).to_broadcast(square),
                                       starts[:, :].unsqueeze(1).to_broadcast(square), ALU.is_gt))
            do(nc.vector.tensor_reduce(tiles_of[:, :], table[:, :, :], AX.X, ALU.add))
            do(nc.vector.tensor_tensor(table[:, :, :], experts_row.to_broadcast(square),
                                       count[:, 0:EXPERTS].unsqueeze(2).to_broadcast(square), ALU.is_le))
            do(nc.vector.tensor_tensor(table[:, :, :], table[:, :, :], tiles_of[:, :].unsqueeze(1).to_broadcast(square),
                                       ALU.mult))
            do(nc.vector.tensor_reduce(tile_end[:, :], table[:, :, :], AX.X, ALU.add))
            do(nc.vector.tensor_tensor(base[:, :], tile_end[:, :], tiles_of[:, :], ALU.subtract))
            do(nc.vector.tensor_scalar(base[:, :], base[:, :], float(CHUNK), None, ALU.mult))
            do(nc.vector.tensor_tensor(rank[:, :, :], rank[:, :, :],
                                       base[:, :].unsqueeze(1).to_broadcast([P, TILES, EXPERTS]), ALU.add))
            for n in range(TOP):
                do(nc.vector.tensor_tensor(picks[:, n, :, :], picks[:, n, :, :], rank[:, :, :], ALU.mult))
                do(nc.vector.tensor_reduce(slot_f[:, n, :], picks[:, n, :, :], AX.X, ALU.add))
                do(nc.vector.tensor_scalar(slot_of[:, :, n], slot_f[:, n, :], 1.0, None, ALU.mult))
            do(nc.vector.tensor_tensor(over[:, :, :], tile_end[:, :].unsqueeze(1).to_broadcast([P, NT, EXPERTS]),
                                       count[:, :].unsqueeze(2).to_broadcast([P, NT, EXPERTS]), ALU.is_le))
            do(nc.vector.tensor_reduce(expert_f[:, :], over[:, :, :], AX.X, ALU.add))
            do(nc.vector.tensor_scalar(tile_expert[:, :], expert_f[:, :], float(EXPERTS - 1), None, ALU.min))
            dve.sem_inc(slots_ready, 1)


def experts(nc, dram, keep):
    with ExitStack() as ctx:
        def sb(name, shape, dt=F32):
            return ctx.enter_context(nc.sbuf_tensor(name, shape, dt))

        def sem(name):
            return ctx.enter_context(nc.semaphore(name))

        ident, tile_expert = keep["ident"], keep["tile_expert"]
        gain2 = sb("gain2_e", [P, HALVES])
        bias2 = sb("bias2_e", [P, HALVES])
        rows = sb("rows_e", [P, 2, TPC, D])
        mT = sb("mT_e", [P, HALVES, CHUNK])
        m_high = sb("m_high", [P, 2, HALVES, CHUNK], F32R)
        m_low = sb("m_low", [P, 2, HALVES, CHUNK], F32R)
        w1_in = sb("w1_in", [P, HALVES, FF])
        w2_in = sb("w2_in", [P, FT, D])
        w1_high = sb("w1_high", [P, 2, HALVES, FT, P], F32R)
        w1_low = sb("w1_low", [P, 2, HALVES, FT, P], F32R)
        w2_high = sb("w2_high", [P, 2, FT, D], F32R)
        w2_low = sb("w2_low", [P, 2, FT, D], F32R)
        b1_here = sb("b1_here", [P, 2, FT])
        zero = sb("zero", [P, 1])
        hidden = sb("hidden", [P, 2, CHUNK])
        hidden_high = sb("hidden_high", [P, 4, CHUNK], F32R)
        hidden_low = sb("hidden_low", [P, 4, CHUNK], F32R)
        y_out = sb("y_out", [P, TPC, D])
        h_ps = ctx.enter_context(nc.psum_tensor("h_ps", [P, 4, CHUNK], F32))
        y_ps = ctx.enter_context(nc.psum_tensor("y_ps", [P, 2, CHUNK], F32))
        tr_ps = ctx.enter_context(nc.psum_tensor("tr_ps", [P, 2, CHUNK], F32))

        affine_in, zero_set = sem("affine_in_e"), sem("zero_set")
        rows_full, b1_full = [sem("rows_full0"), sem("rows_full1")], [sem("b1_full0"), sem("b1_full1")]
        rows_used, turned, mT_ready, m_high_ready, m_ready = (
            sem("rows_used"), sem("turned_e"), sem("mT_ready_e"), sem("m_high_ready_e"), sem("m_ready"))
        w1_full, w2_full, w1_split, w2_split, w_ready = (
            sem("w1_full"), sem("w2_full"), sem("w1_split"), sem("w2_split"), sem("w_ready"))
        sync_passed, pool_passed = sem("sync_passed_e"), sem("pool_passed_e")
        h_done, h_read, high_done, low_done, hidden_used = (
            sem("h_done"), sem("h_read"), sem("high_done"), sem("low_done_e"), sem("hidden_used"))
        y_done, y_read, stored = sem("y_done"), sem("y_read"), sem("stored_e")
        W_OPS = 6
        block = ctx.enter_context(nc.Block())

        def nth(j, b):
            return (j + (2 - b)) * 8

        def per_tile(body):
            def run(eng):
                body(0, 0, True)
                with eng.Fori(0, (SLOT_TILES - 1) // 2) as it:
                    for n in range(2):
                        body(eng.snap(it * 2 + (n + 1)), (n + 1) % 2, False)
            return run
        assert SLOT_TILES % 2 == 1

        @block.sync
        def _(sp):
            def load_rows(j, b):
                sp.wait_ge(rows_used, j + 1)
                sp.sem_inc(sync_passed, 1)
                sp.dma_start(rows[:, b, :, :], dram["slots"][ds(j * CHUNK, CHUNK), :].rearrange("(t p) d -> p t d", p=P)
                             ).then_inc(rows_full[b], 16)

            def load_b1(j, b):
                e = sp.value_load(tile_expert[0:1, ds(j, 1)], min_val=0, max_val=EXPERTS - 1)
                sp.dma_start(b1_here[:, b, :], dram["b1"][ds(e, 1), :].rearrange("a (p t) -> (a p) t", t=FT)
                             ).then_inc(b1_full[b], 16)

            def load(j, b, first):
                load_rows(j, b)
                e = sp.value_load(tile_expert[0:1, ds(j, 1)], min_val=0, max_val=EXPERTS - 1)
                if not first:
                    sp.wait_ge(w1_split, j)
                    sp.sem_inc(sync_passed, 1)
                sp.dma_start(w1_in[:, :, :], dram["W1"][ds(e, 1), :, :].rearrange("a (j p) f -> p (a j) f", p=P)
                             ).then_inc(w1_full, 16)
                if not first:
                    load_b1(j - 1, 1 - b)
                    sp.wait_ge(w2_split, j)
                    sp.sem_inc(sync_passed, 1)
                e = sp.value_load(tile_expert[0:1, ds(j, 1)], min_val=0, max_val=EXPERTS - 1)
                sp.dma_start(w2_in[:, :, :], dram["W2"][ds(e, 1), :, :].rearrange("a (p t) d -> (a p) t d", t=FT)
                             ).then_inc(w2_full, 16)

            per_tile(load)(sp)
            sp.wait_ge(w1_split, SLOT_TILES)
            load_b1(SLOT_TILES - 1, (SLOT_TILES - 1) % 2)
            load_rows(SLOT_TILES, SLOT_TILES % 2)

        @block.gpsimd
        def _(pool):
            pool.dma_start(gain2[:, :], dram["ln2_g"].rearrange("(j p) -> p j", p=P),
                           allow_slow_non_contiguous=True).then_inc(affine_in, 16)
            pool.dma_start(bias2[:, :], dram["ln2_b"].rearrange("(j p) -> p j", p=P),
                           allow_slow_non_contiguous=True).then_inc(affine_in, 16)
            nc.gpsimd.memset(zero[:, :], 0.0).then_inc(zero_set, 1)
            pool.wait_ge(zero_set, 1)

            def split(j, b, first):
                pool.wait_ge(y_done, j + 1)
                pool.wait_ge(w1_full, j * 16 + 16)
                w1 = w1_in[:, :, :].rearrange("p j (i t) -> p j t i", t=FT)
                for half in range(HALVES):
                    nc.gpsimd.tensor_tensor(w1_high[:, b, half, :, :], w1[:, half, :, :],
                                            zero[:, :].unsqueeze(2).to_broadcast([P, FT, P]), ALU.add
                                            ).then_inc(w_ready, 1)
                pool.wait_ge(w_ready, j * W_OPS + 2)
                for half in range(HALVES):
                    nc.gpsimd.tensor_tensor(w1_low[:, b, half, :, :], w1[:, half, :, :],
                                            w1_high[:, b, half, :, :].bitcast(F32), ALU.subtract).then_inc(w_ready, 1)
                pool.wait_ge(w_ready, j * W_OPS + 4)
                pool.sem_inc(w1_split, 1)
                pool.wait_ge(w2_full, j * 16 + 16)
                nc.gpsimd.tensor_tensor(w2_high[:, b, :, :], w2_in[:, :, :],
                                        zero[:, :].unsqueeze(2).to_broadcast([P, FT, D]), ALU.add).then_inc(w_ready, 1)
                pool.wait_ge(w_ready, j * W_OPS + 5)
                nc.gpsimd.tensor_tensor(w2_low[:, b, :, :], w2_in[:, :, :], w2_high[:, b, :, :].bitcast(F32),
                                        ALU.subtract).then_inc(w_ready, 1)
                pool.wait_ge(w_ready, j * W_OPS + 6)
                pool.sem_inc(w2_split, 1)

            per_tile(split)(pool)

        @block.tensor
        def _(pe):
            pe.sem_inc(y_done, 2)
            pe.sem_inc(hidden_used, 4)
            pe.sem_inc(rows_used, 2)

            def turn(j, b):
                pe.wait_ge(rows_full[b], nth(j, b))
                for half in range(HALVES):
                    for t in range(TPC):
                        last = nc.tensor.transpose(tr_ps[:, half, P * t:P * t + P], rows[:, b, t, P * half:P * half + P],
                                                   ident[:, :])
                last.then_inc(turned, 1)

            def tile(j, b, first):
                pe.wait_ge(w_ready, j * W_OPS + 6)
                pe.wait_ge(m_ready, j + 1)
                pe.sem_inc(rows_used, 1)

                def up(f):
                    pe.wait_ge(h_read, j * FT + (f + 1))
                    for half in range(HALVES):
                        for n, (w, m) in enumerate(((w1_high, m_high), (w1_high, m_low), (w1_low, m_high))):
                            last = nc.tensor.matmul(h_ps[:, f % 4, :], w[:, b, half, f, :], m[:, b, half, :],
                                                    start=(half == 0 and n == 0), stop=(half == HALVES - 1 and n == 2))
                    last.then_inc(h_done, 1)

                def down(f):
                    pe.wait_ge(low_done, j * FT + (f + 3))
                    if f == 0:
                        pe.wait_ge(y_read, j * 2 + 2)
                    for t in range(TPC):
                        cols = slice(P * t, P * t + P)
                        for n, (h, w) in enumerate(((hidden_high, w2_high), (hidden_high, w2_low), (hidden_low, w2_high))):
                            last = nc.tensor.matmul(y_ps[:, t // 2, D * (t % 2):D * (t % 2) + D], h[:, f % 4, cols],
                                                    w[:, b, f, :], start=(f == 0 and n == 0 and t % 2 == 0),
                                                    stop=(f == FT - 1 and n == 2), skip_group_check=True)
                    last.then_inc(hidden_used, 1)

                for f in range(FT):
                    up(f)
                    if f >= 2:
                        down(f - 2)
                    if f == 4:
                        turn(j + 1, 1 - b)
                down(FT - 2)
                down(FT - 1)
                pe.wait_ge(hidden_used, j * FT + (FT + 4))
                pe.sem_inc(y_done, 1)

            turn(0, 0)
            per_tile(tile)(pe)

        @block.scalar
        def _(act):
            act.preload_act_table(ACT.Gelu_apprx_tanh)
            act.sem_inc(h_read, 4)
            act.sem_inc(low_done, 2)
            act.sem_inc(y_read, 2)
            act.wait_ge(affine_in, 2 * 16)

            def split_rows(j, b):
                act.wait_ge(turned, j + 1)
                for half in range(HALVES):
                    nc.scalar.activation(mT[:, half, :], tr_ps[:, half, :], ACT.Identity, bias=bias2[:, half:half + 1],
                                         scale=gain2[:, half:half + 1]).then_inc(mT_ready, 1)
                act.wait_ge(mT_ready, j * 2 + 2)
                nc.scalar.activation(m_high[:, b, :, :], mT[:, :, :], ACT.Copy).then_inc(m_high_ready, 1)

            def store(j):
                act.wait_ge(y_done, j + 3)
                for n in range(2):
                    nc.scalar.activation(y_out[:, 2 * n:2 * n + 2, :], y_ps[:, n, :].rearrange("p (t d) -> p t d", t=2),
                                         ACT.Copy).then_inc(y_read, 1)
                act.wait_ge(y_read, j * 2 + 4)
                act.dma_start(dram["y_slots"][ds(j * CHUNK, CHUNK), :].rearrange("(t p) d -> p t d", p=P), y_out[:, :, :]
                              ).then_inc(stored, 16)

            def tile(j, b, first):
                act.wait_ge(b1_full[b], nth(j, b))
                for f in range(FT):
                    act.wait_ge(h_done, j * FT + (f + 1))
                    act.wait_ge(low_done, j * FT + (f + 1))
                    nc.scalar.activation(hidden[:, f % 2, :], h_ps[:, f % 4, :], ACT.Gelu_apprx_tanh,
                                         bias=b1_here[:, b, f:f + 1]).then_inc(h_read, 1)
                    act.wait_ge(h_read, j * FT + (f + 5))
                    act.wait_ge(hidden_used, j * FT + (f + 1))
                    nc.scalar.activation(hidden_high[:, f % 4, :], hidden[:, f % 2, :], ACT.Copy).then_inc(high_done, 1)
                    if f == 0 and not first:
                        store(j - 1)
                    if f == 5:
                        act.wait_ge(m_ready, j + 1)
                        split_rows(j + 1, 1 - b)
                    if f == FT - 2 and not first:
                        act.wait_ge(stored, j * 16)

            split_rows(0, 0)
            per_tile(tile)(act)
            store(SLOT_TILES - 1)
            act.wait_ge(stored, SLOT_TILES * 16)

        @block.vector
        def _(dve):
            def low_rows(j, b):
                dve.wait_ge(m_high_ready, j + 1)
                nc.vector.tensor_tensor(m_low[:, b, :, :], mT[:, :, :], m_high[:, b, :, :].bitcast(F32), ALU.subtract
                                        ).then_inc(m_ready, 1)

            def tile(j, b, first):
                for f in range(FT):
                    dve.wait_ge(high_done, j * FT + (f + 1))
                    nc.vector.tensor_tensor(hidden_low[:, f % 4, :], hidden[:, f % 2, :],
                                            hidden_high[:, f % 4, :].bitcast(F32), ALU.subtract).then_inc(low_done, 1)
                    if f == 6:
                        low_rows(j + 1, 1 - b)

            low_rows(0, 0)
            per_tile(tile)(dve)


def last_norm(nc, dram, keep):
    with ExitStack() as ctx:
        def sem(name):
            return ctx.enter_context(nc.semaphore(name))

        acc, stats = keep["x_all"], keep["stats"]
        mean_var, std, rstd = keep["mean_var"], keep["std"], keep["rstd"]
        rows_out = ctx.enter_context(nc.sbuf_tensor("rows_out", [P, 2, TPC, D], F32))
        var_ready, std_ready, rows_ready, rows_free = sem("var3_ready"), sem("std3_ready"), sem("rows_ready"), sem("rows_free")
        stored = [sem("stored0"), sem("stored1")]
        dve_chain, passed = sem("dve_chain_n"), sem("sync_passed_n")
        slot_of, chosen_share = keep["slot_of"], keep["chosen_share"]
        slot_here = ctx.enter_context(nc.sbuf_tensor("slot_here_n", [P, 2, TPC * TOP], U32))
        gathered = ctx.enter_context(nc.sbuf_tensor("gathered", [P, 2, TPC * TOP, D], F32))
        rows_in, rows_added = [sem("rows_in0"), sem("rows_in1")], sem("rows_added")
        slot_copied, pool_passed, dve_passed = sem("slot_copied_n"), sem("pool_passed_n"), sem("dve_passed_n")
        out_chunks = dram["out"].rearrange("a (c t p) d -> (a c) p t d", p=P, t=TPC)
        block = ctx.enter_context(nc.Block())

        @block.scalar
        def _(act):
            act.preload_act_table(ACT.Sqrt)
            act.wait_ge(var_ready, 1)
            nc.scalar.activation(std[:, :], std[:, :], ACT.Sqrt).then_inc(std_ready, 1)

        @block.vector
        def _(dve):
            ch = Chain(dve, dve_chain)
            dve.sem_inc(rows_added, 2)
            with dve.Fori(0, CHUNKS // 2) as it:
                ch.enter(it, 2 * (TOP + 1) * TPC)
                for b in range(2):
                    c = it * 2 + b
                    dve.wait_ge(rows_in[b], it * (16 * TPC * TOP) + 16 * TPC * TOP)
                    for n in range(TOP):
                        for t in range(TPC):
                            rows = acc[:, ds(c * TPC + t, 1), :].rearrange("p a d -> p (a d)")
                            ch.inc(nc.vector.scalar_tensor_tensor(
                                rows, gathered[:, b, t * TOP + n, :], chosen_share[:, ds(c * TPC + t, 1), n], rows,
                                ALU.mult, ALU.add))
                        ch.wait()
                    dve.sem_inc(rows_added, 1)
                    for t in range(TPC):
                        ch.inc(nc.vector.bn_stats(stats[:, ds(c * (TPC * 6) + 6 * t, 6)],
                                                  acc[:, ds(c * TPC + t, 1), :].rearrange("p a d -> p (a d)")))
                ch.leave(CHUNKS // 2)
            ch.wait()
            row_statistics(nc, dve, ch, stats, mean_var, std, rstd, var_ready, std_ready, 0)
            with dve.Fori(0, CHUNKS // 2) as it:
                for b in range(2):
                    c = it * 2 + b
                    dve.wait_ge(rows_free, c + 1)
                    for t in range(TPC):
                        last = nc.vector.tensor_scalar(
                            rows_out[:, b, t, :], acc[:, ds(c * TPC + t, 1), :].rearrange("p a d -> p (a d)"),
                            mean_var[:, ds(c * TPC + t, 1), 0], rstd[:, ds(c * TPC + t, 1)], ALU.subtract, ALU.mult)
                    last.then_inc(rows_ready, 1)

        @block.gpsimd
        def _(pool):
            with pool.Fori(0, CHUNKS // 2) as it:
                for b in range(2):
                    c = it * 2 + b
                    pool.wait_ge(rows_added, c + 1)
                    pool.sem_inc(pool_passed, 1)
                    nc.gpsimd.tensor_copy(slot_here[:, b, :].rearrange("p (t n) -> p t n", n=TOP),
                                          slot_of[:, ds(c * TPC, TPC), :]).then_inc(slot_copied, 1)
                    pool.wait_ge(slot_copied, c + 1)
                    pool.sem_inc(pool_passed, 1)
                    for k in range(TPC * TOP):
                        nc.gpsimd.indirect_dma_start(
                            gathered[:, b, k, :], None, dram["y_slots"],
                            bass.IndirectOffsetOnAxis(slot_here[:, b, k:k + 1], 0)).then_inc(rows_in[b], 16)

        @block.sync
        def _(sp):
            sp.sem_inc(rows_free, 2)
            with sp.Fori(0, CHUNKS // 2) as it:
                for b in range(2):
                    c = it * 2 + b
                    sp.wait_ge(rows_ready, c + 1)
                    sp.sem_inc(passed, 1)
                    sp.dma_start(out_chunks[ds(c, 1), :, :, :].rearrange("a p t d -> (a p) t d"), rows_out[:, b, :, :]
                                 ).then_inc(stored[b], 16)
                    sp.wait_ge(stored[b], it * 16 + 16)
                    sp.sem_inc(rows_free, 1)
            for b in range(2):
                sp.wait_ge(stored[b], 16 * CHUNKS // 2)


def program(nc, dram):
    def left(stack, name, shape, dt=F32):
        return stack.enter_context(nc.sbuf_tensor(name, shape, dt))

    def right(stack, name, shape, dt=F32):
        return stack.enter_context(nc.sbuf_tensor(name, shape, dt, side="right"))

    with ExitStack() as whole:
        keep = {
            "ident": left(whole, "ident", [P, P]),
            "stats": left(whole, "row_stats", [P, TILES * 6]),
            "mean_var": left(whole, "row_mean_var", [P, TILES, 2]),
            "std": left(whole, "row_std", [P, TILES]),
            "rstd": left(whole, "row_rstd", [P, TILES]),
            "chosen_at": left(whole, "chosen_at", [P, TILES, TOP]),
            "chosen_share": left(whole, "chosen_share", [P, TILES, TOP]),
            "slot_of": left(whole, "slot_of", [P, TILES, TOP], U32),
            "tile_expert": left(whole, "tile_expert", [P, SLOT_TILES + 1], U32),
        }
        with ExitStack() as through_routing:
            keep["v_all"] = right(through_routing, "v_all", [P, TILES, D])
            with ExitStack() as through_attention:
                with ExitStack() as first:
                    keep["x_all"] = left(first, "x_all", [P, TILES, D])
                    linear_attention(nc, dram, keep)
                keep["ctx_slots"] = right(through_attention, "ctx_slots", [P, RING + 1, TPC, DH])
                softmax_attention(nc, dram, keep)
                keep["x_all"] = left(whole, "x1_back", [P, TILES, D])
                output_projection(nc, dram, keep)
            routing(nc, dram, keep)
            dispatch(nc, dram, keep)
        experts(nc, dram, keep)
        last_norm(nc, dram, keep)


_INS = ["x", "q_proj", "k_proj", "ln1_g", "ln1_b", "ln2_g", "ln2_b", "Wq", "Wk", "Wv", "Wo", "Wg", "W1", "b1", "W2", "b2"]
_OF = {"x": "L0_attn_x", "q_proj": "L0_attn_q_proj", "k_proj": "L0_attn_k_proj"}


def kernel(**inputs):
    import numpy as np
    import concourse.bacc as bacc
    from concourse.bass_utils import run_bass_kernel_spmd as run

    nc = bacc.Bacc("TRN2", target_bir_lowering=False, num_devices=1)
    arrays, dram = {}, {}
    for name in _INS:
        a = np.ascontiguousarray(inputs[_OF.get(name, "L0_ffn_" + name)])
        arrays["in_" + name] = a
        dram[name] = nc.dram_tensor("in_" + name, a.shape, F32, kind="ExternalInput").ap()
    for name in ("qs", "ks"):
        dram[name] = nc.dram_tensor(name + "_dram", (PARTS, D, TOKENS), BF16).ap()
    dram["kd"] = nc.dram_tensor("kd_dram", (PARTS, D, TOKENS // 2), BF16).ap()
    dram["x1"] = nc.dram_tensor("x1_dram", (P, TILES, D), F32).ap()
    dram["slots"] = nc.dram_tensor("slots_dram", ((SLOT_TILES + 1) * CHUNK, D), F32).ap()
    dram["y_slots"] = nc.dram_tensor("y_slots_dram", (SLOT_TILES * CHUNK, D), F32).ap()
    dram["out"] = nc.dram_tensor("out_0", (1, TOKENS, D), F32, kind="ExternalOutput").ap()
    program(nc, dram)
    r = run(nc, [arrays], core_ids=[0])
    return r.results[0]["out_0"]
```

```python
import concourse.bass as bass
from concourse import mybir
from concourse.alu_op_type import AluOpType as ALU
from contextlib import ExitStack

F32 = mybir.dt.float32
F32R = mybir.dt.float32r
BF16 = mybir.dt.bfloat16
F16 = mybir.dt.float16
U32 = mybir.dt.uint32
I32 = mybir.dt.int32
ACT = mybir.ActivationFunctionType
AX = mybir.AxisListType
ds = bass.ds

P = 128
TOKENS, D = 4096, 256
HALVES = D // P
TILES = TOKENS // P
CHUNK = 512
CHUNKS = TOKENS // CHUNK
TPC = CHUNK // P
PROJ = 64
HEADS, DH = 16, 16
EXPERTS, FF = 8, 1024
FT = FF // P
TOP = 2
SLOT_TILES = (TOP * TOKENS + EXPERTS * (CHUNK - 1)) // CHUNK
EPS = 1e-5
Z_EPS = 1e-8
PARTS = 3

Q_PARTS = (0, 0, 0, 1, 1, 2)
K_PARTS = (0, 1, 2, 0, 1, 0)
SROWS = len(Q_PARTS) * DH
MROWS = 2
AROWS = SROWS + MROWS

V_ONE = PARTS * DH
V_COLS = 64
O_COLS = DH + 1

STEP = 2 * P
STEPS = TOKENS // STEP
KCH = TOKENS // CHUNK // 2
UNITS = TPC * KCH
HALF = CHUNK // 2
LEAST = -3.4e38
LAG = 5
BUFS = 8
POOL_SPLITS = tuple(t for t in range(STEPS) if (t + 1) * 5 // STEPS > t * 5 // STEPS)
DVE_SPLITS = tuple(t for t in range(STEPS) if t not in POOL_SPLITS)
RING = HEADS * CHUNKS


class Chain:

    def __init__(self, eng, sem):
        self.eng, self.sem, self.base, self.n = eng, sem, 0, 0

    def enter(self, it, per):
        self.outer, self.per, self.before = self.base, per, self.n
        self.base, self.n = self.base + self.n + it * per, 0

    def leave(self, rounds):
        assert self.n == self.per, (self.n, self.per)
        self.base, self.n = self.outer, self.before + self.per * rounds

    def inc(self, ins):
        ins.then_inc(self.sem, 1)
        self.n += 1

    def wait(self):
        self.eng.wait_ge(self.sem, self.base + self.n)


def linear_attention(nc, dram, keep):
    with ExitStack() as ctx:
        def sb(name, shape, dt=F32):
            return ctx.enter_context(nc.sbuf_tensor(name, shape, dt))

        def ps(name, shape, dt=F32):
            return ctx.enter_context(nc.psum_tensor(name, shape, dt))

        def sem(name):
            return ctx.enter_context(nc.semaphore(name))

        x_all, v_all, ident = keep["x_all"], keep["v_all"], keep["ident"]
        x_in = sb("x_in", [P, 2, TPC, D])
        xT = sb("xT", [P, 2, HALVES, CHUNK])
        proj_q = sb("proj_q", [P, HALVES, PROJ])
        proj_k = sb("proj_k", [P, HALVES, PROJ])
        w_qkv = sb("w_qkv", [P, 3, HALVES, D])
        gain1 = sb("gain1", [P, HALVES])
        bias1 = sb("bias1", [P, HALVES])
        k_feat = sb("k_feat", [P, 2, TPC, PROJ])
        q_feat = sb("q_feat", [PROJ, TOKENS])
        q_here = sb("q_here", [PROJ, 2, CHUNK])
        kv = sb("kv", [PROJ, D + 1])
        z = sb("z", [P, TPC])
        y_here = sb("y_here", [P, TPC, D])
        stats_here = sb("stats_here", [P, TPC * 6])
        stats = sb("stats", [P, TILES * 6])
        mean_var = sb("mean_var", [P, TILES, 2])
        std = sb("std", [P, TILES])
        rstd = sb("rstd", [P, TILES])
        hn = sb("hn", [P, 2, TPC, D])
        hT = sb("hT", [P, 2, HALVES, CHUNK])
        k_diff = sb("k_diff", [P, HALVES, HALF])
        rest = sb("rest", [P, 5, CHUNK])
        parts = sb("parts", [P, 2, 5, PARTS, CHUNK], BF16)

        banks = ps("banks", [P, 8, CHUNK])
        tr_ps = banks[:, 0:2, :]
        kf_ps = banks[:, 2, 0:TPC * PROJ].rearrange("p (t e) -> p t e", t=TPC)
        qf_ps = banks[0:PROJ, 3, :]
        kv_ps = banks[0:PROJ, 2, 0:D]
        num_ps = banks[:, :, 0:D + 1].rearrange("p (n t) d -> p n t d", n=2)
        qk_ps = banks[:, 2:6, :]
        v_ps = banks[:, 6:8, :].rearrange("p b (t d) -> p (b t) d", t=2)

        proj_in, weights_in, affine_in = sem("proj_in"), sem("weights_in"), sem("affine_in")
        consts_set = sem("consts_set")
        x_in_full, x_in_free = [sem("x_in_full0"), sem("x_in_full1")], sem("x_in_free")
        x_all_full = sem("x_all_full")
        xT_in_psum, xT_ready = sem("xT_in_psum"), sem("xT_ready")
        feat_in_psum, feat_ready = sem("feat_in_psum"), sem("feat_ready")
        kv_in_psum, kv_added = sem("kv_in_psum"), sem("kv_added")
        q_here_ready = sem("q_here_ready")
        num_in_psum, y_ready = sem("num_in_psum"), sem("y_ready")
        var_ready, std_ready = sem("var_ready"), sem("std_ready")
        hn_ready, hnT_in_psum, hT_ready = sem("hn_ready"), sem("hnT_in_psum"), sem("hT_ready")
        qk_in_psum, v_in_psum, v_copied = sem("qk_in_psum"), sem("v_in_psum"), sem("v_copied")
        high_ready, rest_ready, mid_ready, low_ready = (
            sem("high_ready"), sem("rest_ready"), sem("mid_ready"), sem("low_ready"))
        parts_out = [sem("parts_out0"), sem("parts_out1")]
        parts_free = sem("parts_free")
        half_copied, rest_used = sem("half_copied"), sem("rest_used")
        diff_ready, x1_ready, x1_out = sem("diff_ready"), sem("x1_ready"), sem("x1_out")
        dve_chain = sem("dve_chain")

        x_chunks = dram["x"].rearrange("a (c t p) d -> (a c) p t d", p=P, t=TPC)
        block = ctx.enter_context(nc.Block())

        def per_chunk(eng, body):
            with eng.Fori(0, CHUNKS // 2 - 1) as it:
                for b in range(2):
                    body(eng.snap(it * 2 + b), b, True)
            body(CHUNKS - 2, 0, True)
            body(CHUNKS - 1, 1, False)

        @block.sync
        def _(sp):
            sp.dma_start(proj_q[:, :, :], dram["q_proj"].rearrange("(j p) e -> p j e", p=P)).then_inc(proj_in, 16)
            sp.dma_start(proj_k[:, :, :], dram["k_proj"].rearrange("(j p) e -> p j e", p=P)).then_inc(proj_in, 16)
            with sp.Fori(0, CHUNKS // 2) as it:
                for b in range(2):
                    c = it * 2 + b
                    sp.wait_ge(x_in_free, c + 1)
                    sp.dma_start(x_in[:, b, :, :], x_chunks[ds(c, 1), :, :, :].rearrange("a p t d -> (a p) t d")
                                 ).then_inc(x_in_full[b], 16)
            sp.dma_start(x_all[:, :, :], dram["x"].rearrange("a (t p) d -> p (a t) d", p=P)).then_inc(x_all_full, 16)
            for n, w in enumerate(("Wq", "Wk", "Wv")):
                sp.dma_start(w_qkv[:, n, :, :], dram[w].rearrange("(j p) e -> p j e", p=P)).then_inc(weights_in, 16)
            sp.wait_ge(x1_ready, 1)
            sp.dma_start(dram["x1"], x_all[:, :, :]).then_inc(x1_out, 16)
            sp.sem_inc(parts_free, 2)
            with sp.Fori(0, CHUNKS // 2) as it:
                for b in range(2):
                    c = it * 2 + b
                    for s in range(4):
                        sp.wait_ge(low_ready, c * 5 + (s + 1))
                        dst = dram["qs" if s < 2 else "ks"][:, P * (s % 2):P * (s % 2) + P, ds(c * CHUNK, CHUNK)]
                        sp.dma_start(dst.rearrange("n p t -> p n t"), parts[:, b, s, :, :]).then_inc(parts_out[b], 16)
                    sp.wait_ge(low_ready, c * 5 + 5)
                    for j in range(HALVES):
                        dst = dram["kd"][:, P * j:P * j + P, ds(c * HALF, HALF)]
                        sp.dma_start(dst.rearrange("n p t -> p n t"), parts[:, b, 4, :, HALF * j:HALF * j + HALF]
                                     ).then_inc(parts_out[b], 16)
                    sp.wait_ge(parts_out[b], it * 96 + 96)
                    sp.sem_inc(parts_free, 1)
            for b in range(2):
                sp.wait_ge(parts_out[b], 16 * 6 * CHUNKS // 2)
            sp.wait_ge(x1_out, 16)

        @block.gpsimd
        def _(pool):
            nc.gpsimd.memset(ident[:, :], 0.0).then_inc(consts_set, 1)
            nc.gpsimd.memset(kv[:, :], 0.0).then_inc(consts_set, 1)
            pool.wait_ge(consts_set, 2)
            nc.gpsimd.affine_select(out=ident[:, :], in_=ident[:, :], compare_op=ALU.not_equal, fill=1.0,
                                    base=0, pattern=[[-1, P]], channel_multiplier=1).then_inc(consts_set, 1)
            nc.gpsimd.memset(kv[:, D:D + 1], 1.0).then_inc(consts_set, 1)
            pool.dma_start(gain1[:, :], dram["ln1_g"].rearrange("(j p) -> p j", p=P), allow_slow_non_contiguous=True).then_inc(affine_in, 16)
            pool.dma_start(bias1[:, :], dram["ln1_b"].rearrange("(j p) -> p j", p=P), allow_slow_non_contiguous=True).then_inc(affine_in, 16)
        @block.tensor
        def _(pe):
            pe.sem_inc(x_in_free, 2)
            pe.wait_ge(consts_set, 4)
            pe.wait_ge(proj_in, 32)
            def turn_x(c, b):
                pe.wait_ge(x_in_full[b], (c + (2 - b)) * 8)
                for j in range(HALVES):
                    for t in range(TPC):
                        last = nc.tensor.transpose(tr_ps[:, j, P * t:P * t + P], x_in[:, b, t, P * j:P * j + P],
                                                   ident[:, :])
                last.then_inc(xT_in_psum, 1)

            def features(c, b, more):
                pe.wait_ge(xT_ready, c * 2 + 2)
                for t in range(TPC):
                    for j in range(HALVES):
                        nc.tensor.matmul(kf_ps[:, t, :], xT[:, b, j, P * t:P * t + P], proj_k[:, j, :],
                                         start=(j == 0), stop=(j == HALVES - 1))
                for j in range(HALVES):
                    last = nc.tensor.matmul(qf_ps, proj_q[:, j, :], xT[:, b, j, :],
                                            start=(j == 0), stop=(j == HALVES - 1))
                last.then_inc(feat_in_psum, 1)
                if more:
                    turn_x(c + 1, 1 - b)
                pe.wait_ge(feat_ready, c * 2 + 2)
                for t in range(TPC):
                    last = nc.tensor.matmul(kv_ps, k_feat[:, b, t, :], x_in[:, b, t, :],
                                            start=(t == 0), stop=(t == TPC - 1))
                last.then_inc(kv_in_psum, 1)
                pe.wait_ge(kv_added, c + 1)
                pe.sem_inc(x_in_free, 1)

            turn_x(0, 0)
            per_chunk(pe, features)
            with pe.Fori(0, CHUNKS // 2) as it:
                for b in range(2):
                    c = it * 2 + b
                    pe.wait_ge(q_here_ready, c + 1)
                    pe.wait_ge(y_ready, c * TPC + TPC)
                    for t in range(TPC):
                        last = nc.tensor.matmul(num_ps[:, b, t, :], q_here[:, b, P * t:P * t + P], kv[:, :],
                                                start=True, stop=True)
                    last.then_inc(num_in_psum, 1)
            pe.wait_ge(weights_in, 3 * 16)
            pe.wait_ge(y_ready, TILES + 2 * TPC)
            def turn(c, b):
                pe.wait_ge(hn_ready, c + 1)
                for j in range(HALVES):
                    for t in range(TPC):
                        last = nc.tensor.transpose(tr_ps[:, j, P * t:P * t + P], hn[:, b, t, P * j:P * j + P], ident[:, :])
                last.then_inc(hnT_in_psum, 1)

            def project(c, b, more):
                pe.wait_ge(hT_ready, c * 2 + 2)
                for s in range(4):
                    pe.wait_ge(rest_ready, c * 5 + (s + 1))
                    for j in range(HALVES):
                        last = nc.tensor.matmul(qk_ps[:, s, :], w_qkv[:, s // 2, j, P * (s % 2):P * (s % 2) + P],
                                                hT[:, b, j, :], start=(j == 0), stop=(j == HALVES - 1))
                    last.then_inc(qk_in_psum, 1)
                pe.wait_ge(v_copied, c * 2 + 2)
                for t in range(TPC):
                    for j in range(HALVES):
                        last = nc.tensor.matmul(v_ps[:, t, :], hT[:, b, j, P * t:P * t + P], w_qkv[:, 2, j, :],
                                                start=(j == 0), stop=(j == HALVES - 1))
                    if t % 2:
                        last.then_inc(v_in_psum, 1)
                    if t == 1 and more:
                        turn(c + 1, 1 - b)

            turn(0, 0)
            per_chunk(pe, project)

        @block.scalar
        def _(act):
            act.preload_act_table(ACT.Exp)
            with act.Fori(0, CHUNKS // 2) as it:
                for b in range(2):
                    c = it * 2 + b
                    act.wait_ge(xT_in_psum, c + 1)
                    for j in range(HALVES):
                        nc.scalar.activation(xT[:, b, j, :], tr_ps[:, j, :], ACT.Copy).then_inc(xT_ready, 1)
                    act.wait_ge(feat_in_psum, c + 1)
                    nc.scalar.activation(k_feat[:, b, :, :], kf_ps, ACT.Exp).then_inc(feat_ready, 1)
                    nc.scalar.activation(q_feat[:, ds(c * CHUNK, CHUNK)], qf_ps, ACT.Exp).then_inc(feat_ready, 1)
            act.wait_ge(feat_ready, 2 * CHUNKS)
            act.sem_inc(num_in_psum, 2)
            with act.Fori(0, CHUNKS // 2) as it:
                for b in range(2):
                    c = it * 2 + b
                    act.wait_ge(num_in_psum, c + 1)
                    nc.scalar.activation(q_here[:, b, :], q_feat[:, ds(c * CHUNK, CHUNK)], ACT.Copy
                                         ).then_inc(q_here_ready, 1)
            act.preload_act_table(ACT.Sqrt)
            for n in range(2):
                act.wait_ge(var_ready, n + 1)
                nc.scalar.activation(std[:, :], std[:, :], ACT.Sqrt).then_inc(std_ready, 1)
            act.preload_act_table(ACT.Exp)
            act.wait_ge(affine_in, 2 * 16)
            act.sem_inc(v_copied, 2)
            def gain_and_bias(c, b):
                act.wait_ge(hnT_in_psum, c + 1)
                for j in range(HALVES):
                    nc.scalar.activation(hT[:, b, j, :], tr_ps[:, j, :], ACT.Identity,
                                         bias=bias1[:, j:j + 1], scale=gain1[:, j:j + 1]).then_inc(hT_ready, 1)

            def split(c, b, more):
                act.wait_ge(parts_free, c + 1)
                for s in range(4):
                    act.wait_ge(qk_in_psum, c * 4 + (s + 1))
                    nc.scalar.activation(parts[:, b, s, 0, :], qk_ps[:, s, :], ACT.Copy,
                                         scale=(DH ** -0.5 if s < 2 else 1.0)).then_inc(high_ready, 1)
                act.wait_ge(diff_ready, c + 1)
                nc.scalar.activation(parts[:, b, 4, 0, :], k_diff[:, :, :], ACT.Copy).then_inc(high_ready, 1)
                for s in range(5):
                    act.wait_ge(rest_ready, c * 5 + (s + 6))
                    nc.scalar.activation(parts[:, b, s, 1, :], rest[:, s, :], ACT.Copy).then_inc(mid_ready, 1)
                if more:
                    gain_and_bias(c + 1, 1 - b)
                for n in range(2):
                    act.wait_ge(v_in_psum, c * 2 + (n + 1))
                    nc.scalar.activation(v_all[:, ds(c * TPC + 2 * n, 2), :], v_ps[:, 2 * n:2 * n + 2, :],
                                         ACT.Copy).then_inc(v_copied, 1)

            gain_and_bias(0, 0)
            per_chunk(act, split)

        @block.vector
        def _(dve):
            ch = Chain(dve, dve_chain)
            dve.wait_ge(consts_set, 4)
            with dve.Fori(0, CHUNKS) as c:
                dve.wait_ge(kv_in_psum, c + 1)
                nc.vector.tensor_tensor(kv[:, 0:D], kv[:, 0:D], kv_ps, ALU.add).then_inc(kv_added, 1)
                dve.wait_ge(kv_added, c + 1)
            dve.wait_ge(x_all_full, 16)
            dve.sem_inc(y_ready, 2 * TPC)

            def tile(c, t):
                return x_all[:, ds(c * TPC + t, 1), :].rearrange("p a d -> p (a d)")

            def keep_rows(c):
                ch.wait()
                for t in range(TPC):
                    ch.inc(nc.vector.bn_stats(stats_here[:, 6 * t:6 * t + 6], y_here[:, t, :]))
                ch.wait()
                ch.inc(nc.vector.tensor_scalar(stats[:, ds(c * TPC * 6, TPC * 6)], stats_here[:, :], 1.0, None, ALU.mult))
                ch.inc(nc.vector.tensor_scalar(x_all[:, ds(c * TPC, TPC), :], y_here[:, :, :], 1.0, None, ALU.mult))
                ch.wait()

            def reciprocal_std(n):
                for t in range(TILES):
                    ch.inc(nc.vector.bn_aggr(mean_var[:, t, :], stats[:, 6 * t:6 * t + 6]))
                ch.wait()
                nc.vector.tensor_scalar(std[:, :], mean_var[:, :, 1], EPS, None, ALU.add).then_inc(var_ready, 1)
                dve.wait_ge(std_ready, n + 1)
                ch.inc(nc.vector.reciprocal(rstd[:, :], std[:, :]))
                ch.wait()

            with dve.Fori(0, CHUNKS // 2) as it:
                ch.enter(it, 2 * (2 + 2 * TPC + 2))
                for b in range(2):
                    c = it * 2 + b
                    dve.wait_ge(num_in_psum, c + 3)
                    ch.inc(nc.vector.tensor_scalar(z[:, :], num_ps[:, b, :, D], Z_EPS, None, ALU.add))
                    ch.wait()
                    ch.inc(nc.vector.reciprocal(z[:, :], z[:, :]))
                    ch.wait()
                    for t in range(TPC):
                        ch.inc(nc.vector.scalar_tensor_tensor(y_here[:, t, :], num_ps[:, b, t, 0:D], z[:, t:t + 1],
                                                              tile(c, t), ALU.mult, ALU.add))
                    keep_rows(c)
                    dve.sem_inc(y_ready, TPC)
                ch.leave(CHUNKS // 2)
            reciprocal_std(0)
            with dve.Fori(0, CHUNKS) as c:
                ch.enter(c, 2 * TPC + 2)
                for t in range(TPC):
                    ch.inc(nc.vector.tensor_scalar(
                        y_here[:, t, :], tile(c, t), mean_var[:, ds(c * TPC + t, 1), 0], rstd[:, ds(c * TPC + t, 1)],
                        ALU.subtract, ALU.mult))
                keep_rows(c)
                ch.leave(CHUNKS)
            reciprocal_std(1)
            dve.sem_inc(x1_ready, 1)
            dve.sem_inc(rest_ready, 5)

            def normalize(c, b):
                for t in range(TPC):
                    last = nc.vector.tensor_scalar(
                        hn[:, b, t, :], tile(c, t), mean_var[:, ds(c * TPC + t, 1), 0], rstd[:, ds(c * TPC + t, 1)],
                        ALU.subtract, ALU.mult)
                last.then_inc(hn_ready, 1)

            def split(c, b, more):
                for s in range(4):
                    if s == 2:
                        dve.wait_ge(high_ready, c * 5 + 4)
                        nc.vector.tensor_scalar(k_diff[:, :, :], qk_ps[:, 2:4, HALF:CHUNK], 1.0, None, ALU.mult
                                                ).then_inc(half_copied, 1)
                        dve.wait_ge(half_copied, c + 1)
                        nc.vector.tensor_tensor(k_diff[:, :, :], qk_ps[:, 2:4, 0:HALF], k_diff[:, :, :],
                                                ALU.subtract).then_inc(diff_ready, 1)
                    dve.wait_ge(high_ready, c * 5 + (s + 1))
                    nc.vector.scalar_tensor_tensor(rest[:, s, :], qk_ps[:, s, :], DH ** -0.5 if s < 2 else 1.0,
                                                   parts[:, b, s, 0, :], ALU.mult, ALU.subtract
                                                   ).then_inc(rest_ready, 1)
                dve.wait_ge(high_ready, c * 5 + 5)
                nc.vector.tensor_tensor(rest[:, 4, :].rearrange("p (j t) -> p j t", j=HALVES), k_diff[:, :, :],
                                        parts[:, b, 4, 0, :].rearrange("p (j t) -> p j t", j=HALVES), ALU.subtract
                                        ).then_inc(rest_ready, 1)
                if more:
                    normalize(c + 1, 1 - b)
                for s in range(5):
                    dve.wait_ge(mid_ready, c * 5 + (s + 1))
                    nc.vector.tensor_tensor(parts[:, b, s, 2, :], rest[:, s, :], parts[:, b, s, 1, :], ALU.subtract
                                            ).then_inc(low_ready, 1)
                dve.wait_ge(low_ready, c * 5 + 5)
                dve.sem_inc(rest_used, 1)

            normalize(0, 0)
            per_chunk(dve, split)


def softmax_attention(nc, dram, keep):
    with ExitStack() as ctx:
        def sb(name, shape, dt=F32):
            return ctx.enter_context(nc.sbuf_tensor(name, shape, dt))

        def ps(name, shape, dt=F32):
            return ctx.enter_context(nc.psum_tensor(name, shape, dt))

        def sem(name):
            return ctx.enter_context(nc.semaphore(name))

        v_all, ident, ctx_slots = keep["v_all"], keep["ident"], keep["ctx_slots"]
        q_ring = sb("q_ring", [AROWS, 2 * TOKENS], BF16)
        k_ring = sb("k_ring", [AROWS, 2 * TOKENS], BF16)
        kd_ring = sb("kd_ring", [SROWS, 2 * TOKENS // 2], BF16)
        v_parts = sb("v_parts", [P, 2, TILES, V_COLS], BF16)
        v_here = sb("v_here", [P, TILES, DH])
        v_rest = sb("v_rest", [P, TILES, DH])
        zeros = sb("zeros", [P, TILES, DH])
        gather = sb("gather", [P, O_COLS])
        probs = sb("probs", [P, BUFS, STEP // P, CHUNK])
        probs_low = sb("probs_low", [P, BUFS, STEP // P, CHUNK], F16)
        excess = sb("excess", [P, 2, CHUNK])
        unit_max = sb("unit_max", [P, TPC, KCH])
        tile_max = sb("tile_max", [P, TPC])
        max_parts = sb("max_parts", [TPC, MROWS, P], BF16)
        o_here = sb("o_here", [P, CHUNK])
        o_scale = sb("o_scale", [P, TPC])

        s2_ps = ps("s2_ps", [P, STEP // P, CHUNK])
        diff_ps = ps("diff_ps", [P, 2, CHUNK])
        b_ps = ps("b_ps", [P, 2, CHUNK])
        o_ps = ps("o_ps", [P, CHUNK])
        misc_ps = ps("misc_ps", [P, CHUNK])
        out_ps = misc_ps[:, 0:TPC * O_COLS].rearrange("p (t c) -> p t c", t=TPC)
        maxT_ps = misc_ps[0:TPC, P:2 * P]

        qk_in, head_ready = sem("qk_in"), sem("head_ready")
        v_ready, consts_ready, gather_ready = sem("v_ready"), sem("consts_ready"), sem("gather_ready")
        s2_done, exp_done, low_done, pv_done = sem("s2_done"), sem("exp_done"), sem("low_done"), sem("pv_done")
        pool_low_done = sem("pool_low_done")
        diff_done, b_done, excess_ready = sem("diff_done"), sem("b_done"), sem("excess_ready")
        s1_read, tile_max_done = sem("s1_read"), sem("tile_max_done")
        maxT_done, max_split, rows_made = sem("maxT_done"), sem("max_split"), sem("rows_made")
        row_in, rows_in = sem("row_in"), sem("rows_in")
        o_copied, o_turned, o_scaled, o_stored = sem("o_copied"), sem("o_turned"), sem("o_scaled"), sem("o_stored")
        pool_chain, start_values, sync_passed = sem("pool_chain"), sem("start_values"), sem("sync_passed")
        pool_passed, dve_passed = sem("pool_passed"), sem("dve_passed")

        def per_step(eng, body):
            def steps(head, par, last_ahead):
                with eng.Fori(0, 1) as qc:
                    body(head * CHUNKS + qc, head, par, 1 - par, qc, True)
                with eng.Fori(1, CHUNKS) as qc:
                    body(head * CHUNKS + qc, head, par, par, qc, last_ahead)

            with eng.Fori(0, HEADS // 2 - 1) as pair:
                for par in range(2):
                    steps(pair * 2 + par, par, True)
            steps(HEADS - 2, 0, True)
            steps(HEADS - 1, 1, False)

        block = ctx.enter_context(nc.Block())

        @block.sync
        def _(sp):
            def load_head(h, col, kd_col):
                for ring, src, of in ((q_ring, "qs", Q_PARTS), (k_ring, "ks", K_PARTS)):
                    for n, part in enumerate(of):
                        sp.dma_start(ring[DH * n:DH * n + DH, ds(col, TOKENS)],
                                     dram[src][part, ds(h * DH, DH), :]).then_inc(qk_in, 16)
                for n, part in enumerate(K_PARTS):
                    sp.dma_start(kd_ring[DH * n:DH * n + DH, ds(kd_col, TOKENS // 2)],
                                 dram["kd"][part, ds(h * DH, DH), :]).then_inc(qk_in, 16)
                sp.wait_ge(qk_in, (h + 1) * (3 * len(Q_PARTS) * 16))
                sp.sem_inc(head_ready, 1)

            def rows(n):
                col = sp.snap(((n + 15) & 15) * CHUNK)
                sp.wait_ge(rows_made, n + 2)
                sp.sem_inc(sync_passed, 1)
                for r in range(MROWS):
                    sp.dma_start(q_ring[SROWS + r:SROWS + r + 1, ds(col, CHUNK)].rearrange("a (t n) -> a t n", t=TPC),
                                 max_parts[:, r, :]).then_inc(row_in, 16)
                sp.wait_ge(row_in, n * (MROWS * 16) + MROWS * 16)
                sp.sem_inc(rows_in, 1)

            load_head(sp.snap(0), sp.snap(0), sp.snap(0))
            with sp.Fori(0, CHUNKS - 1) as n:
                rows(n)
            with sp.Fori(0, HEADS - 1) as h:
                next_head, col = sp.snap(h + 1), sp.snap(((h + 1) & 1) * TOKENS)
                sp.wait_ge(pv_done, h * (CHUNKS * STEPS) + BUFS)
                sp.sem_inc(sync_passed, 1)
                load_head(next_head, col, sp.snap(((h + 1) & 1) * (TOKENS // 2)))
                with sp.Fori(0, CHUNKS) as qc:
                    rows(h * CHUNKS + (qc + CHUNKS - 1))
            with sp.Fori(0, CHUNKS) as qc:
                rows(qc + HEADS * CHUNKS - 1)

        @block.gpsimd
        def _(pool):
            ch = Chain(pool, pool_chain)
            nc.gpsimd.memset(k_ring[SROWS:AROWS, :], 1.0).then_inc(consts_ready, 1)
            pool.wait_ge(consts_ready, 1)
            nc.gpsimd.memset(v_parts[:, :, :, V_ONE:V_COLS], 0.0).then_inc(consts_ready, 1)
            nc.gpsimd.memset(zeros[:, :, :], 0.0).then_inc(consts_ready, 1)
            pool.wait_ge(consts_ready, 3)
            nc.gpsimd.memset(v_parts[:, :, :, V_ONE:V_ONE + 1], 1.0).then_inc(consts_ready, 1)
            ch.inc(nc.gpsimd.tensor_tensor(gather[:, 0:DH], ident[:, 0:DH], ident[:, DH:2 * DH], ALU.add))
            for r in (2 * DH, V_COLS, V_COLS + DH, V_COLS + 2 * DH):
                ch.wait()
                ch.inc(nc.gpsimd.tensor_tensor(gather[:, 0:DH], gather[:, 0:DH], ident[:, r:r + DH], ALU.add))
            nc.gpsimd.tensor_tensor(gather[:, DH:O_COLS], ident[:, V_ONE:V_ONE + 1],
                                    ident[:, V_COLS + V_ONE:V_COLS + V_ONE + 1], ALU.add).then_inc(gather_ready, 1)

            def split_v(h, par):
                high, mid, low = (v_parts[:, par, :, DH * n:DH * n + DH] for n in range(PARTS))
                ch.inc(nc.gpsimd.tensor_copy(v_here[:, :, :], v_all[:, :, ds(h * DH, DH)]))
                ch.wait()
                ch.inc(nc.gpsimd.tensor_tensor(high, v_here[:, :, :], zeros[:, :, :], ALU.add))
                ch.wait()
                ch.inc(nc.gpsimd.tensor_tensor(v_rest[:, :, :], v_here[:, :, :], high, ALU.subtract))
                ch.wait()
                ch.inc(nc.gpsimd.tensor_tensor(mid, v_rest[:, :, :], zeros[:, :, :], ALU.add))
                ch.wait()
                nc.gpsimd.tensor_tensor(low, v_rest[:, :, :], mid, ALU.subtract).then_inc(v_ready, 1)
                pool.wait_ge(v_ready, h + 1)
                pool.sem_inc(pool_passed, 1)

            def split_probs(i):
                for t in POOL_SPLITS:
                    high = probs[:, t % BUFS, :, :].bitcast(BF16).rearrange("p k (n two) -> p k n two", two=2)
                    pool.wait_ge(exp_done, i * (2 * STEPS) + (2 * t + 4))
                    pool.sem_inc(pool_passed, 1)
                    nc.gpsimd.tensor_tensor(probs_low[:, t % BUFS, :, :], probs[:, t % BUFS, :, :], high[:, :, :, 1],
                                            ALU.subtract).then_inc(pool_low_done, 1)

            def split_head(head, lo=0):
                with pool.Fori(lo, CHUNKS) as qc:
                    split_probs(pool.snap(head * CHUNKS + qc))

            pool.wait_ge(consts_ready, 4)
            for h in range(2):
                split_v(h, h)
            pool.wait_ge(start_values, 4)
            pool.sem_inc(pool_low_done, len(POOL_SPLITS))
            split_head(0)
            with pool.Fori(0, HEADS // 2 - 1) as pair:
                ch.enter(pair, 8)
                for par in range(2):
                    split_probs(pool.snap((pair * 2 + (par + 1)) * CHUNKS))
                    pool.wait_ge(pv_done, (pair * 2 + (par + 1)) * (CHUNKS * STEPS) + BUFS)
                    split_v(pair * 2 + (par + 2), par)
                    split_head(pair * 2 + (par + 1), 1)
                ch.leave(HEADS // 2 - 1)
            split_head(HEADS - 1)

        @block.tensor
        def _(pe):
            pe.wait_ge(consts_ready, 4)
            pe.wait_ge(gather_ready, 1)
            pe.wait_ge(v_ready, 2)
            pe.sem_inc(o_turned, 1)
            pe.sem_inc(pv_done, BUFS - LAG)

            def diff_unit(n, u):
                pe.wait_ge(excess_ready, n * UNITS + (u + 1))
                q = (n & 15) * CHUNK + P * (u // KCH)
                k = ((n >> 3) & 1) * (TOKENS // 2) + CHUNK * (u % KCH)
                nc.tensor.matmul(diff_ps[:, u % 2, :], q_ring[0:SROWS, ds(q, P)], kd_ring[:, ds(k, CHUNK)],
                                 start=True, stop=True).then_inc(diff_done, 1)

            def b_unit(n, u):
                pe.wait_ge(s1_read, n * UNITS + (u + 1))
                q = (n & 15) * CHUNK + P * (u // KCH)
                k = ((n >> 3) & 1) * TOKENS + 2 * CHUNK * (u % KCH)
                keys = k_ring[0:SROWS, ds(k, 2 * CHUNK)].rearrange("r (c h n) -> r c h n", c=2, h=2)
                nc.tensor.matmul(b_ps[:, u % 2, :], q_ring[0:SROWS, ds(q, P)], keys[:, :, 1, :],
                                 start=True, stop=True).then_inc(b_done, 1)

            def turn_max(n):
                pe.wait_ge(tile_max_done, n + 1)
                pe.wait_ge(rows_made, n + 1)
                nc.tensor.transpose(maxT_ps, tile_max[:, :], ident[:, :]).then_inc(maxT_done, 1)

            def turn_o(i, t):
                if t == 0:
                    pe.wait_ge(o_copied, i + 1)
                    pe.wait_ge(o_stored, i + 1)
                last = nc.tensor.matmul(out_ps[:, t, :], o_here[:, P * t:P * t + P], gather[:, :],
                                        start=True, stop=True)
                if t == TPC - 1:
                    last.then_inc(o_turned, 1)

            def values(i, par, t):
                at, rows = t % STEPS, t // STEPS
                if at in POOL_SPLITS:
                    pe.wait_ge(pool_low_done, (i + (1 + rows)) * len(POOL_SPLITS) + (POOL_SPLITS.index(at) + 1))
                else:
                    pe.wait_ge(low_done, (i + (1 + rows)) * len(DVE_SPLITS) + (DVE_SPLITS.index(at) + 1))
                if t == 0:
                    pe.wait_ge(o_copied, i + 1)
                high = probs[:, at % BUFS, :, :].bitcast(BF16).rearrange("p k (n two) -> p k n two", two=2)
                for low, part in enumerate((high[:, :, :, 1], probs_low[:, at % BUFS, :, :])):
                    for k in range(2):
                        last = nc.tensor.matmul(
                            o_ps[V_COLS * k:V_COLS * k + V_COLS, :], v_parts[:, par, 2 * at + k, :], part[:, k, :],
                            start=(t == 0 and low == 0), stop=(at == STEPS - 1 and low == 1))
                last.then_inc(pv_done, 1)

            def step(i, head, par, par_before, qc, ahead):
                i = pe.snap(i)
                n = i + (CHUNKS - 1)
                if ahead:
                    pe.wait_ge(head_ready, (n >> 3) + 1)
                pe.wait_ge(rows_in, i + 3)
                pe.wait_ge(v_ready, head + 1)
                q = q_ring[:, ds(qc * CHUNK + par * TOKENS, CHUNK)]

                def scores(t, k):
                    pe.wait_ge(exp_done, i * (2 * STEPS) + (2 * t + k + 1))
                    col = par * TOKENS + STEP * t + P * k
                    nc.tensor.matmul(s2_ps[:, k, :], k_ring[:, col:col + P], q, start=True, stop=True
                                     ).then_inc(s2_done, 1)

                for t in range(STEPS):
                    scores(t, 0)
                    if ahead:
                        diff_unit(n, t)
                    scores(t, 1)
                    if ahead:
                        b_unit(n, t)
                    values(i, par if t >= LAG else par_before, t - LAG)
                    if t == LAG + 1:
                        pe.wait_ge(rows_made, n + 1)
                    if LAG < t <= LAG + TPC:
                        turn_o(i, t - LAG - 1)
                    if t == LAG + TPC + 1:
                        turn_max(n)

            pe.wait_ge(head_ready, 1)
            with pe.Fori(0, CHUNKS - 1) as n:
                for u in range(UNITS):
                    diff_unit(n, u)
                    b_unit(n, u)
                    if u == 3:
                        turn_max(n)
            pe.wait_ge(start_values, 4)
            for k in range(2):
                nc.tensor.matmul(o_ps[V_COLS * k:V_COLS * k + V_COLS, :], v_parts[:, 1, 0, :], probs_low[:, 0, 0, :],
                                 start=True, stop=False)
            per_step(pe, step)
            for t in range(-LAG, 0):
                values(pe.snap(RING), 1, t)
            for t in range(TPC):
                turn_o(RING, t)

        @block.scalar
        def _(act):
            act.preload_act_table(ACT.Exp)
            act.sem_inc(exp_done, 2)
            act.sem_inc(excess_ready, 2)

            def excess_unit(n, u):
                act.wait_ge(diff_done, n * UNITS + (u + 1))
                act.wait_ge(s1_read, n * UNITS + (u + 1))
                nc.scalar.activation(excess[:, u % 2, :], diff_ps[:, u % 2, :], ACT.Relu).then_inc(excess_ready, 1)

            def copy_o(i):
                act.wait_ge(pv_done, i * STEPS + BUFS)
                act.wait_ge(o_turned, i + 1)
                nc.scalar.activation(o_here[:, :], o_ps[:, :], ACT.Copy).then_inc(o_copied, 1)

            def step(i, head, par, par_before, qc, ahead):
                i = act.snap(i)
                for t in range(STEPS):
                    act.wait_ge(pv_done, i * STEPS + (t + 1))
                    for k in range(2):
                        act.wait_ge(s2_done, i * (2 * STEPS) + (2 * t + k + 1))
                        nc.scalar.activation(probs[:, t % BUFS, k, :], s2_ps[:, k, :], ACT.Exp).then_inc(exp_done, 1)
                        if k == 0 and t == LAG:
                            copy_o(i)
                        if k == 0 and ahead:
                            excess_unit(i + (CHUNKS - 1), t)

            act.wait_ge(start_values, 4)
            with act.Fori(0, CHUNKS - 1) as n:
                for u in range(UNITS):
                    excess_unit(n, u)
            per_step(act, step)
            copy_o(RING)

        @block.vector
        def _(dve):
            dve.sem_inc(o_scaled, 1)
            nc.vector.memset(unit_max[:, :, :], 0.0).then_inc(start_values, 1)
            nc.vector.memset(probs[:, :, :, :], 1.0).then_inc(start_values, 1)
            nc.vector.memset(probs_low[:, :, :, :], 0.0).then_inc(start_values, 1)
            dve.wait_ge(start_values, 3)
            dve.sem_inc(start_values, 1)
            dve.sem_inc(low_done, len(DVE_SPLITS))
            dve.sem_inc(s1_read, 2)
            dve.sem_inc(rows_made, 1)
            dve.sem_inc(rows_in, 1)
            dve.sem_inc(o_stored, 1)

            def finish_max(n):
                dve.wait_ge(maxT_done, n + 1)
                dve.wait_ge(rows_in, n + 1)
                nc.vector.tensor_scalar(max_parts[:, 0, :], maxT_ps, -1.0, None, ALU.mult).then_inc(max_split, 1)
                dve.wait_ge(max_split, n + 1)
                nc.vector.scalar_tensor_tensor(max_parts[:, 1, :], maxT_ps, -1.0, max_parts[:, 0, :],
                                               ALU.mult, ALU.subtract).then_inc(rows_made, 1)

            def finish_o(i):
                dve.wait_ge(o_turned, i + 2)
                nc.vector.reciprocal(o_scale[:, :], out_ps[:, :, DH]).then_inc(o_scaled, 1)
                dve.wait_ge(o_scaled, i + 2)
                nc.vector.tensor_tensor(ctx_slots[:, ds(i, 1), :, :].rearrange("p a t c -> p (a t) c"), out_ps[:, :, 0:DH],
                                        o_scale[:, :].unsqueeze(2).to_broadcast([P, TPC, DH]), ALU.mult
                                        ).then_inc(o_stored, 1)

            def reduce_tiles(n, units):
                dve.wait_ge(s1_read, units)
                nc.vector.tensor_reduce(tile_max[:, :], unit_max[:, :, :], AX.X, ALU.max).then_inc(tile_max_done, 1)
                dve.wait_ge(tile_max_done, n + 1)

            def unit(n, u):
                dve.wait_ge(b_done, n * UNITS + (u + 1))
                dve.wait_ge(excess_ready, n * UNITS + (u + 3))
                dve.sem_inc(dve_passed, 1)
                nc.vector.tensor_tensor_reduce(excess[:, u % 2, :], b_ps[:, u % 2, :], excess[:, u % 2, :], 1.0, LEAST,
                                               ALU.add, ALU.max, unit_max[:, u // KCH, u % KCH:u % KCH + 1]
                                               ).then_inc(s1_read, 1)

            def low(i, t):
                dve.wait_ge(exp_done, i * (2 * STEPS) + (2 * t + 4))
                high = probs[:, t % BUFS, :, :].bitcast(BF16).rearrange("p k (n two) -> p k n two", two=2)
                nc.vector.tensor_tensor(probs_low[:, t % BUFS, :, :], probs[:, t % BUFS, :, :], high[:, :, :, 1],
                                        ALU.subtract).then_inc(low_done, 1)

            def step(i, head, par, par_before, qc, ahead):
                i = dve.snap(i)
                n = i + (CHUNKS - 1)
                reduce_tiles(n, n * UNITS + 2 if ahead else RING * UNITS + 2)
                for t in range(STEPS):
                    if t - 1 in DVE_SPLITS:
                        low(i, t - 1)
                    if ahead:
                        unit(n, t)
                    if t == LAG + TPC + 3:
                        finish_max(n)
                        finish_o(i)

            with dve.Fori(0, CHUNKS - 1) as n:
                reduce_tiles(n, n * UNITS + 2)
                for u in range(UNITS):
                    unit(n, u)
                    if u == 4:
                        finish_max(n)
            per_step(dve, step)
            finish_o(RING)


def row_statistics(nc, dve, ch, stats, mean_var, std, rstd, var_ready, std_ready, n):
    for t in range(TILES):
        ch.inc(nc.vector.bn_aggr(mean_var[:, t, :], stats[:, 6 * t:6 * t + 6]))
    ch.wait()
    nc.vector.tensor_scalar(std[:, :], mean_var[:, :, 1], EPS, None, ALU.add).then_inc(var_ready, 1)
    dve.wait_ge(std_ready, n + 1)
    ch.inc(nc.vector.reciprocal(rstd[:, :], std[:, :]))
    ch.wait()


def output_projection(nc, dram, keep):
    with ExitStack() as ctx:
        def sb(name, shape, dt=F32):
            return ctx.enter_context(nc.sbuf_tensor(name, shape, dt))

        def sem(name):
            return ctx.enter_context(nc.semaphore(name))

        x1, x2, ident, ctx_slots = keep["x_all"], keep["v_all"], keep["ident"], keep["ctx_slots"]
        stats = keep["stats"]
        w_o = sb("w_o", [P, HALVES, D])
        heads_here = sb("heads_here", [P, 2, TPC, D])
        headsT = sb("headsT", [P, 2, HALVES, CHUNK])
        y_here = sb("y2_here", [P, TPC, D])
        stats_here = sb("stats2_here", [P, TPC * 6])
        banks = ctx.enter_context(nc.psum_tensor("banks_o", [P, 8, CHUNK], F32))
        tr_ps = banks[:, 0:2, :]
        att_ps = banks[:, 2:4, :].rearrange("p b (t d) -> p (b t) d", t=2)

        wo_in, heads_ready, turned, headsT_ready, att_done, x2_ready = (
            sem("wo_in"), sem("heads_ready"), sem("turned"), sem("headsT_ready"), sem("att_done"), sem("x2_ready"))
        dve_chain, x1_in = sem("dve_chain_o"), sem("x1_in")
        block = ctx.enter_context(nc.Block())

        @block.sync
        def _(sp):
            sp.dma_start(w_o[:, :, :], dram["Wo"].rearrange("(j p) e -> p j e", p=P)).then_inc(wo_in, 16)
            sp.dma_start(x1[:, :, :], dram["x1"]).then_inc(x1_in, 16)

        @block.scalar
        def _(act):
            act.preload_act_table(ACT.Copy)
            slots = ctx_slots[:, 1:RING + 1, :, :].rearrange("p (h q) t c -> p h q t c", q=CHUNKS)
            with act.Fori(0, CHUNKS // 2) as it:
                for b in range(2):
                    c = it * 2 + b
                    for t in range(TPC):
                        last = nc.scalar.activation(
                            heads_here[:, b, t, :].rearrange("p (h c) -> p h c", c=DH),
                            slots[:, :, ds(c, 1), t, :].rearrange("p h q c -> p (h q) c"), ACT.Copy)
                    last.then_inc(heads_ready, 1)
                    act.wait_ge(turned, c + 1)
                    for j in range(HALVES):
                        nc.scalar.activation(headsT[:, b, j, :], tr_ps[:, j, :], ACT.Copy).then_inc(headsT_ready, 1)

        @block.tensor
        def _(pe):
            pe.wait_ge(wo_in, 16)
            with pe.Fori(0, CHUNKS // 2) as it:
                for b in range(2):
                    c = it * 2 + b
                    pe.wait_ge(heads_ready, c + 1)
                    for j in range(HALVES):
                        for t in range(TPC):
                            last = nc.tensor.transpose(tr_ps[:, j, P * t:P * t + P],
                                                       heads_here[:, b, t, P * j:P * j + P], ident[:, :])
                    last.then_inc(turned, 1)
                    pe.wait_ge(headsT_ready, c * 2 + 2)
                    pe.wait_ge(x2_ready, c + 1)
                    for t in range(TPC):
                        for j in range(HALVES):
                            last = nc.tensor.matmul(att_ps[:, t, :], headsT[:, b, j, P * t:P * t + P], w_o[:, j, :],
                                                    start=(j == 0), stop=(j == HALVES - 1))
                    last.then_inc(att_done, 1)

        @block.vector
        def _(dve):
            ch = Chain(dve, dve_chain)
            dve.wait_ge(x1_in, 16)
            dve.sem_inc(x2_ready, 1)
            with dve.Fori(0, CHUNKS) as c:
                dve.wait_ge(att_done, c + 1)
                ch.enter(c, TPC + 3)
                nc.vector.tensor_tensor(y_here[:, :, :], att_ps, x1[:, ds(c * TPC, TPC), :], ALU.add).then_inc(x2_ready, 1)
                dve.wait_ge(x2_ready, c + 2)
                for t in range(TPC):
                    ch.inc(nc.vector.bn_stats(stats_here[:, 6 * t:6 * t + 6], y_here[:, t, :]))
                ch.wait()
                ch.inc(nc.vector.tensor_scalar(stats[:, ds(c * TPC * 6, TPC * 6)], stats_here[:, :], 1.0, None, ALU.mult))
                ch.inc(nc.vector.tensor_scalar(x2[:, ds(c * TPC, TPC), :], y_here[:, :, :], 1.0, None, ALU.mult))
                ch.inc(nc.vector.tensor_tensor(x1[:, ds(c * TPC, TPC), :], x1[:, ds(c * TPC, TPC), :], y_here[:, :, :],
                                               ALU.add))
                ch.wait()
                ch.leave(CHUNKS)


def routing(nc, dram, keep):
    with ExitStack() as ctx:
        def sb(name, shape, dt=F32):
            return ctx.enter_context(nc.sbuf_tensor(name, shape, dt))

        def sem(name):
            return ctx.enter_context(nc.semaphore(name))

        x2, ident, stats = keep["v_all"], keep["ident"], keep["stats"]
        chosen_at, chosen_share = keep["chosen_at"], keep["chosen_share"]
        mean_var, std, rstd = keep["mean_var"], keep["std"], keep["rstd"]
        w_g = sb("w_g", [P, HALVES, EXPERTS])
        gain2 = sb("gain2", [P, HALVES])
        bias2 = sb("bias2", [P, HALVES])
        hn = sb("hn2", [P, 2, TPC, D])
        mT = sb("mT", [P, 2, HALVES, CHUNK])
        logits = sb("logits", [P, TILES, EXPERTS])
        top_logit = sb("top_logit", [P, TILES])
        prob = sb("prob", [P, TILES, EXPERTS])
        total = sb("total", [P, TILES])
        top = sb("top", [P, TILES, EXPERTS])
        top_at = sb("top_at", [P, TILES, EXPERTS], U32)
        pair = sb("pair", [P, TILES])
        zeros = sb("zero_rows", [P, TPC, D])
        banks = ctx.enter_context(nc.psum_tensor("banks_r", [P, 4, CHUNK], F32))
        tr_ps = banks[:, 0:2, :]
        logit_ps = banks[:, 2:4, 0:TPC * EXPERTS]

        router_in, affine_in = sem("router_in"), sem("affine2_in")
        var_ready, std_ready = sem("var2_ready"), sem("std2_ready")
        hn_ready, hn_kept, turned, mT_ready = sem("hn2_ready"), sem("hn_kept"), sem("turned2"), sem("mT_ready")
        logits_done, logits_kept, shifted_ready, exp_ready = (
            sem("logits_done"), sem("logits_kept"), sem("shifted_ready"), sem("exp_ready"))
        zeros_set, zeros_out = sem("zeros_set"), sem("zeros_out")
        dve_chain, pool_passed = sem("dve_chain_r"), sem("pool_passed_r")
        block = ctx.enter_context(nc.Block())

        @block.sync
        def _(sp):
            sp.dma_start(w_g[:, :, :], dram["Wg"].rearrange("(j p) e -> p j e", p=P)).then_inc(router_in, 16)
            sp.wait_ge(zeros_set, 1)
            with sp.Fori(0, SLOT_TILES + 1) as j:
                sp.dma_start(dram["slots"][ds(j * CHUNK, CHUNK), :].rearrange("(t p) d -> p t d", p=P), zeros[:, :, :]
                             ).then_inc(zeros_out, 16)
            sp.wait_ge(zeros_out, 16 * (SLOT_TILES + 1))

        @block.gpsimd
        def _(pool):
            pool.dma_start(gain2[:, :], dram["ln2_g"].rearrange("(j p) -> p j", p=P),
                           allow_slow_non_contiguous=True).then_inc(affine_in, 16)
            pool.dma_start(bias2[:, :], dram["ln2_b"].rearrange("(j p) -> p j", p=P),
                           allow_slow_non_contiguous=True).then_inc(affine_in, 16)
            nc.gpsimd.memset(zeros[:, :, :], 0.0).then_inc(zeros_set, 1)
            with pool.Fori(0, CHUNKS // 2) as it:
                for b in range(2):
                    c = it * 2 + b
                    pool.wait_ge(hn_ready, c + 1)
                    pool.sem_inc(pool_passed, 1)
                    nc.gpsimd.tensor_copy(x2[:, ds(c * TPC, TPC), :], hn[:, b, :, :]).then_inc(hn_kept, 1)

        @block.scalar
        def _(act):
            act.preload_act_table(ACT.Sqrt)
            act.wait_ge(var_ready, 1)
            nc.scalar.activation(std[:, :], std[:, :], ACT.Sqrt).then_inc(std_ready, 1)
            act.preload_act_table(ACT.Exp)
            act.wait_ge(affine_in, 2 * 16)
            with act.Fori(0, CHUNKS // 2) as it:
                for b in range(2):
                    c = it * 2 + b
                    act.wait_ge(turned, c + 1)
                    for j in range(HALVES):
                        nc.scalar.activation(mT[:, b, j, :], tr_ps[:, j, :], ACT.Identity,
                                             bias=bias2[:, j:j + 1], scale=gain2[:, j:j + 1]).then_inc(mT_ready, 1)
                    act.wait_ge(logits_done, c + 3)
                    nc.scalar.activation(logits[:, ds(c * TPC, TPC), :],
                                         logit_ps[:, b, :].rearrange("p (t e) -> p t e", t=TPC), ACT.Copy
                                         ).then_inc(logits_kept, 1)
            act.wait_ge(shifted_ready, 1)
            nc.scalar.activation(prob[:, :, :], logits[:, :, :], ACT.Exp).then_inc(exp_ready, 1)

        @block.tensor
        def _(pe):
            pe.wait_ge(router_in, 16)
            with pe.Fori(0, CHUNKS // 2) as it:
                for b in range(2):
                    c = it * 2 + b
                    pe.wait_ge(hn_ready, c + 1)
                    for j in range(HALVES):
                        for t in range(TPC):
                            last = nc.tensor.transpose(tr_ps[:, j, P * t:P * t + P],
                                                       hn[:, b, t, P * j:P * j + P], ident[:, :])
                    last.then_inc(turned, 1)
                    pe.wait_ge(mT_ready, c * 2 + 2)
                    for t in range(TPC):
                        for j in range(HALVES):
                            last = nc.tensor.matmul(logit_ps[:, b, EXPERTS * t:EXPERTS * t + EXPERTS],
                                                    mT[:, b, j, P * t:P * t + P], w_g[:, j, :],
                                                    start=(j == 0), stop=(j == HALVES - 1))
                    last.then_inc(logits_done, 1)

        @block.vector
        def _(dve):
            ch = Chain(dve, dve_chain)

            def do(ins):
                ch.inc(ins)
                ch.wait()

            row_statistics(nc, dve, ch, stats, mean_var, std, rstd, var_ready, std_ready, 0)
            dve.sem_inc(hn_kept, 2)
            dve.sem_inc(logits_done, 2)
            with dve.Fori(0, CHUNKS // 2) as it:
                for b in range(2):
                    c = it * 2 + b
                    dve.wait_ge(hn_kept, c + 1)
                    dve.wait_ge(logits_done, c + 1)
                    for t in range(TPC):
                        last = nc.vector.tensor_scalar(
                            hn[:, b, t, :], x2[:, ds(c * TPC + t, 1), :].rearrange("p a d -> p (a d)"),
                            mean_var[:, ds(c * TPC + t, 1), 0], rstd[:, ds(c * TPC + t, 1)], ALU.subtract, ALU.mult)
                    last.then_inc(hn_ready, 1)
            wide = [P, TILES, EXPERTS]
            dve.wait_ge(logits_kept, CHUNKS)
            do(nc.vector.tensor_reduce(top_logit[:, :], logits[:, :, :], AX.X, ALU.max))
            nc.vector.tensor_tensor(logits[:, :, :], logits[:, :, :], top_logit[:, :].unsqueeze(2).to_broadcast(wide),
                                    ALU.subtract).then_inc(shifted_ready, 1)
            dve.wait_ge(exp_ready, 1)
            do(nc.vector.tensor_reduce(total[:, :], prob[:, :, :], AX.X, ALU.add))
            do(nc.vector.reciprocal(total[:, :], total[:, :]))
            do(nc.vector.tensor_tensor(prob[:, :, :], prob[:, :, :], total[:, :].unsqueeze(2).to_broadcast(wide),
                                       ALU.mult))
            for t in range(TILES):
                ch.inc(nc.vector.max(top[:, t, :], prob[:, t, :]))
            ch.wait()
            for t in range(TILES):
                ch.inc(nc.vector.max_index(top_at[:, t, :], top[:, t, :], prob[:, t, :]))
            do(nc.vector.tensor_tensor(pair[:, :], top[:, :, 0], top[:, :, 1], ALU.add))
            do(nc.vector.reciprocal(pair[:, :], pair[:, :]))
            ch.inc(nc.vector.tensor_scalar(chosen_at[:, :, :], top_at[:, :, 0:TOP], 1.0, None, ALU.mult))
            do(nc.vector.tensor_tensor(chosen_share[:, :, :], top[:, :, 0:TOP],
                                       pair[:, :].unsqueeze(2).to_broadcast([P, TILES, TOP]), ALU.mult))


def dispatch(nc, dram, keep):
    with ExitStack() as ctx:
        def sb(name, shape, dt=F32):
            return ctx.enter_context(nc.sbuf_tensor(name, shape, dt))

        def sem(name):
            return ctx.enter_context(nc.semaphore(name))

        hn, chosen_at, slot_of, tile_expert = keep["v_all"], keep["chosen_at"], keep["slot_of"], keep["tile_expert"]
        w1_in, w2_in = keep["w1_in"], keep["w2_in"]
        w1_high, w1_low, w2_high, w2_low = keep["w1_high"], keep["w1_low"], keep["w2_high"], keep["w2_low"]
        NT = SLOT_TILES + 1
        earlier = sb("earlier", [P, P])
        ones = sb("ones", [P, P])
        count_i = sb("count_i_d", [P, NT], I32)
        count = sb("count_d", [P, NT])
        picks = sb("picks", [P, TOP, TILES, EXPERTS])
        both = sb("both", [P, TILES, EXPERTS])
        totals = sb("totals", [P, TILES, EXPERTS])
        sums = sb("sums", [P, 2, TILES, EXPERTS])
        rank = sb("rank", [P, TILES, EXPERTS])
        starts = sb("starts", [P, EXPERTS])
        table = sb("table", [P, EXPERTS, EXPERTS])
        tiles_of = sb("tiles_of", [P, EXPERTS])
        tile_end = sb("tile_end", [P, EXPERTS])
        base = sb("base", [P, EXPERTS])
        slot_f = sb("slot_f", [P, TOP, TILES])
        over = sb("over", [P, NT, EXPERTS])
        expert_f = sb("expert_f", [P, NT])
        rows = sb("rows", [P, 2, TPC, D])
        slot_here = sb("slot_here", [P, 2, TPC * TOP], U32)
        counts_ps = ctx.enter_context(nc.psum_tensor("counts_ps", [P, 2, CHUNK], F32))
        within_ps = counts_ps[:, 0, 0:TILES * EXPERTS].rearrange("p (t e) -> p t e", e=EXPERTS)
        total_ps = counts_ps[:, 1, 0:TILES * EXPERTS].rearrange("p (t e) -> p t e", e=EXPERTS)

        consts_ready, both_ready, counted, slots_ready = (
            sem("consts_ready_d"), sem("both_ready"), sem("counted"), sem("slots_ready"))
        rows_staged, slot_copied, rows_free, pool_passed = (
            sem("rows_staged"), sem("slot_copied"), sem("rows_free_d"), sem("pool_passed_d"))
        scattered = [sem("scattered0"), sem("scattered1")]
        dve_chain, w_in = sem("dve_chain_d"), sem("w_in")
        block = ctx.enter_context(nc.Block())

        @block.sync
        def _(sp):
            sp.wait_ge(slots_ready, 1)
            e = sp.value_load(tile_expert[0:1, 0:1], min_val=0, max_val=EXPERTS - 1)
            sp.dma_start(w1_in[:, :, :], dram["W1"][ds(e, 1), :, :].rearrange("a (j p) f -> p (a j) f", p=P)
                         ).then_inc(w_in, 16)
            sp.dma_start(w2_in[:, :, :], dram["W2"][ds(e, 1), :, :].rearrange("a (p t) d -> (a p) t d", t=FT)
                         ).then_inc(w_in, 16)

        @block.gpsimd
        def _(pool):
            nc.gpsimd.iota(count_i[:, :], [[1, NT]], base=0, channel_multiplier=0).then_inc(consts_ready, 1)
            nc.gpsimd.memset(ones[:, :], 1.0).then_inc(consts_ready, 1)
            pool.wait_ge(consts_ready, 2)
            nc.gpsimd.tensor_copy(count[:, :], count_i[:, :]).then_inc(consts_ready, 1)
            nc.gpsimd.affine_select(out=earlier[:, :], in_=ones[:, :], compare_op=ALU.is_gt, fill=0.0,
                                    base=0, pattern=[[1, P]], channel_multiplier=-1).then_inc(consts_ready, 1)
            pool.wait_ge(slots_ready, 1)
            with pool.Fori(0, CHUNKS // 2) as it:
                for b in range(2):
                    c = it * 2 + b
                    nc.gpsimd.tensor_copy(slot_here[:, b, :].rearrange("p (t n) -> p t n", n=TOP),
                                          slot_of[:, ds(c * TPC, TPC), :]).then_inc(slot_copied, 1)
                    pool.wait_ge(slot_copied, c + 1)
                    pool.wait_ge(rows_staged, c + 1)
                    pool.sem_inc(pool_passed, 1)
                    for k in range(TPC * TOP):
                        nc.gpsimd.indirect_dma_start(
                            dram["slots"], bass.IndirectOffsetOnAxis(slot_here[:, b, k:k + 1], 0),
                            rows[:, b, k // TOP, :], None).then_inc(scattered[b], 16)
                for b in range(2):
                    pool.wait_ge(scattered[b], it * (16 * TPC * TOP) + 16 * TPC * TOP)
                    pool.sem_inc(rows_free, 1)

        @block.tensor
        def _(pe):
            pe.wait_ge(consts_ready, 4)
            pe.wait_ge(both_ready, 1)
            flat = both[:, :, :].rearrange("p t e -> p (t e)")
            for n, of in enumerate((earlier, ones)):
                nc.tensor.matmul(counts_ps[:, n, 0:TILES * EXPERTS], of[:, :], flat, start=True, stop=True
                                 ).then_inc(counted, 1)

        @block.scalar
        def _(act):
            act.sem_inc(rows_free, 2)
            with act.Fori(0, CHUNKS // 2) as it:
                for b in range(2):
                    c = it * 2 + b
                    act.wait_ge(rows_free, c + 1)
                    nc.scalar.activation(rows[:, b, :, :], hn[:, ds(c * TPC, TPC), :], ACT.Copy).then_inc(rows_staged, 1)

        @block.vector
        def _(dve):
            ch = Chain(dve, dve_chain)

            def do(ins):
                ch.inc(ins)
                ch.wait()

            dve.wait_ge(consts_ready, 4)
            experts_row = count[:, 0:EXPERTS].unsqueeze(1)
            for n in range(TOP):
                do(nc.vector.tensor_tensor(picks[:, n, :, :], experts_row.to_broadcast([P, TILES, EXPERTS]),
                                           chosen_at[:, :, n].unsqueeze(2).to_broadcast([P, TILES, EXPERTS]),
                                           ALU.is_equal))
            nc.vector.tensor_tensor(both[:, :, :], picks[:, 0, :, :], picks[:, 1, :, :], ALU.add).then_inc(both_ready, 1)
            dve.wait_ge(counted, 2)
            ch.inc(nc.vector.tensor_scalar(totals[:, :, :], total_ps, 1.0, None, ALU.mult))
            do(nc.vector.tensor_scalar(sums[:, 0, :, :], total_ps, 1.0, None, ALU.mult))
            now, far = 0, 1
            while far < TILES:
                ch.inc(nc.vector.tensor_scalar(sums[:, 1 - now, 0:far, :], sums[:, now, 0:far, :], 1.0, None, ALU.mult))
                do(nc.vector.tensor_tensor(sums[:, 1 - now, far:TILES, :], sums[:, now, far:TILES, :],
                                           sums[:, now, 0:TILES - far, :], ALU.add))
                now, far = 1 - now, far * 2
            do(nc.vector.tensor_tensor(rank[:, :, :], sums[:, now, :, :], totals[:, :, :], ALU.subtract))
            do(nc.vector.tensor_tensor(rank[:, :, :], rank[:, :, :], within_ps, ALU.add))
            do(nc.vector.tensor_scalar(starts[:, :], count[:, 0:EXPERTS], float(CHUNK), None, ALU.mult))
            square = [P, EXPERTS, EXPERTS]
            do(nc.vector.tensor_tensor(table[:, :, :], sums[:, now, TILES - 1, :].unsqueeze(2).to_broadcast(square),
                                       starts[:, :].unsqueeze(1).to_broadcast(square), ALU.is_gt))
            do(nc.vector.tensor_reduce(tiles_of[:, :], table[:, :, :], AX.X, ALU.add))
            do(nc.vector.tensor_tensor(table[:, :, :], experts_row.to_broadcast(square),
                                       count[:, 0:EXPERTS].unsqueeze(2).to_broadcast(square), ALU.is_le))
            do(nc.vector.tensor_tensor(table[:, :, :], table[:, :, :], tiles_of[:, :].unsqueeze(1).to_broadcast(square),
                                       ALU.mult))
            do(nc.vector.tensor_reduce(tile_end[:, :], table[:, :, :], AX.X, ALU.add))
            do(nc.vector.tensor_tensor(base[:, :], tile_end[:, :], tiles_of[:, :], ALU.subtract))
            do(nc.vector.tensor_scalar(base[:, :], base[:, :], float(CHUNK), None, ALU.mult))
            do(nc.vector.tensor_tensor(rank[:, :, :], rank[:, :, :],
                                       base[:, :].unsqueeze(1).to_broadcast([P, TILES, EXPERTS]), ALU.add))
            for n in range(TOP):
                do(nc.vector.tensor_tensor(picks[:, n, :, :], picks[:, n, :, :], rank[:, :, :], ALU.mult))
                do(nc.vector.tensor_reduce(slot_f[:, n, :], picks[:, n, :, :], AX.X, ALU.add))
                do(nc.vector.tensor_scalar(slot_of[:, :, n], slot_f[:, n, :], 1.0, None, ALU.mult))
            do(nc.vector.tensor_tensor(over[:, :, :], tile_end[:, :].unsqueeze(1).to_broadcast([P, NT, EXPERTS]),
                                       count[:, :].unsqueeze(2).to_broadcast([P, NT, EXPERTS]), ALU.is_le))
            do(nc.vector.tensor_reduce(expert_f[:, :], over[:, :, :], AX.X, ALU.add))
            do(nc.vector.tensor_scalar(tile_expert[:, :], expert_f[:, :], float(EXPERTS - 1), None, ALU.min))
            dve.sem_inc(slots_ready, 1)
            dve.wait_ge(w_in, 32)
            w1 = w1_in[:, :, :].rearrange("p j (i t) -> p j t i", t=FT)
            for half in range(HALVES):
                ch.inc(nc.vector.tensor_scalar(w1_high[:, 0, half, :, :], w1[:, half, :, :], 1.0, None, ALU.mult))
            do(nc.vector.tensor_scalar(w2_high[:, 0, :, :], w2_in[:, :, :], 1.0, None, ALU.mult))
            for half in range(HALVES):
                ch.inc(nc.vector.tensor_tensor(w1_low[:, 0, half, :, :], w1[:, half, :, :],
                                               w1_high[:, 0, half, :, :].bitcast(F32), ALU.subtract))
            do(nc.vector.tensor_tensor(w2_low[:, 0, :, :], w2_in[:, :, :], w2_high[:, 0, :, :].bitcast(F32),
                                       ALU.subtract))


def experts(nc, dram, keep):
    with ExitStack() as ctx:
        def sb(name, shape, dt=F32):
            return ctx.enter_context(nc.sbuf_tensor(name, shape, dt))

        def sem(name):
            return ctx.enter_context(nc.semaphore(name))

        ident, tile_expert = keep["ident"], keep["tile_expert"]
        gain2 = sb("gain2_e", [P, HALVES])
        bias2 = sb("bias2_e", [P, HALVES])
        rows = sb("rows_e", [P, 2, TPC, D])
        mT = sb("mT_e", [P, HALVES, CHUNK])
        m_high = sb("m_high", [P, 2, HALVES, CHUNK], F32R)
        m_low = sb("m_low", [P, 2, HALVES, CHUNK], F32R)
        w1_in, w2_in = keep["w1_in"], keep["w2_in"]
        w1_high, w1_low, w2_high, w2_low = keep["w1_high"], keep["w1_low"], keep["w2_high"], keep["w2_low"]
        b1_here = sb("b1_here", [P, 2, FT])
        b2_here = sb("b2_here", [P, 2, D])
        zero = sb("zero", [P, 1])
        hidden = sb("hidden", [P, 2, CHUNK])
        hidden_high = sb("hidden_high", [P, 4, CHUNK], F32R)
        hidden_low = sb("hidden_low", [P, 4, CHUNK], F32R)
        y_out = sb("y_out", [P, TPC, D])
        h_ps = ctx.enter_context(nc.psum_tensor("h_ps", [P, 2, CHUNK], F32))
        y_ps = ctx.enter_context(nc.psum_tensor("y_ps", [P, 2, 2, CHUNK], F32))
        tr_ps = ctx.enter_context(nc.psum_tensor("tr_ps", [P, 2, CHUNK], F32))

        affine_in, zero_set = sem("affine_in_e"), sem("zero_set")
        rows_full, bias_full = [sem("rows_full0"), sem("rows_full1")], [sem("bias_full0"), sem("bias_full1")]
        rows_used, turned, mT_ready, m_high_ready, m_ready = (
            sem("rows_used"), sem("turned_e"), sem("mT_ready_e"), sem("m_high_ready_e"), sem("m_ready"))
        w1_full, w2_full, w1_split, w2_split, w_ready = (
            sem("w1_full"), sem("w2_full"), sem("w1_split"), sem("w2_split"), sem("w_ready"))
        sync_passed, pool_passed = sem("sync_passed_e"), sem("pool_passed_e")
        h_done, h_read, high_done, low_done, hidden_used = (
            sem("h_done"), sem("h_read"), sem("high_done"), sem("low_done_e"), sem("hidden_used"))
        ups_done, y_read, stored, y_free = sem("ups_done"), sem("y_read"), sem("stored_e"), sem("y_free")
        W_OPS = 6
        block = ctx.enter_context(nc.Block())

        def nth(j, b):
            return (j + (2 - b)) * 8

        def per_tile(body):
            def run(eng):
                body(0, 0, True)
                with eng.Fori(0, (SLOT_TILES - 1) // 2) as it:
                    for n in range(2):
                        body(eng.snap(it * 2 + (n + 1)), (n + 1) % 2, False)
            return run
        assert SLOT_TILES % 2 == 1

        @block.sync
        def _(sp):
            def load_rows(j, b):
                sp.wait_ge(rows_used, j + 1)
                sp.sem_inc(sync_passed, 1)
                sp.dma_start(rows[:, b, :, :], dram["slots"][ds(j * CHUNK, CHUNK), :].rearrange("(t p) d -> p t d", p=P)
                             ).then_inc(rows_full[b], 16)

            def load_bias(j, b):
                sp.wait_ge(y_read, j * 2 + 2)
                sp.sem_inc(sync_passed, 1)
                e = sp.value_load(tile_expert[0:1, ds(j, 1)], min_val=0, max_val=EXPERTS - 1)
                sp.dma_start(b1_here[:, b, :], dram["b1"][ds(e, 1), :].rearrange("a (p t) -> (a p) t", t=FT)
                             ).then_inc(bias_full[b], 16)
                sp.dma_start(b2_here[:, b, :], dram["b2"][ds(e, 1), :].to_broadcast([P, D])).then_inc(bias_full[b], 16)

            def load(j, b, first):
                load_rows(j, b)
                if first:
                    return
                e = sp.value_load(tile_expert[0:1, ds(j, 1)], min_val=0, max_val=EXPERTS - 1)
                sp.wait_ge(w1_split, j)
                sp.sem_inc(sync_passed, 1)
                sp.dma_start(w1_in[:, :, :], dram["W1"][ds(e, 1), :, :].rearrange("a (j p) f -> p (a j) f", p=P)
                             ).then_inc(w1_full, 16)
                load_bias(j - 1, 1 - b)
                sp.wait_ge(w2_split, j)
                sp.sem_inc(sync_passed, 1)
                e = sp.value_load(tile_expert[0:1, ds(j, 1)], min_val=0, max_val=EXPERTS - 1)
                sp.dma_start(w2_in[:, :, :], dram["W2"][ds(e, 1), :, :].rearrange("a (p t) d -> (a p) t d", t=FT)
                             ).then_inc(w2_full, 16)

            per_tile(load)(sp)
            sp.wait_ge(w1_split, SLOT_TILES)
            load_bias(SLOT_TILES - 1, (SLOT_TILES - 1) % 2)
            load_rows(SLOT_TILES, SLOT_TILES % 2)

        @block.gpsimd
        def _(pool):
            pool.dma_start(gain2[:, :], dram["ln2_g"].rearrange("(j p) -> p j", p=P),
                           allow_slow_non_contiguous=True).then_inc(affine_in, 16)
            pool.dma_start(bias2[:, :], dram["ln2_b"].rearrange("(j p) -> p j", p=P),
                           allow_slow_non_contiguous=True).then_inc(affine_in, 16)
            nc.gpsimd.memset(zero[:, :], 0.0).then_inc(zero_set, 1)
            pool.wait_ge(zero_set, 1)

            def split(j, b, first):
                if first:
                    pool.sem_inc(w_ready, W_OPS)
                    pool.sem_inc(w1_split, 1)
                    pool.sem_inc(w2_split, 1)
                    return
                pool.wait_ge(ups_done, j + 1)
                pool.wait_ge(w1_full, j * 16)
                w1 = w1_in[:, :, :].rearrange("p j (i t) -> p j t i", t=FT)
                for half in range(HALVES):
                    nc.gpsimd.tensor_tensor(w1_high[:, b, half, :, :], w1[:, half, :, :],
                                            zero[:, :].unsqueeze(2).to_broadcast([P, FT, P]), ALU.add
                                            ).then_inc(w_ready, 1)
                pool.wait_ge(w_ready, j * W_OPS + 2)
                for half in range(HALVES):
                    nc.gpsimd.tensor_tensor(w1_low[:, b, half, :, :], w1[:, half, :, :],
                                            w1_high[:, b, half, :, :].bitcast(F32), ALU.subtract).then_inc(w_ready, 1)
                pool.wait_ge(w_ready, j * W_OPS + 4)
                pool.sem_inc(w1_split, 1)
                pool.wait_ge(hidden_used, j * FT + (4 - FT))
                pool.wait_ge(w2_full, j * 16)
                nc.gpsimd.tensor_tensor(w2_high[:, b, :, :], w2_in[:, :, :],
                                        zero[:, :].unsqueeze(2).to_broadcast([P, FT, D]), ALU.add).then_inc(w_ready, 1)
                pool.wait_ge(w_ready, j * W_OPS + 5)
                nc.gpsimd.tensor_tensor(w2_low[:, b, :, :], w2_in[:, :, :], w2_high[:, b, :, :].bitcast(F32),
                                        ALU.subtract).then_inc(w_ready, 1)
                pool.wait_ge(w_ready, j * W_OPS + 6)
                pool.sem_inc(w2_split, 1)

            per_tile(split)(pool)

        @block.tensor
        def _(pe):
            pe.sem_inc(ups_done, 2)
            pe.sem_inc(hidden_used, 4)
            pe.sem_inc(rows_used, 2)

            def turn(j, b):
                pe.wait_ge(rows_full[b], nth(j, b))
                for half in range(HALVES):
                    for t in range(TPC):
                        last = nc.tensor.transpose(tr_ps[:, half, P * t:P * t + P], rows[:, b, t, P * half:P * half + P],
                                                   ident[:, :])
                last.then_inc(turned, 1)

            def up(j, b, f):
                pe.wait_ge(h_read, j * FT + (f + 1))
                for half in range(HALVES):
                    for n, (w, m) in enumerate(((w1_high, m_high), (w1_high, m_low), (w1_low, m_high))):
                        last = nc.tensor.matmul(h_ps[:, f % 2, :], w[:, b, half, f, :], m[:, b, half, :],
                                                start=(half == 0 and n == 0), stop=(half == HALVES - 1 and n == 2))
                last.then_inc(h_done, 1)

            def down(j, b, f):
                pe.wait_ge(low_done, j * FT + (f + 3))
                if f == 0:
                    pe.wait_ge(y_read, j * 2 + 2)
                for t in range(TPC):
                    cols = slice(P * t, P * t + P)
                    for n, (h, w) in enumerate(((hidden_high, w2_high), (hidden_high, w2_low), (hidden_low, w2_high))):
                        last = nc.tensor.matmul(y_ps[:, b, t // 2, D * (t % 2):D * (t % 2) + D], h[:, f % 4, cols],
                                                w[:, b, f, :], start=(f == 0 and n == 0 and t % 2 == 0),
                                                stop=(f == FT - 1 and n == 2), skip_group_check=True)
                last.then_inc(hidden_used, 1)

            def tile(j, b, first):
                pe.wait_ge(w_ready, j * W_OPS + 6)
                pe.wait_ge(m_ready, j + 1)
                pe.sem_inc(rows_used, 1)
                for f in range(FT):
                    up(j, b, f)
                    if f >= 2:
                        down(j, b, f - 2)
                    elif not first:
                        down(j - 1, 1 - b, FT - 2 + f)
                    if f == 4:
                        turn(j + 1, 1 - b)
                pe.wait_ge(h_done, j * FT + FT)
                pe.sem_inc(ups_done, 1)

            turn(0, 0)
            per_tile(tile)(pe)
            for f in range(FT - 2, FT):
                down(SLOT_TILES - 1, (SLOT_TILES - 1) % 2, f)

        @block.scalar
        def _(act):
            act.preload_act_table(ACT.Gelu_apprx_tanh)
            act.sem_inc(h_read, 2)
            act.sem_inc(low_done, 2)
            act.sem_inc(y_read, 4)
            act.wait_ge(affine_in, 2 * 16)

            def split_rows(j, b):
                act.wait_ge(turned, j + 1)
                for half in range(HALVES):
                    nc.scalar.activation(mT[:, half, :], tr_ps[:, half, :], ACT.Identity, bias=bias2[:, half:half + 1],
                                         scale=gain2[:, half:half + 1]).then_inc(mT_ready, 1)
                act.wait_ge(mT_ready, j * 2 + 2)
                nc.scalar.activation(m_high[:, b, :, :], mT[:, :, :], ACT.Copy).then_inc(m_high_ready, 1)

            def store(j):
                act.wait_ge(y_read, j * 2 + 6)
                act.dma_start(dram["y_slots"][ds(j * CHUNK, CHUNK), :].rearrange("(t p) d -> p t d", p=P), y_out[:, :, :]
                              ).then_inc(stored, 16)

            def tile(j, b, first):
                act.wait_ge(bias_full[b], nth(j, b) * 2)
                for f in range(FT):
                    act.wait_ge(h_done, j * FT + (f + 1))
                    act.wait_ge(low_done, j * FT + (f + 1))
                    nc.scalar.activation(hidden[:, f % 2, :], h_ps[:, f % 2, :], ACT.Gelu_apprx_tanh,
                                         bias=b1_here[:, b, f:f + 1]).then_inc(h_read, 1)
                    act.wait_ge(h_read, j * FT + (f + 3))
                    act.wait_ge(hidden_used, j * FT + (f + 1))
                    nc.scalar.activation(hidden_high[:, f % 4, :], hidden[:, f % 2, :], ACT.Copy).then_inc(high_done, 1)
                    if f == 4 and not first:
                        store(j - 1)
                    if f == 5:
                        act.wait_ge(m_ready, j + 1)
                        split_rows(j + 1, 1 - b)
                    if f == FT - 1 and not first:
                        act.wait_ge(stored, j * 16)
                        act.sem_inc(y_free, 1)

            split_rows(0, 0)
            per_tile(tile)(act)
            store(SLOT_TILES - 1)
            act.wait_ge(stored, SLOT_TILES * 16)

        @block.vector
        def _(dve):
            def low_rows(j, b):
                dve.wait_ge(m_high_ready, j + 1)
                nc.vector.tensor_tensor(m_low[:, b, :, :], mT[:, :, :], m_high[:, b, :, :].bitcast(F32), ALU.subtract
                                        ).then_inc(m_ready, 1)

            def add_b2(j, b):
                dve.wait_ge(hidden_used, j * FT + (FT + 4))
                dve.wait_ge(y_free, j + 1)
                for n in range(2):
                    nc.vector.tensor_tensor(y_out[:, 2 * n:2 * n + 2, :], y_ps[:, b, n, :].rearrange("p (t d) -> p t d", t=2),
                                            b2_here[:, b, :].unsqueeze(1).to_broadcast([P, 2, D]), ALU.add
                                            ).then_inc(y_read, 1)

            def tile(j, b, first):
                for f in range(FT):
                    if f == 3 and not first:
                        add_b2(j - 1, 1 - b)
                    dve.wait_ge(high_done, j * FT + (f + 1))
                    nc.vector.tensor_tensor(hidden_low[:, f % 4, :], hidden[:, f % 2, :],
                                            hidden_high[:, f % 4, :].bitcast(F32), ALU.subtract).then_inc(low_done, 1)
                    if f == 6:
                        low_rows(j + 1, 1 - b)

            dve.sem_inc(y_free, 1)
            low_rows(0, 0)
            per_tile(tile)(dve)
            add_b2(SLOT_TILES - 1, (SLOT_TILES - 1) % 2)


def combine(nc, dram, keep):
    with ExitStack() as ctx:
        def sb(name, shape, dt=F32):
            return ctx.enter_context(nc.sbuf_tensor(name, shape, dt))

        def sem(name):
            return ctx.enter_context(nc.semaphore(name))

        acc, slot_of, chosen_share = keep["x_all"], keep["slot_of"], keep["chosen_share"]
        slot_here = sb("slot_here_n", [P, 2, TPC * TOP], U32)
        share_here = sb("share_here", [P, TPC, TOP])
        gathered = sb("gathered", [P, 2, TPC * TOP, D])
        sum_here = sb("sum_here", [P, TPC, D])
        stats_here = sb("stats_here_n", [P, TPC, 6])
        mean_var = sb("mean_var_n", [P, TPC, 2])
        std = sb("std_n", [P, TPC])
        rstd = sb("rstd_n", [P, TPC])
        rows_out = sb("rows_out", [P, 2, TPC, D])
        rows_in, rows_added = [sem("rows_in0"), sem("rows_in1")], sem("rows_added")
        var_ready, std_ready, rows_ready, rows_free = (
            sem("var3_ready"), sem("std3_ready"), sem("rows_ready"), sem("rows_free"))
        stored = [sem("stored0"), sem("stored1")]
        dve_chain, sync_passed = sem("dve_chain_n"), sem("sync_passed_n")
        slot_copied, pool_passed, dve_passed = sem("slot_copied_n"), sem("pool_passed_n"), sem("dve_passed_n")
        out_chunks = dram["out"].rearrange("a (c t p) d -> (a c) p t d", p=P, t=TPC)
        block = ctx.enter_context(nc.Block())

        @block.gpsimd
        def _(pool):
            with pool.Fori(0, CHUNKS // 2) as it:
                for b in range(2):
                    c = it * 2 + b
                    pool.wait_ge(rows_added, c + 1)
                    pool.sem_inc(pool_passed, 1)
                    nc.gpsimd.tensor_copy(slot_here[:, b, :].rearrange("p (t n) -> p t n", n=TOP),
                                          slot_of[:, ds(c * TPC, TPC), :]).then_inc(slot_copied, 1)
                    pool.wait_ge(slot_copied, c + 1)
                    pool.sem_inc(pool_passed, 1)
                    for k in range(TPC * TOP):
                        nc.gpsimd.indirect_dma_start(
                            gathered[:, b, k, :], None, dram["y_slots"],
                            bass.IndirectOffsetOnAxis(slot_here[:, b, k:k + 1], 0)).then_inc(rows_in[b], 16)

        @block.scalar
        def _(act):
            act.preload_act_table(ACT.Sqrt)
            with act.Fori(0, CHUNKS) as c:
                act.wait_ge(var_ready, c + 1)
                nc.scalar.activation(std[:, :], std[:, :], ACT.Sqrt).then_inc(std_ready, 1)

        @block.vector
        def _(dve):
            ch = Chain(dve, dve_chain)
            dve.sem_inc(rows_added, 2)
            with dve.Fori(0, CHUNKS // 2) as it:
                ch.enter(it, 2 * ((TOP + 2) * TPC + 3))
                for b in range(2):
                    c = it * 2 + b
                    ch.inc(nc.vector.tensor_scalar(share_here[:, :, :], chosen_share[:, ds(c * TPC, TPC), :], 1.0, None,
                                                   ALU.mult))
                    ch.inc(nc.vector.tensor_scalar(sum_here[:, :, :], acc[:, ds(c * TPC, TPC), :], 1.0, None, ALU.mult))
                    ch.wait()
                    dve.wait_ge(rows_in[b], it * (16 * TPC * TOP) + 16 * TPC * TOP)
                    for n in range(TOP):
                        for t in range(TPC):
                            ch.inc(nc.vector.scalar_tensor_tensor(
                                sum_here[:, t, :], gathered[:, b, t * TOP + n, :], share_here[:, t, n:n + 1],
                                sum_here[:, t, :], ALU.mult, ALU.add))
                        ch.wait()
                    dve.sem_inc(rows_added, 1)
                    for t in range(TPC):
                        ch.inc(nc.vector.bn_stats(stats_here[:, t, :], sum_here[:, t, :]))
                    ch.wait()
                    dve.sem_inc(dve_passed, 1)
                    for t in range(TPC):
                        ch.inc(nc.vector.bn_aggr(mean_var[:, t, :], stats_here[:, t, :]))
                    ch.wait()
                    nc.vector.tensor_scalar(std[:, :], mean_var[:, :, 1], EPS, None, ALU.add).then_inc(var_ready, 1)
                    dve.wait_ge(std_ready, c + 1)
                    ch.inc(nc.vector.reciprocal(rstd[:, :], std[:, :]))
                    ch.wait()
                    dve.wait_ge(rows_free, c + 1)
                    for t in range(TPC):
                        last = nc.vector.tensor_scalar(rows_out[:, b, t, :], sum_here[:, t, :], mean_var[:, t, 0:1],
                                                       rstd[:, t:t + 1], ALU.subtract, ALU.mult)
                    last.then_inc(rows_ready, 1)
                    dve.wait_ge(rows_ready, c + 1)
                    dve.sem_inc(dve_passed, 1)
                ch.leave(CHUNKS // 2)

        @block.sync
        def _(sp):
            sp.sem_inc(rows_free, 2)
            with sp.Fori(0, CHUNKS // 2) as it:
                for b in range(2):
                    c = it * 2 + b
                    sp.wait_ge(rows_ready, c + 1)
                    sp.sem_inc(sync_passed, 1)
                    sp.dma_start(out_chunks[ds(c, 1), :, :, :].rearrange("a p t d -> (a p) t d"), rows_out[:, b, :, :]
                                 ).then_inc(stored[b], 16)
                    sp.wait_ge(stored[b], it * 16 + 16)
                    sp.sem_inc(rows_free, 1)
            for b in range(2):
                sp.wait_ge(stored[b], 16 * CHUNKS // 2)


def program(nc, dram):
    def left(stack, name, shape, dt=F32):
        return stack.enter_context(nc.sbuf_tensor(name, shape, dt))

    def right(stack, name, shape, dt=F32):
        return stack.enter_context(nc.sbuf_tensor(name, shape, dt, side="right"))

    with ExitStack() as whole:
        keep = {
            "ident": left(whole, "ident", [P, P]),
            "stats": left(whole, "row_stats", [P, TILES * 6]),
            "mean_var": left(whole, "row_mean_var", [P, TILES, 2]),
            "std": left(whole, "row_std", [P, TILES]),
            "rstd": left(whole, "row_rstd", [P, TILES]),
            "chosen_at": left(whole, "chosen_at", [P, TILES, TOP]),
            "chosen_share": left(whole, "chosen_share", [P, TILES, TOP]),
            "slot_of": left(whole, "slot_of", [P, TILES, TOP], U32),
            "tile_expert": left(whole, "tile_expert", [P, SLOT_TILES + 1], U32),
        }
        with ExitStack() as through_routing:
            keep["v_all"] = right(through_routing, "v_all", [P, TILES, D])
            with ExitStack() as through_attention:
                with ExitStack() as first:
                    keep["x_all"] = left(first, "x_all", [P, TILES, D])
                    linear_attention(nc, dram, keep)
                keep["ctx_slots"] = right(through_attention, "ctx_slots", [P, RING + 1, TPC, DH])
                softmax_attention(nc, dram, keep)
                keep["x_all"] = left(whole, "x1_back", [P, TILES, D])
                output_projection(nc, dram, keep)
            routing(nc, dram, keep)
            keep["w1_in"] = left(whole, "w1_in", [P, HALVES, FF])
            keep["w2_in"] = left(whole, "w2_in", [P, FT, D])
            for name in ("w1_high", "w1_low"):
                keep[name] = left(whole, name, [P, 2, HALVES, FT, P], F32R)
            for name in ("w2_high", "w2_low"):
                keep[name] = left(whole, name, [P, 2, FT, D], F32R)
            dispatch(nc, dram, keep)
        experts(nc, dram, keep)
        combine(nc, dram, keep)


_INS = ["x", "q_proj", "k_proj", "ln1_g", "ln1_b", "ln2_g", "ln2_b", "Wq", "Wk", "Wv", "Wo", "Wg", "W1", "b1", "W2", "b2"]
_OF = {"x": "L0_attn_x", "q_proj": "L0_attn_q_proj", "k_proj": "L0_attn_k_proj"}


def kernel(**inputs):
    import numpy as np
    import concourse.bacc as bacc
    from concourse.bass_utils import run_bass_kernel_spmd as run

    nc = bacc.Bacc("TRN2", target_bir_lowering=False, num_devices=1)
    arrays, dram = {}, {}
    for name in _INS:
        a = np.ascontiguousarray(inputs[_OF.get(name, "L0_ffn_" + name)])
        arrays["in_" + name] = a
        dram[name] = nc.dram_tensor("in_" + name, a.shape, F32, kind="ExternalInput").ap()
    for name in ("qs", "ks"):
        dram[name] = nc.dram_tensor(name + "_dram", (PARTS, D, TOKENS), BF16).ap()
    dram["kd"] = nc.dram_tensor("kd_dram", (PARTS, D, TOKENS // 2), BF16).ap()
    dram["x1"] = nc.dram_tensor("x1_dram", (P, TILES, D), F32).ap()
    dram["slots"] = nc.dram_tensor("slots_dram", ((SLOT_TILES + 1) * CHUNK, D), F32).ap()
    dram["y_slots"] = nc.dram_tensor("y_slots_dram", (SLOT_TILES * CHUNK, D), F32).ap()
    dram["out"] = nc.dram_tensor("out_0", (1, TOKENS, D), F32, kind="ExternalOutput").ap()
    program(nc, dram)
    r = run(nc, [arrays], core_ids=[0])
    return r.results[0]["out_0"]
```
